# Optimizing a Trainium2 kernel written in Bass

```python
import numpy as np
import jax
import jax.numpy as jnp

def _softmax(x, axis=-1):
    return jax.nn.softmax(x, axis=axis)

def _gelu(x):
    return jax.nn.gelu(x, approximate=True)

def _silu(x):
    return jax.nn.silu(x)

def _sigmoid(x):
    return jax.nn.sigmoid(x)

def _layernorm(x, axis=-1, eps=1e-05):
    m = jnp.mean(x, axis=axis, keepdims=True)
    v = jnp.var(x, axis=axis, keepdims=True)
    return (x - m) / jnp.sqrt(v + eps)

def _scatter_add(tgt, idx, src, axis=0):
    return tgt.at[idx].add(src)

def _segment_sum(src, seg, n):
    return jax.ops.segment_sum(src, seg, n)
kernel_name = 'mk_early_fusion_embed_d1_tok_img768_r4_b86a06'

def setup_inputs(seed: int=0):
    np.random.seed(seed)
    _w = jnp.asarray

    def _rec_inputs():
        import jax
        import jax.numpy as jnp
        _rk = jax.random.key(seed)
        x = -0.00016672 + 0.999947 * jax.random.normal(jax.random.fold_in(_rk, 1), (8, 3, 112, 112), jnp.float32)
        x_txt = jax.random.randint(jax.random.fold_in(_rk, 51), (8, 512), 0, 31983, jnp.int32)
        return (x, x_txt)
    x, x_txt = _rec_inputs()

    def _L0_tok_setup():
        import jax, jax.numpy as jnp
        import numpy as np
        P = 16
        EPS = 1e-05

        def _patchify(x):
            B, C, H, W = x.shape
            x = x.reshape(B, C, H // P, P, W // P, P)
            x = x.transpose(0, 2, 4, 1, 3, 5)
            return x.reshape(B, H // P * (W // P), C * P * P)
        key = jax.random.key(seed)
        k1, k2, k3 = jax.random.split(key, 3)
        dim = 192
        patch_dim = 3 * P * P
        x = jax.random.normal(k1, (64, 3, 96, 96), dtype=jnp.float32)
        W_proj = jax.random.normal(k2, (dim, patch_dim), dtype=jnp.float32) * (1.0 / np.sqrt(patch_dim))
        b_proj = jax.random.normal(k3, (dim,), dtype=jnp.float32) * 0.01
        gamma = jnp.ones((dim,), dtype=jnp.float32)
        beta = jnp.zeros((dim,), dtype=jnp.float32)
        return {'x': x, 'W_proj': W_proj, 'b_proj': b_proj, 'gamma': gamma, 'beta': beta}
    _L0_tok_all = _L0_tok_setup()
    _L0_tok_in = {k: v for k, v in _L0_tok_all.items() if k in ('W_proj', 'b_proj', 'gamma', 'beta')}
    del _L0_tok_all

    def _L0_txt_setup():
        import jax, jax.numpy as jnp
        import numpy as np
        NUM_HEADS = 12
        LN_EPS = 1e-05

        def _pe(seq_len, d_model):
            pos = np.arange(seq_len, dtype=np.float32)[:, None]
            div = np.exp(np.arange(0, d_model, 2, dtype=np.float32) * (-np.log(10000.0) / d_model))
            pe = np.zeros((seq_len, d_model), dtype=np.float32)
            pe[:, 0::2] = np.sin(pos * div)
            pe[:, 1::2] = np.cos(pos * div)
            return jnp.asarray(pe)

        def _ln(x, g, b):
            m = jnp.mean(x, axis=-1, keepdims=True)
            v = jnp.mean(jnp.square(x - m), axis=-1, keepdims=True)
            return (x - m) * jax.lax.rsqrt(v + LN_EPS) * g + b
        key = jax.random.key(seed)
        B, S, V, D, L, F = (8, 128, 8000, 192, 4, 768)
        ks = jax.random.split(key, 8)
        sc = 0.02
        return {'x_ids': jax.random.randint(ks[0], (B, S), 0, V), 'emb': jax.random.normal(ks[1], (V, D), jnp.float32) * sc, 'Wq': jax.random.normal(ks[2], (L, D, D), jnp.float32) * sc, 'bq': jnp.zeros((L, D), jnp.float32), 'Wk': jax.random.normal(ks[3], (L, D, D), jnp.float32) * sc, 'bk': jnp.zeros((L, D), jnp.float32), 'Wv': jax.random.normal(ks[4], (L, D, D), jnp.float32) * sc, 'bv': jnp.zeros((L, D), jnp.float32), 'Wo': jax.random.normal(ks[5], (L, D, D), jnp.float32) * sc, 'bo': jnp.zeros((L, D), jnp.float32), 'g1': jnp.ones((L, D), jnp.float32), 'bn1': jnp.zeros((L, D), jnp.float32), 'W1': jax.random.normal(ks[6], (L, D, F), jnp.float32) * sc, 'bw1': jnp.zeros((L, F), jnp.float32), 'W2': jax.random.normal(ks[7], (L, F, D), jnp.float32) * sc, 'bw2': jnp.zeros((L, D), jnp.float32), 'g2': jnp.ones((L, D), jnp.float32), 'bn2': jnp.zeros((L, D), jnp.float32)}
    _L0_txt_all = _L0_txt_setup()
    _L0_txt_in = {k: v for k, v in _L0_txt_all.items() if k in ('emb', 'Wq', 'bq', 'Wk', 'bk', 'Wv', 'bv', 'Wo', 'bo', 'g1', 'bn1', 'W1', 'bw1', 'W2', 'bw2', 'g2', 'bn2')}
    del _L0_txt_all

    def _L0_attn_setup():
        import jax, jax.numpy as jnp
        import numpy as np
        B, N, D, H, DH = (64, 197, 192, 12, 64)
        MASK_VAL = -987654321.0
        key = jax.random.key(seed)
        k1, k2, k3 = jax.random.split(key, 3)
        x = jax.random.normal(k1, (B, N, D), dtype=jnp.float32)
        W_qkv = jax.random.normal(k2, (3 * H * DH, D), dtype=jnp.float32) * 0.02
        scale = jnp.full((H,), DH ** (-0.5), dtype=jnp.float32)
        W_out = jax.random.normal(k3, (D, H * DH), dtype=jnp.float32) * 0.02
        b_out = jnp.zeros((D,), dtype=jnp.float32)
        return {'x': x, 'W_qkv': W_qkv, 'scale': scale, 'W_out': W_out, 'b_out': b_out}
    _L0_attn_all = _L0_attn_setup()
    _L0_attn_in = {k: v for k, v in _L0_attn_all.items() if k in ('W_qkv', 'scale', 'W_out', 'b_out')}
    del _L0_attn_all

    def _L0_ffn_setup():
        import jax, jax.numpy as jnp
        import numpy as np
        NUM_EXPERTS = 8
        TOP_K = 2
        INIT_STD = 0.02
        key = jax.random.key(seed)
        k = jax.random.split(key, 6)
        B, S, D, F, E = (2, 512, 192, 768, NUM_EXPERTS)
        hidden_states = jax.random.normal(k[0], (B, S, D), dtype=jnp.float32)
        gate_w = jax.random.normal(k[1], (D, E), dtype=jnp.float32) * (1.0 / np.sqrt(D))
        w_up = jax.random.normal(k[2], (E, D, F), dtype=jnp.float32) * INIT_STD
        b_up = jnp.zeros((E, F), dtype=jnp.float32)
        w_down = jax.random.normal(k[3], (E, F, D), dtype=jnp.float32) * INIT_STD
        b_down = jnp.zeros((E, D), dtype=jnp.float32)
        return {'hidden_states': hidden_states, 'gate_w': gate_w, 'w_up': w_up, 'b_up': b_up, 'w_down': w_down, 'b_down': b_down}
    _L0_ffn_all = _L0_ffn_setup()
    _L0_ffn_in = {k: v for k, v in _L0_ffn_all.items() if k in ('gate_w', 'w_up', 'b_up', 'w_down', 'b_down')}
    del _L0_ffn_all
    return {'x': x, 'x_txt': x_txt, 'L0_tok_W_proj': _L0_tok_in['W_proj'], 'L0_tok_b_proj': _L0_tok_in['b_proj'], 'L0_tok_gamma': _L0_tok_in['gamma'], 'L0_tok_beta': _L0_tok_in['beta'], 'L0_txt_emb': _L0_txt_in['emb'], 'L0_txt_Wq': _L0_txt_in['Wq'], 'L0_txt_bq': _L0_txt_in['bq'], 'L0_txt_Wk': _L0_txt_in['Wk'], 'L0_txt_bk': _L0_txt_in['bk'], 'L0_txt_Wv': _L0_txt_in['Wv'], 'L0_txt_bv': _L0_txt_in['bv'], 'L0_txt_Wo': _L0_txt_in['Wo'], 'L0_txt_bo': _L0_txt_in['bo'], 'L0_txt_g1': _L0_txt_in['g1'], 'L0_txt_bn1': _L0_txt_in['bn1'], 'L0_txt_W1': _L0_txt_in['W1'], 'L0_txt_bw1': _L0_txt_in['bw1'], 'L0_txt_W2': _L0_txt_in['W2'], 'L0_txt_bw2': _L0_txt_in['bw2'], 'L0_txt_g2': _L0_txt_in['g2'], 'L0_txt_bn2': _L0_txt_in['bn2'], 'L0_attn_W_qkv': _L0_attn_in['W_qkv'], 'L0_attn_scale': _L0_attn_in['scale'], 'L0_attn_W_out': _L0_attn_in['W_out'], 'L0_attn_b_out': _L0_attn_in['b_out'], 'L0_ffn_gate_w': _L0_ffn_in['gate_w'], 'L0_ffn_w_up': _L0_ffn_in['w_up'], 'L0_ffn_b_up': _L0_ffn_in['b_up'], 'L0_ffn_w_down': _L0_ffn_in['w_down'], 'L0_ffn_b_down': _L0_ffn_in['b_down']}

def reference(x, x_txt, L0_tok_W_proj, L0_tok_b_proj, L0_tok_gamma, L0_tok_beta, L0_txt_emb, L0_txt_Wq, L0_txt_bq, L0_txt_Wk, L0_txt_bk, L0_txt_Wv, L0_txt_bv, L0_txt_Wo, L0_txt_bo, L0_txt_g1, L0_txt_bn1, L0_txt_W1, L0_txt_bw1, L0_txt_W2, L0_txt_bw2, L0_txt_g2, L0_txt_bn2, L0_attn_W_qkv, L0_attn_scale, L0_attn_W_out, L0_attn_b_out, L0_ffn_gate_w, L0_ffn_w_up, L0_ffn_b_up, L0_ffn_w_down, L0_ffn_b_down):
    import jax
    import jax.numpy as jnp

    def _L0_tok_ref(x, W_proj, b_proj, gamma, beta):
        import jax, jax.numpy as jnp
        import numpy as np
        P = 16
        EPS = 1e-05

        def _patchify(x):
            B, C, H, W = x.shape
            x = x.reshape(B, C, H // P, P, W // P, P)
            x = x.transpose(0, 2, 4, 1, 3, 5)
            return x.reshape(B, H // P * (W // P), C * P * P)
        patches = _patchify(x)
        y = jnp.einsum('bnp,dp->bnd', patches, W_proj) + b_proj
        mean = jnp.mean(y, axis=-1, keepdims=True)
        var = jnp.var(y, axis=-1, keepdims=True)
        y = (y - mean) * jax.lax.rsqrt(var + EPS)
        return y * gamma + beta

    def _L0_txt_ref(x_ids, emb, Wq, bq, Wk, bk, Wv, bv, Wo, bo, g1, bn1, W1, bw1, W2, bw2, g2, bn2):
        import jax, jax.numpy as jnp
        import numpy as np
        NUM_HEADS = 12
        LN_EPS = 1e-05

        def _pe(seq_len, d_model):
            pos = np.arange(seq_len, dtype=np.float32)[:, None]
            div = np.exp(np.arange(0, d_model, 2, dtype=np.float32) * (-np.log(10000.0) / d_model))
            pe = np.zeros((seq_len, d_model), dtype=np.float32)
            pe[:, 0::2] = np.sin(pos * div)
            pe[:, 1::2] = np.cos(pos * div)
            return jnp.asarray(pe)

        def _ln(x, g, b):
            m = jnp.mean(x, axis=-1, keepdims=True)
            v = jnp.mean(jnp.square(x - m), axis=-1, keepdims=True)
            return (x - m) * jax.lax.rsqrt(v + LN_EPS) * g + b
        B, S = x_ids.shape
        D = emb.shape[1]
        H = NUM_HEADS
        dk = D // H
        h = emb[x_ids] + _pe(S, D)

        def layer(h, p):
            wq, bq_, wk, bk_, wv, bv_, wo, bo_, g1_, bn1_, w1, b1_, w2, b2_, g2_, bn2_ = p

            def heads(y):
                return y.reshape(B, S, H, dk).transpose(0, 2, 1, 3)
            q = heads(h @ wq + bq_)
            k = heads(h @ wk + bk_)
            v = heads(h @ wv + bv_)
            scores = jnp.einsum('bhqd,bhkd->bhqk', q, k) / jnp.sqrt(jnp.float32(dk))
            attn = jax.nn.softmax(scores, axis=-1)
            o = jnp.einsum('bhqk,bhkd->bhqd', attn, v)
            o = o.transpose(0, 2, 1, 3).reshape(B, S, D)
            h = _ln(h + o @ wo + bo_, g1_, bn1_)
            ff = jax.nn.relu(h @ w1 + b1_) @ w2 + b2_
            h = _ln(h + ff, g2_, bn2_)
            return (h, None)
        h, _ = jax.lax.scan(layer, h, (Wq, bq, Wk, bk, Wv, bv, Wo, bo, g1, bn1, W1, bw1, W2, bw2, g2, bn2))
        return h

    def _L0_attn_ref(x, W_qkv, scale, W_out, b_out):
        import jax, jax.numpy as jnp
        import numpy as np
        B, N, D, H, DH = (64, 197, 192, 12, 64)
        MASK_VAL = -987654321.0
        b, n, _ = x.shape
        h, d = (H, DH)
        qkv = x @ W_qkv.T
        q, k, v = jnp.split(qkv, 3, axis=-1)

        def split_heads(t):
            return t.reshape(b, n, h, d).transpose(0, 2, 1, 3)
        q, k, v = (split_heads(q), split_heads(k), split_heads(v))
        dots = jnp.einsum('bhid,bhjd->bhij', q, k) * scale[None, :, None, None]
        diag = jnp.eye(n, dtype=bool)
        dots = jnp.where(diag[None, None], MASK_VAL, dots)
        attn = jax.nn.softmax(dots, axis=-1)
        out = jnp.einsum('bhij,bhjd->bhid', attn, v)
        out = out.transpose(0, 2, 1, 3).reshape(b, n, h * d)
        return out @ W_out.T + b_out

    def _L0_ffn_ref(hidden_states, gate_w, w_up, b_up, w_down, b_down):
        import jax, jax.numpy as jnp
        import numpy as np
        NUM_EXPERTS = 8
        TOP_K = 2
        INIT_STD = 0.02
        B, S, D = hidden_states.shape
        E = gate_w.shape[1]
        x = hidden_states.reshape(-1, D)
        T = x.shape[0]
        logits = x @ gate_w
        probs = jax.nn.softmax(logits, axis=-1)
        top_w, top_i = jax.lax.top_k(probs, TOP_K)
        combine = jnp.zeros((T, E), dtype=x.dtype).at[jnp.arange(T)[:, None], top_i].add(top_w)
        h = jax.nn.gelu(jnp.einsum('td,edf->tef', x, w_up) + b_up, approximate=False)
        y = jnp.einsum('tef,efd->ted', h, w_down) + b_down[None, :, :]
        out = jnp.einsum('ted,te->td', y, combine)
        return out.reshape(B, S, D)
    h = _L0_tok_ref(x, L0_tok_W_proj, L0_tok_b_proj, L0_tok_gamma, L0_tok_beta)
    h = jnp.concatenate([h, _L0_txt_ref(x_txt, L0_txt_emb, L0_txt_Wq, L0_txt_bq, L0_txt_Wk, L0_txt_bk, L0_txt_Wv, L0_txt_bv, L0_txt_Wo, L0_txt_bo, L0_txt_g1, L0_txt_bn1, L0_txt_W1, L0_txt_bw1, L0_txt_W2, L0_txt_bw2, L0_txt_g2, L0_txt_bn2)], axis=1)
    h = h + _L0_attn_ref(_layernorm(h, axis=-1), L0_attn_W_qkv, L0_attn_scale, L0_attn_W_out, L0_attn_b_out)
    h = h + _L0_ffn_ref(_layernorm(h, axis=-1), L0_ffn_gate_w, L0_ffn_w_up, L0_ffn_b_up, L0_ffn_w_down, L0_ffn_b_down)
    return h

_drawn_inputs = setup_inputs


def setup_inputs(seed=0):
    import zlib

    import numpy as np

    out = dict(_drawn_inputs(seed))
    spreads = {'L0_tok_gamma': (1.0, 0.2),
     'L0_tok_beta': (0.0, 0.355),
     'L0_txt_bq': (0.0, 0.8),
     'L0_txt_bk': (0.0, 0.8),
     'L0_txt_bv': (0.0, 0.1),
     'L0_txt_bo': (0.0, 0.1),
     'L0_txt_g1': (1.0, 0.2),
     'L0_txt_bn1': (0.0, 0.1),
     'L0_txt_bw1': (0.0, 0.1),
     'L0_txt_bw2': (0.0, 0.1),
     'L0_txt_g2': (1.0, 0.2),
     'L0_txt_bn2': (0.0, 0.1),
     'L0_attn_scale': (0.125, 0.6),
     'L0_attn_b_out': (0.0, 0.1),
     'L0_ffn_b_up': (0.0, 0.632),
     'L0_ffn_b_down': (0.0, 0.1)}
    factors = {'L0_tok_b_proj': 8.0, 'L0_txt_Wq': 8.0, 'L0_txt_Wk': 8.0}
    for name, (base, spread) in spreads.items():
        noise = np.random.default_rng([zlib.crc32(name.encode()), seed]).standard_normal(out[name].shape)
        drawn = base * np.exp(spread * noise) if base else spread * noise
        out[name] = jnp.asarray(drawn.astype(out[name].dtype))
    for name, factor in factors.items():
        out[name] = (out[name] * factor).astype(out[name].dtype)
    return out
```

```python
import numpy as np
import concourse.bass as bass
from concourse import mybir
from contextlib import ExitStack

F32 = mybir.dt.float32
F32R = mybir.dt.float32r
BF16 = mybir.dt.bfloat16
I32 = mybir.dt.int32
U32 = mybir.dt.uint32
ALU = mybir.AluOpType
ACT = mybir.ActivationFunctionType
AX = mybir.AxisListType.X

B, IMG, TXT, D = 8, 49, 512, 192
N = IMG + TXT
P = 128
KC = 96
EPS = 1e-5
LAYERS, H1, DK = 4, 12, 16
FF = 768
H2, DH = 12, 64
EXPERTS = 8
VOCAB = 8000
BIG = 987654321.0
BASE = 4


def rsqrt_steps(nc, g, tick, rstd, mv, var_eps, half, pool, count):
    g.sem_inc(tick, 1)
    nc.gpsimd.tensor_scalar(var_eps, mv, EPS, None, ALU.add).then_inc(pool, 1)
    g.wait_ge(pool, count)
    nc.gpsimd.tensor_tensor(rstd, var_eps, half, ALU.pow).then_inc(pool, 1)


def embed_phase(nc, dram, tokens):
    TILES = B * TXT // P
    IT = B * IMG // 98
    KT = 768 // P
    with ExitStack() as ctx:
        sb = lambda n, s, d=F32: ctx.enter_context(nc.sbuf_tensor(n, s, d))
        sem = lambda n: ctx.enter_context(nc.semaphore(n))
        ids = sb("ids", [P, TILES], I32)
        idf = sb("idf", [P, TILES])
        neg = sb("neg", [P, TILES])
        idu = sb("idu", [P, TILES], U32)
        words = sb("words", [P, TILES, D])
        pos = sb("pos", [P, 4, D])
        patches = sb("patches", [P, KT, B * IMG])
        wproj = sb("wproj", [P, KT, D])
        rows = sb("tok_rows", [P, 3, D])
        y = sb("tok_y", [P, IT, D])
        z = sb("tok_z", [P, IT, D])
        zero = sb("zero_rows", [P, D])
        stats = sb("tok_stats", [P, IT, 6])
        mv = sb("tok_mv", [P, IT, 2])
        rstd = sb("tok_rstd", [P, IT])
        var_eps = sb("tok_var_eps", [P, IT])
        half = sb("tok_half", [P, IT])
        ps = [ctx.enter_context(nc.psum_tensor(f"tok_ps{i}", [P, 512], F32)) for i in range(IT)]
        ids_in, loaded, gathered, mm, dve, pool, stored = (
            sem(n) for n in ("ids_in", "tok_loaded", "gathered", "tok_mm", "tok_dve", "tok_pool", "tok_stored"))
        tick = sem("tok_tick")
        block = ctx.enter_context(nc.Block())

        @block.sync
        def _(sp):
            sp.dma_start(ids[:, :], dram["ids"]).then_inc(ids_in, 16)
            sp.dma_start(patches[:, :, :], dram["patches"]).then_inc(loaded, 16)
            sp.dma_start(wproj[:, :, :], dram["wproj"]).then_inc(loaded, 16)
            sp.dma_start(rows[:, :, :], dram["tok_rows"].partition_broadcast(P)).then_inc(loaded, 16)
            sp.dma_start(pos[:, :, :], dram["pos"]).then_inc(loaded, 16)
            sp.wait_ge(pool, 7)
            for b in range(B):
                sp.dma_start(tokens[b * N + IMG:(b + 1) * N, :].rearrange("(i p) d -> p i d", p=P),
                             words[:, 4 * b:4 * b + 4, :]).then_inc(stored, 16)
            sp.wait_ge(dve, 6 + 4 * IT)
            for b in range(B):
                p0 = IMG * (b % 2)
                sp.dma_start(tokens[b * N:b * N + IMG, :], z[p0:p0 + IMG, b // 2, :]).then_inc(stored, 16)
            sp.wait_ge(stored, 16 * 2 * B)

        @block.gpsimd
        def _(g):
            g.wait_ge(dve, 4)
            for i in range(TILES):
                g.indirect_dma_start(words[:, i, :], None, dram["emb"],
                                     bass.IndirectOffsetOnAxis(ap=idu[:, i:i + 1], axis=0)).then_inc(gathered, 16)
            g.wait_ge(dve, 4 + 3 * IT)
            nc.gpsimd.memset(half[:, :], -0.5).then_inc(pool, 1)
            g.wait_ge(pool, 1)
            rsqrt_steps(nc, g, tick, rstd[0:98, :], mv[0:98, :, 1], var_eps[0:98, :], half[0:98, :], pool, 2)
            g.wait_ge(gathered, 16 * TILES)
            g.wait_ge(loaded, 64)
            for i in range(4):
                v = words[:, :, :].rearrange("p (b i) d -> p i b d", i=4)[:, i, :, :]
                nc.gpsimd.tensor_tensor(v, v, pos[:, i:i + 1, :].to_broadcast([P, B, D]), ALU.add).then_inc(pool, 1)

        @block.tensor
        def _(pe):
            pe.wait_ge(loaded, 64)
            for i in range(IT):
                for k in range(KT):
                    last = nc.tensor.matmul(ps[i][0:98, 0:D], patches[:, k, 98 * i:98 * i + 98], wproj[:, k, :],
                                            start=(k == 0), stop=(k == KT - 1))
                last.then_inc(mm, 1)

        @block.vector
        def _(v):
            v.wait_ge(ids_in, 16)
            nc.vector.tensor_copy(idf[:, :], ids[:, :]).then_inc(dve, 1)
            v.wait_ge(dve, 1)
            nc.vector.tensor_scalar(neg[:, :], idf[:, :], 0.0, float(VOCAB), ALU.is_lt, ALU.mult).then_inc(dve, 1)
            v.wait_ge(dve, 2)
            nc.vector.tensor_tensor(idf[:, :], idf[:, :], neg[:, :], ALU.add).then_inc(dve, 1)
            v.wait_ge(dve, 3)
            nc.vector.tensor_scalar(idu[:, :], idf[:, :], 0.0, float(VOCAB - 1), ALU.max, ALU.min).then_inc(dve, 1)
            for i in range(IT):
                v.wait_ge(mm, i + 1)
                nc.vector.tensor_tensor(y[0:98, i, :], ps[i][0:98, 0:D], rows[0:98, 0, :], ALU.add).then_inc(dve, 1)
                v.wait_ge(dve, 5 + 3 * i)
                nc.vector.bn_stats(stats[0:98, i, :], y[0:98, i, :]).then_inc(dve, 1)
                v.wait_ge(dve, 6 + 3 * i)
                nc.vector.bn_aggr(mv[0:98, i, :], stats[0:98, i, :]).then_inc(dve, 1)
            v.wait_ge(pool, 3)
            for i in range(IT):
                nc.vector.tensor_scalar(z[0:98, i, :], y[0:98, i, :], mv[0:98, i, 0:1], rstd[0:98, i:i + 1],
                                        ALU.subtract, ALU.mult).then_inc(dve, 1)
            c = 4 + 4 * IT
            v.wait_ge(dve, c)
            nc.vector.tensor_tensor(y[0:98, :, :], z[0:98, :, :], rows[0:98, 1:2, :].to_broadcast([98, IT, D]), ALU.mult).then_inc(dve, 1)
            v.wait_ge(dve, c + 1)
            nc.vector.tensor_tensor(z[0:98, :, :], y[0:98, :, :], rows[0:98, 2:3, :].to_broadcast([98, IT, D]), ALU.add).then_inc(dve, 1)


RING = 3
JOBS = ("tx", "qk", "v", "max", "maxt", "exp", "wo", "ft", "f1", "f2")
ON_ACT = ("tx", "qk", "maxt", "exp", "ft", "f1")
ON_DVE = ("qk", "v", "max", "norm", "wo", "f2")


def merged(main, side, every):
    out, side = [], list(side)
    for i, step in enumerate(main):
        out.append(step)
        if i % every == every - 1 and side:
            out.append(side.pop(0))
    return out + side


def attend_steps(s):
    out, due = [], []
    for n in range(6):
        for hh in range(4):
            out.append(("exp", s, n, hh))
            due = [(left - 1, steps) for left, steps in due]
            while due and due[0][0] == 0:
                out += due.pop(0)[1]
        due.append((2, [("pv", s, n)] + ([("norm", s, n // 2)] if n % 2 else [])))
    return out + [step for _, steps in due for step in steps]


def project_steps(s):
    return [("tx", s), ("qk", s, 0), ("qk", s, 1), ("qk", s, 2), ("v", s)]


def feed_steps(s):
    return [("wo", s), ("ft", s), ("f1", s, 0), ("f1", s, 1), ("f1", s, 2), ("f2", s)]


def max_steps(s):
    return [("max", s, h, a) for h in range(H1) for a in range(2)]


def weave(a, b):
    return [x for i in range(max(len(a), len(b))) for x in (a[i:i + 1] + b[i:i + 1])]


BODY = (merged(attend_steps(0), max_steps(1), 1) + [("maxt", 1)]
        + merged(attend_steps(1), weave(feed_steps(0), project_steps(0)), 2)
        + merged(max_steps(0), weave(feed_steps(1), project_steps(1)), 2) + [("maxt", 0)])
AHEAD = project_steps(0) + project_steps(1) + max_steps(0) + [("maxt", 0)]


class Counts:

    def __init__(self, steps, jobs, on_act, on_dve, start=None, first_job=0):
        self.steps, self.on_dve, self.first_job = steps, on_dve, first_job
        number = lambda kinds: {s: n for n, s in enumerate(x for x in steps if x[0] in kinds)}
        self.jobs = number(jobs)
        self.tables = {"mm": number(jobs + ("pv",)), "act": number(on_act), "dve": number(on_dve)}
        self.start = start or {"mm": BASE, "act": BASE, "dve": BASE}

    def total(self, name):
        return len(self.tables[name])

    def end(self):
        return {name: self.start[name] + self.total(name) for name in self.tables}

    def value(self, turn, name, step, turns_back=0):
        fixed = self.start[name] + self.tables[name][step] + 1 - turns_back * self.total(name)
        return turn * self.total(name) + fixed if self.looped else fixed

    looped = False

    def buffer(self, step):
        return (self.jobs[step] + self.first_job) % RING

    def freed(self, turn, step):
        j, order = self.jobs[step], list(self.jobs)
        if j < RING and not self.looped:
            return None
        before = order[j - RING]
        name = "dve" if before[0] in self.on_dve else "act"
        return name, self.value(turn, name, before, turns_back=1 if j < RING else 0)


def encoder_phase(nc, dram, tokens):
    ahead_jobs = sum(x[0] in JOBS for x in AHEAD)
    PRO = Counts(AHEAD, JOBS, ON_ACT, ON_DVE, first_job=-ahead_jobs % RING)
    LOOP = Counts(BODY, JOBS, ON_ACT, ON_DVE, start=PRO.end())
    LOOP.looped = True
    assert len(LOOP.jobs) % RING == 0
    TURNS = LAYERS * B // 2
    with ExitStack() as ctx:
        sb = lambda n, s, d=F32: ctx.enter_context(nc.sbuf_tensor(n, s, d))
        sem = lambda n: ctx.enter_context(nc.semaphore(n))
        two = lambda n, s, d=F32: [sb(f"{n}{i}", s, d) for i in range(2)]
        ident = sb("ident", [P, P])
        wqk = sb("wqk", [KC, 2, 2 * D])
        wv = sb("wv", [KC, 2, D])
        bqk = sb("bqk", [P, 3])
        bv = sb("bv_rows", [P, 2 * D])
        wo = sb("wo", [P, 3, D])
        w1 = sb("w1", [KC, 2, FF])
        b1 = sb("b1", [P, 6])
        w2 = sb("w2", [P, 6, D])
        rows = sb("enc_rows", [P, 6, D])
        h_in = two("h_in", [P, 4, D])
        res = two("res", [P, 4, D])
        hT = two("hT", [KC, 2, TXT])
        qk_hi = sb("qk_hi", [P, 3, TXT], F32R)
        qk_lo = sb("qk_lo", [P, 3, TXT], F32R)
        q_st = two("q_stack", [P, H1 // 2, TXT], F32R)
        k_st = two("k_stack", [P, H1 // 2, TXT], F32R)
        vals = two("vals", [P, 4, H1, 32])
        mx = two("mx", [P, 4, H1])
        nmax = two("nmax", [H1, TXT], F32R)
        probs = two("probs", [P, 4, 2, TXT])
        sums = sb("sums", [P, TXT])
        oT = two("oT", [P, 3, TXT])
        h1 = two("h1", [P, 4, D])
        h1T = two("h1T", [KC, 2, TXT])
        relu = sb("relu", [P, 6, TXT])
        y = sb("y", [P, 4, D])
        yn = sb("yn", [P, 4, D])
        h_out = sb("h_out", [P, 4, D])
        stats = sb("stats", [P, 4, 6])
        mv = sb("mv", [P, 4, 2])
        rstd = sb("rstd", [P, 4])
        var_eps = sb("var_eps", [P, 4])
        half = sb("half", [P, 4])
        ring = [ctx.enter_context(nc.psum_tensor(f"ring{i}", [P, 2, 512], F32)) for i in range(RING)]
        acc = [ctx.enter_context(nc.psum_tensor(f"acc{i}", [P, 512], F32)) for i in range(2)]
        qk_dram = [nc.dram_tensor(f"qk_scratch{s}", [2, 2 * D, TXT], F32, kind="Internal").ap() for s in range(2)]

        fixed_in, mm, act, dve, ln, pool = (sem(n) for n in ("fixed_in", "mm", "act", "dve", "ln", "pool"))
        wx_in, wf_in = sem("wx_in"), sem("wf_in")
        h_loaded, spilled, stacked, max_in, stored = ([sem(f"{n}{s}") for s in range(2)] for n in
                                                      ("h_loaded", "spilled", "stacked", "max_in", "stored"))
        ones_set, tick = sem("ones_set"), sem("tick")
        h_dram = tokens[0:B * N, :].rearrange("(b n) d -> b n d", n=N)[:, IMG:N, :].rearrange(
            "b (i p) d -> b p i d", p=P)
        pool_at, count = {("res", 0): 1, ("res", 1): 2}, 2
        ln_at, links = {}, 0
        for step in BODY:
            if step[0] == "norm":
                links += 2
            elif step[0] in ("wo", "f2"):
                which = 1 if step[0] == "wo" else 2
                pool_at[("rstd", step[1], which)] = count + 2
                pool_at[("ln", step[1], which)] = count + 4
                count += 4
                if which == 1:
                    count += 1
                    pool_at[("res2", step[1])] = count
                ln_at[(step[1], which)] = (links + 8, links + 12)
                links += 12
        N_POOL, N_LN = count, links
        POOL_BASE = N_POOL

        def pool_value(it, *piece, turns_back=0):
            return it * N_POOL + (POOL_BASE + pool_at[piece] - turns_back * N_POOL)

        sems = {"mm": mm, "act": act, "dve": dve}
        block = ctx.enter_context(nc.Block())

        @block.tensor
        def _(pe):
            pe.wait_ge(fixed_in, 16)

            def steps(counts, it):
                k = it if counts is LOOP else 0
                loads = 1 if counts is LOOP else 0
                for step in counts.steps:
                    kind, s = step[0], step[1]
                    if kind == "norm":
                        continue
                    if kind != "pv":
                        buf = ring[counts.buffer(step)]
                        freed = counts.freed(it, step)
                        if freed:
                            pe.wait_ge(sems[freed[0]], freed[1])
                    if kind == "tx":
                        pe.wait_ge(h_loaded[s], k * 16 + 16 * (1 + loads))
                        for c in range(2):
                            for i in range(4):
                                last = nc.tensor.transpose(buf[0:KC, c, P * i:P * i + P], h_in[s][:, i, KC * c:KC * c + KC],
                                                           ident[:, :])
                    elif kind == "qk":
                        m = step[2]
                        if m == 0:
                            pe.wait_ge(act, counts.value(it, "act", ("tx", s)))
                            pe.wait_ge(wx_in, k * 64 + 64 * (1 + loads))
                        for c in range(2):
                            last = nc.tensor.matmul(buf[:, 0, :], wqk[:, c, P * m:P * m + P], hT[s][:, c, :],
                                                    start=(c == 0), stop=(c == 1))
                    elif kind == "v":
                        for i in range(4):
                            for c in range(2):
                                last = nc.tensor.matmul(buf[:, i // 2, D * (i % 2):D * (i % 2) + D],
                                                        hT[s][:, c, P * i:P * i + P], wv[:, c, :],
                                                        start=(c == 0), stop=(c == 1))
                    elif kind == "max":
                        h, a = step[2:]
                        r, t = 64 * (h % 2), h // 2
                        if h == 0 and a == 0:
                            ahead = loads if s == 0 else 0
                            pe.wait_ge(stacked[s], k * 192 + 192 * (1 + ahead))
                            pe.wait_ge(ones_set, 1)
                        for i in (2 * a, 2 * a + 1):
                            last = nc.tensor.matmul(buf[:, i % 2, :], q_st[s][r:r + 3 * DK, t, P * i:P * i + P],
                                                    k_st[s][r:r + 3 * DK, t, :], start=True, stop=True)
                    elif kind == "maxt":
                        pe.wait_ge(dve, counts.value(it, "dve", ("max", s, H1 - 1, 1)))
                        for i in range(4):
                            last = nc.tensor.transpose(buf[0:H1, 0, P * i:P * i + P], mx[s][:, i, :], ident[:, :])
                    elif kind == "exp":
                        n, hh = step[2:]
                        h = 4 * (n // 2) + hh
                        r, t = 64 * (h % 2), h // 2
                        if n == 0 and hh == 0:
                            pe.wait_ge(max_in[s], k * 32 + 32)
                        for j in range(2):
                            kt = 2 * (n % 2) + j
                            last = nc.tensor.matmul(buf[:, j, :], k_st[s][r:r + 3 * DK + 1, t, P * kt:P * kt + P],
                                                    q_st[s][r:r + 3 * DK + 1, t, :], start=True, stop=True)
                    elif kind == "pv":
                        n = step[2]
                        g = 3 * s + n // 2
                        pe.wait_ge(act, counts.value(it, "act", ("exp", s, n, 3)))
                        if n % 2 == 0:
                            back = (g - 2) % 6
                            pe.wait_ge(dve, counts.value(it, "dve", ("norm", back // 3, back % 3), turns_back=int(g < 2)))
                        for j in range(2):
                            kt = 2 * (n % 2) + j
                            for hh in range(4):
                                last = nc.tensor.matmul(acc[g % 2][32 * hh:32 * hh + 32, :],
                                                        vals[s][:, kt, 4 * (n // 2) + hh, :], probs[n % 2][:, hh, j, :],
                                                        start=(n % 2 == 0 and j == 0), stop=(n % 2 == 1 and j == 1),
                                                        tile_position=(0, 32 * hh), skip_group_check=True)
                    elif kind == "wo":
                        pe.wait_ge(dve, counts.value(it, "dve", ("norm", s, 2)))
                        pe.wait_ge(wf_in, k * 80 + 80)
                        for i in range(4):
                            for g in range(3):
                                last = nc.tensor.matmul(buf[:, i // 2, D * (i % 2):D * (i % 2) + D],
                                                        oT[s][:, g, P * i:P * i + P], wo[:, g, :],
                                                        start=(g == 0), stop=(g == 2))
                    elif kind == "ft":
                        pe.wait_ge(pool, pool_value(it, "ln", s, 1))
                        for c in range(2):
                            for i in range(4):
                                last = nc.tensor.transpose(buf[0:KC, c, P * i:P * i + P], h1[s][:, i, KC * c:KC * c + KC],
                                                           ident[:, :])
                    elif kind == "f1":
                        m = step[2]
                        if m == 0:
                            pe.wait_ge(act, counts.value(it, "act", ("ft", s)))
                        for j in range(2):
                            for c in range(2):
                                f = P * (2 * m + j)
                                last = nc.tensor.matmul(buf[:, j, :], w1[:, c, f:f + P], h1T[s][:, c, :],
                                                        start=(c == 0), stop=(c == 1))
                    elif kind == "f2":
                        pe.wait_ge(act, counts.value(it, "act", ("f1", s, 2)))
                        for i in range(4):
                            for k2 in range(6):
                                last = nc.tensor.matmul(buf[:, i // 2, D * (i % 2):D * (i % 2) + D],
                                                        relu[:, k2, P * i:P * i + P], w2[:, k2, :],
                                                        start=(k2 == 0), stop=(k2 == 5))
                    last.then_inc(mm, 1)

            steps(PRO, 0)
            with pe.Fori(0, TURNS) as it:
                steps(LOOP, it)

        @block.scalar
        def _(sc):
            def steps(counts, it):
                for step in counts.steps:
                    kind, s = step[0], step[1]
                    if kind not in ON_ACT:
                        continue
                    buf = ring[counts.buffer(step)]
                    sc.wait_ge(mm, counts.value(it, "mm", step))
                    if kind == "tx":
                        nc.scalar.activation(hT[s][:, :, :], buf[0:KC, :, :], ACT.Copy).then_inc(act, 1)
                    elif kind == "qk":
                        m = step[2]
                        if m == 0:
                            if counts is LOOP:
                                sc.wait_ge(spilled[1 - s], it * 32 + (32 if s == 0 else 64))
                            elif s == 1:
                                sc.wait_ge(spilled[0], 32)
                        nc.scalar.activation(qk_hi[:, m, :], buf[:, 0, :], ACT.Identity, bias=bqk[:, m:m + 1]).then_inc(act, 1)
                    elif kind == "maxt":
                        nc.scalar.activation(nmax[s][:, :], buf[0:H1, 0, :], ACT.Copy, scale=-1.0).then_inc(act, 1)
                    elif kind == "exp":
                        n, hh = step[2:]
                        if hh == 0:
                            back = 6 * s + n - 2
                            if back >= 0:
                                sc.wait_ge(mm, counts.value(it, "mm", ("pv", back // 6, back % 6)))
                        nc.scalar.activation(probs[n % 2][:, hh, :, :], buf[:, :, :], ACT.Exp,
                                             scale=DK ** -0.5).then_inc(act, 1)
                    elif kind == "ft":
                        nc.scalar.activation(h1T[s][:, :, :], buf[0:KC, :, :], ACT.Copy).then_inc(act, 1)
                    elif kind == "f1":
                        m = step[2]
                        nc.scalar.activation(relu[:, 2 * m, :], buf[:, 0, :], ACT.Relu, bias=b1[:, 2 * m:2 * m + 1])
                        nc.scalar.activation(relu[:, 2 * m + 1, :], buf[:, 1, :], ACT.Relu,
                                             bias=b1[:, 2 * m + 1:2 * m + 2]).then_inc(act, 1)

            sc.sem_inc(act, BASE)
            sc.wait_ge(wx_in, 64)
            steps(PRO, 0)
            with sc.Fori(0, TURNS) as it:
                steps(LOOP, it)

        @block.vector
        def _(v):
            def steps(counts, it):
                link_at = [0]

                def link(ins):
                    link_at[0] += 1
                    ins.then_inc(ln, 1)
                    v.wait_ge(ln, it * N_LN + (BASE + link_at[0]))

                def layer_norm(s, which):
                    for i in range(4):
                        last = nc.vector.bn_stats(stats[:, i, :], y[:, i, :])
                        if i < 3:
                            last.then_inc(ln, 1)
                            link_at[0] += 1
                    link(last)
                    v.sem_inc(tick, 1)
                    for i in range(4):
                        last = nc.vector.bn_aggr(mv[:, i, :], stats[:, i, :])
                        last.then_inc(ln, 1)
                        link_at[0] += 1
                    v.wait_ge(pool, pool_value(it, "rstd", s, which))
                    for i in range(4):
                        nc.vector.tensor_scalar(yn[:, i, :], y[:, i, :], mv[:, i, 0:1], rstd[:, i:i + 1],
                                                ALU.subtract, ALU.mult).then_inc(ln, 1)
                        link_at[0] += 1

                for step in counts.steps:
                    kind, s = step[0], step[1]
                    if kind not in ON_DVE:
                        continue
                    if kind == "norm":
                        g = step[2]
                        v.wait_ge(mm, counts.value(it, "mm", ("pv", s, 2 * g + 1)))
                        a, back = acc[(3 * s + g) % 2], (3 * s + g - 1) % 6
                        v.wait_ge(dve, counts.value(it, "dve", ("norm", back // 3, back % 3), turns_back=int(3 * s + g < 1)))
                        v.sem_inc(tick, 1)
                        link(nc.vector.stream_shuffle(sums[:, :], a[:, :], [16 + i % 16 for i in range(32)]))
                        link(nc.vector.reciprocal(sums[:, :], sums[:, :]))
                        nc.vector.tensor_tensor(oT[s][:, g, :], a[:, :], sums[:, :], ALU.mult).then_inc(dve, 1)
                        continue
                    buf = ring[counts.buffer(step)]
                    if kind == "qk":
                        m = step[2]
                        v.wait_ge(act, counts.value(it, "act", step))
                        nc.vector.scalar_tensor_tensor(qk_lo[:, m, :], buf[:, 0, :], bqk[:, m:m + 1],
                                                       qk_hi[:, m, :].bitcast(F32), ALU.add, ALU.subtract).then_inc(dve, 1)
                        continue
                    v.wait_ge(mm, counts.value(it, "mm", step))
                    if kind == "v":
                        nc.vector.tensor_tensor(
                            vals[s][:, :, :, 0:DK].rearrange("p (a b) h d -> p a (b h) d", a=2),
                            buf[:, :, 0:2 * D].rearrange("p a (h d) -> p a h d", d=DK),
                            bv[:, :].rearrange("p (a h d) -> p a h d", a=1, d=DK).to_broadcast([P, 2, 2 * H1, DK]),
                            ALU.add).then_inc(dve, 1)
                    elif kind == "max":
                        h, a = step[2:]
                        row = (h % 2) * 6 + h // 2
                        nc.vector.tensor_reduce(mx[s][:, 2 * a:2 * a + 2, row], buf[:, :, :], AX, ALU.max).then_inc(dve, 1)
                    elif kind in ("wo", "f2"):
                        if kind == "wo":
                            v.wait_ge(pool, pool_value(it, "res", s))
                        if kind == "f2":
                            v.wait_ge(pool, pool_value(it, "res2", s))
                        r = res[s]
                        v.wait_ge(ln, it * N_LN + (BASE + link_at[0]))
                        link_y = nc.vector.tensor_tensor(y[:, :, :].rearrange("p (a b) d -> p a (b d)", a=2), buf[:, :, 0:2 * D],
                                                         r[:, :, :].rearrange("p (a b) d -> p a (b d)", a=2), ALU.add)
                        link_y.then_inc(dve, 1)
                        v.wait_ge(dve, counts.value(it, "dve", step))
                        layer_norm(s, 1 if kind == "wo" else 2)
                return link_at[0]

            for s in range(2):
                nc.vector.memset(k_st[s][:, :, :].bitcast(F32), 1.0)
                nc.vector.memset(q_st[s][:, :, :].bitcast(F32), 1.0)
                last = nc.vector.memset(vals[s][:, :, :, :], 1.0)
            last.then_inc(ones_set, 1)
            v.sem_inc(mm, BASE)
            v.sem_inc(dve, BASE)
            v.sem_inc(ln, BASE)
            v.wait_ge(wx_in, 64)
            v.wait_ge(ones_set, 1)
            steps(PRO, 0)
            with v.Fori(0, TURNS) as it:
                links = steps(LOOP, it)
            assert links == N_LN, links

        @block.gpsimd
        def _(g):
            def lane(name):
                return {"bo": 0, "g1": 1, "bn1": 2, "bw2": 3, "g2": 4, "bn2": 5}[name]

            wide = lambda name: rows[:, lane(name):lane(name) + 1, :].to_broadcast([P, 4, D])
            nc.gpsimd.memset(half[:, :], -0.5)
            g.sem_inc(pool, POOL_BASE)
            with g.Fori(0, TURNS) as it:
                g.wait_ge(wf_in, it * 80 + 80)
                g.wait_ge(dve, it * LOOP.total("dve") + LOOP.start["dve"])
                for s in range(2):
                    g.wait_ge(h_loaded[s], it * 16 + 16)
                    nc.gpsimd.tensor_tensor(res[s][:, :, :], h_in[s][:, :, :], wide("bo"), ALU.add).then_inc(pool, 1)
                for step in LOOP.steps:
                    kind, s = step[0], step[1]
                    if kind in ("wo", "f2"):
                        which = 1 if kind == "wo" else 2
                        moments, normed = ln_at[(s, which)]
                        g.wait_ge(ln, it * N_LN + (BASE + moments))
                        rsqrt_steps(nc, g, tick, rstd[:, :], mv[:, :, 1], var_eps[:, :], half[:, :], pool,
                                    pool_value(it, "rstd", s, which) - 1)
                        g.wait_ge(ln, it * N_LN + (BASE + normed))
                        out = h1[s] if which == 1 else h_out
                        if which == 2:
                            g.wait_ge(stored[1 - s], it * 16 + 16 * (1 + s))
                        nc.gpsimd.tensor_tensor(out[:, :, :], yn[:, :, :], wide("g1" if which == 1 else "g2"),
                                                ALU.mult).then_inc(pool, 1)
                        g.wait_ge(pool, pool_value(it, "ln", s, which) - 1)
                        nc.gpsimd.tensor_tensor(out[:, :, :], out[:, :, :], wide("bn1" if which == 1 else "bn2"),
                                                ALU.add).then_inc(pool, 1)
                        g.wait_ge(pool, pool_value(it, "ln", s, which))
                        if which == 1:
                            nc.gpsimd.tensor_tensor(res[s][:, :, :], out[:, :, :], wide("bw2"), ALU.add).then_inc(pool, 1)

        @block.sync
        def _(sp):
            def load_project_weights(layer):
                sp.dma_start(wqk[:, :, :], dram["wqk"][layer]).then_inc(wx_in, 16)
                sp.dma_start(wv[:, :, :], dram["wv"][layer]).then_inc(wx_in, 16)
                sp.dma_start(bqk[:, :], dram["bqk"][layer]).then_inc(wx_in, 16)
                sp.dma_start(bv[:, :], dram["bv2"][layer].partition_broadcast(P)).then_inc(wx_in, 16)

            def spill_and_stack(counts, it, s, before_count):
                sp.wait_ge(act, counts.value(it, "act", ("qk", s, 2)))
                sp.sem_inc(tick, 1)
                sp.wait_ge(dve, counts.value(it, "dve", ("qk", s, 2)))
                for part, t in ((0, qk_hi), (1, qk_lo)):
                    sp.dma_start(qk_dram[s][part].rearrange("(m p) n -> p m n", p=P),
                                 t[:, :, :].bitcast(F32)).then_inc(spilled[s], 16)
                sp.wait_ge(spilled[s], before_count)
                for r in range(2):
                    for st, first, parts in ((q_st, 0, (0, 1, 0)), (k_st, D, (0, 0, 1))):
                        for c, part in enumerate(parts):
                            src = qk_dram[s][part][first:first + D, :].rearrange("(t r d) n -> r d t n", r=2, d=DK)
                            p0 = 64 * r + DK * c
                            sp.dma_start(st[s][p0:p0 + DK, :, :].bitcast(F32), src[r]).then_inc(stacked[s], 16)

            def max_row(counts, it, s):
                sp.wait_ge(act, counts.value(it, "act", ("maxt", s)))
                for r in range(2):
                    p0 = 64 * r + 3 * DK
                    sp.dma_start(q_st[s][p0:p0 + 1, :, :].bitcast(F32),
                                 nmax[s][6 * r:6 * r + 6, :].bitcast(F32)).then_inc(max_in[s], 16)

            def store(it, s):
                sp.wait_ge(pool, pool_value(it, "ln", s, 2))
                sp.sem_inc(tick, 1)
                sp.dma_start(h_dram[(it % 4) * 2 + s], h_out[:, :, :]).then_inc(stored[s], 16)

            for s in range(2):
                sp.sem_inc(stored[s], 16)
            sp.dma_start(ident[:, :], dram["ident"]).then_inc(fixed_in, 16)
            load_project_weights(0)
            for s in range(2):
                sp.dma_start(h_in[s][:, :, :], h_dram[s]).then_inc(h_loaded[s], 16)
            sp.wait_ge(ones_set, 1)
            for s in range(2):
                spill_and_stack(PRO, 0, s, 32)
            max_row(PRO, 0, 0)
            with sp.Fori(0, TURNS) as it:
                nxt = (it + 1) % TURNS
                sp.wait_ge(dve, it * LOOP.total("dve") + LOOP.start["dve"])
                sp.sem_inc(tick, 1)
                load_project_weights(nxt // 4)
                sp.wait_ge(pool, it * N_POOL + POOL_BASE)
                sp.sem_inc(tick, 1)
                layer = it // 4
                sp.dma_start(wo[:, :, :], dram["wo"][layer]).then_inc(wf_in, 16)
                sp.dma_start(w1[:, :, :], dram["w1"][layer]).then_inc(wf_in, 16)
                sp.dma_start(b1[:, :], dram["b1"][layer]).then_inc(wf_in, 16)
                sp.dma_start(w2[:, :, :], dram["w2"][layer]).then_inc(wf_in, 16)
                sp.dma_start(rows[:, :, :], dram["enc_rows"][layer].partition_broadcast(P)).then_inc(wf_in, 16)
                for s in range(2):
                    sp.wait_ge(pool, pool_value(it, "res", s))
                    sp.wait_ge(stored[s], it * 16 + 16)
                    sp.sem_inc(tick, 1)
                    sp.dma_start(h_in[s][:, :, :], h_dram[(nxt % 4) * 2 + s]).then_inc(h_loaded[s], 16)
                max_row(LOOP, it, 1)
                spill_and_stack(LOOP, it, 0, it * 32 + 64)
                store(it, 0)
                spill_and_stack(LOOP, it, 1, it * 32 + 64)
                max_row(LOOP, it, 0)
                store(it, 1)
            for s in range(2):
                sp.wait_ge(stored[s], 16 * TURNS + 16)
                sp.wait_ge(stacked[s], 192 * (TURNS + 1))
                sp.wait_ge(max_in[s], 32 * (TURNS + 1 - s))


TILES = [(i, min(P, N - P * i)) for i in range((N + P - 1) // P)]
WO_JOBS = ((0, 1), (2,), (3,), (4,))
COLS = ((0, 512), (512, N - 512))
JOBS2 = ("t", "qk", "v", "max", "maxt", "exp", "wo")
ON_ACT2 = ("t", "q", "maxt", "exp")
ON_DVE2 = ("k", "v", "max", "norm", "wo")


def fused_steps():
    out = [("t", 0), ("t", 1)] + [("qk", j) for j in range(H2)] + [("v", i) for i, _ in TILES]
    out += [("max", h, i) for h in range(H2) for i, _ in TILES] + [("maxt",)]
    for h in range(H2):
        for kt, _ in TILES:
            out.append(("exp", h, kt))
            if kt == 1 and h:
                out += [("pv", h - 1), ("norm", h - 1)]
    return out + [("pv", H2 - 1), ("norm", H2 - 1)] + [("wo", n) for n in range(len(WO_JOBS))]


def flat(buf):
    return buf[:, :, :].rearrange("p a b -> p (a b)")


def rows_of(t, b):
    v = t[0:B * N, :].rearrange("(b n) d -> b n d", n=N)
    return (v[:, 0:4 * P, :].rearrange("b (i p) d -> b p i d", p=P)[b], v[:, 4 * P:N, :][b])


def attention_phase(nc, dram, tokens, fused):
    steps_list = fused_steps()
    on_act, on_dve = ("t", "qk_q", "maxt", "exp"), ("qk_k", "v", "max", "norm", "wo")
    name_of = lambda s: (("qk_q",) if s[1] < H2 // 2 else ("qk_k",)) + s[1:] if s[0] == "qk" else s
    steps_list = [name_of(s) for s in steps_list]
    C = Counts(steps_list, ("t", "qk_q", "qk_k", "v", "max", "maxt", "exp", "wo"), on_act, on_dve)
    C.looped = True
    assert len(C.jobs) % RING == 0, len(C.jobs)
    with ExitStack() as ctx:
        sb = lambda n, s, d=F32: ctx.enter_context(nc.sbuf_tensor(n, s, d))
        sem = lambda n: ctx.enter_context(nc.semaphore(n))
        ident = sb("a_ident", [P, P])
        eye16 = sb("eye16", [P, P], BF16)
        mask16 = sb("mask16", [P, P], BF16)
        wqk = sb("a_wqk", [KC, 2, 2 * H2 * DH])
        wv = sb("a_wv", [KC, 2, H2 * DH])
        wo = sb("a_wo", [P, 6, D])
        scale = sb("a_scale", [P, H2])
        b_out = sb("a_bout", [P, 1, D])
        h_in = sb("a_h", [P, 5, D])
        res = sb("a_res", [P, 5, D])
        xn = sb("a_xn", [P, 5, D])
        xT = sb("a_xT", [KC, 2, N])
        qT = sb("a_qT", [DH + 1, H2, N])
        kT = sb("a_kT", [DH + 1, H2, N])
        vals = sb("a_vals", [P, 5, H2, 2 * DH])
        mx = sb("a_mx", [P, 5, H2])
        nmax = sb("a_nmax", [H2, N])
        probs = [sb(f"a_probs{i}", [P, 5, N]) for i in range(2)]
        sums = sb("a_sums", [DH, N])
        oT = sb("a_oT", [P, 6, N])
        out = sb("a_out", [P, 5, D])
        stats = sb("a_stats", [P, 5, 6])
        mv = sb("a_mv", [P, 5, 2])
        rstd = sb("a_rstd", [P, 5])
        var_eps = sb("a_var_eps", [P, 5])
        half = sb("a_half", [P, 5])
        ring = [ctx.enter_context(nc.psum_tensor(f"a_ring{i}", [P, 2, 512], F32)) for i in range(RING)]
        acc = ctx.enter_context(nc.psum_tensor("a_acc", [P, 2, 512], F32))
        fixed_in, ready, loaded, mm, act, dve, ln, pool, max_in, stored = (sem("a_" + n) for n in (
            "fixed_in", "ready", "loaded", "mm", "act", "dve", "ln", "pool", "max_in", "stored"))
        tick = sem("a_tick")
        sems = {"mm": mm, "act": act, "dve": dve}
        N_LN, N_POOL = 15 + H2, 4
        block = ctx.enter_context(nc.Block())

        @block.sync
        def _(sp):
            for dst, src in ((ident[:, :], dram["ident"]), (wqk[:, :, :], dram["a_wqk"]), (wv[:, :, :], dram["a_wv"]),
                             (wo[:, :, :], dram["a_wo"]), (scale[:, :], dram["a_scale"].partition_broadcast(P)),
                             (b_out[:, :, :], dram["a_bout"].partition_broadcast(P))):
                sp.dma_start(dst, src).then_inc(fixed_in, 16)
            with sp.Fori(0, B) as it:
                sp.wait_ge(ln, it * N_LN + BASE)
                sp.wait_ge(pool, it * N_POOL + BASE)
                full, rest = rows_of(tokens, it)
                sp.dma_start(h_in[:, 0:4, :], full).then_inc(loaded, 16)
                sp.dma_start(h_in[0:N - 4 * P, 4, :], rest).then_inc(loaded, 16)
                sp.wait_ge(act, C.value(it, "act", ("maxt",)))
                sp.dma_start(qT[DH:DH + 1, :, :], nmax[:, :]).then_inc(max_in, 16)
                sp.wait_ge(dve, C.value(it, "dve", ("wo", 3)))
                full, rest = rows_of(fused, it)
                sp.dma_start(full, out[:, 0:4, :]).then_inc(stored, 16)
                sp.dma_start(rest, out[0:N - 4 * P, 4, :]).then_inc(stored, 16)
            sp.wait_ge(stored, 32 * B + BASE)
            sp.wait_ge(max_in, 16 * B)

        @block.gpsimd
        def _(g):
            nc.gpsimd.memset(half[:, :], -0.5)
            g.sem_inc(pool, BASE)
            with g.Fori(0, B) as it:
                g.wait_ge(fixed_in, 96)
                g.wait_ge(loaded, it * 32 + 32)
                g.wait_ge(dve, it * C.total("dve") + BASE)
                for n, (t, r) in enumerate(((slice(0, 4), P), (slice(4, 5), N - 4 * P))):
                    nt = t.stop - t.start
                    nc.gpsimd.tensor_tensor(res[0:r, t, :], h_in[0:r, t, :], b_out[0:r, :, :].to_broadcast([r, nt, D]),
                                            ALU.add).then_inc(pool, 1)
                g.wait_ge(ln, it * N_LN + (BASE + 10))
                rsqrt_steps(nc, g, tick, rstd[:, :], mv[:, :, 1], var_eps[:, :], half[:, :], pool, it * N_POOL + (BASE + 3))

        @block.tensor
        def _(pe):
            pe.wait_ge(fixed_in, 96)
            pe.wait_ge(ready, 1)
            with pe.Fori(0, B) as it:
                for step in C.steps:
                    kind = step[0]
                    if kind == "norm":
                        continue
                    if kind != "pv":
                        buf = ring[C.buffer(step)]
                        name, value = C.freed(it, step)
                        pe.wait_ge(sems[name], value)
                    if kind == "t":
                        c = step[1]
                        pe.wait_ge(ln, it * N_LN + (BASE + 15))
                        for i, r in TILES:
                            last = nc.tensor.transpose(flat(buf)[0:KC, P * i:P * i + r], xn[0:r, i, KC * c:KC * c + KC],
                                                       ident[0:r, 0:r])
                    elif kind in ("qk_q", "qk_k"):
                        j = step[1]
                        if j == 0:
                            pe.wait_ge(act, C.value(it, "act", ("t", 1)))
                        for n0, n in COLS:
                            for c in range(2):
                                last = nc.tensor.matmul(flat(buf)[:, n0:n0 + n], wqk[:, c, P * j:P * j + P],
                                                        xT[:, c, n0:n0 + n], start=(c == 0), stop=(c == 1))
                    elif kind == "v":
                        i = step[1]
                        r = TILES[i][1]
                        for half in range(2):
                            w = H2 * DH // 2
                            for c in range(2):
                                last = nc.tensor.matmul(buf[0:r, half, 0:w], xT[:, c, P * i:P * i + r],
                                                        wv[:, c, half * w:half * w + w], start=(c == 0), stop=(c == 1))
                    elif kind in ("max", "exp"):
                        h, i = step[1:]
                        r = TILES[i][1]
                        if kind == "max" and h == 0 and i == 0:
                            pe.wait_ge(act, C.value(it, "act", ("qk_q", 5)))
                            pe.wait_ge(dve, C.value(it, "dve", ("qk_k", 11)))
                        if kind == "exp" and h == 0 and i == 0:
                            pe.wait_ge(max_in, it * 16 + 16)
                        rowsK = DH if kind == "max" else DH + 1
                        a, b = (qT, kT) if kind == "max" else (kT, qT)
                        if i == 4:
                            pe.sem_inc(tick, 1)
                        bank = 0 if i < 4 else 1
                        for n, (n0, w) in enumerate(COLS):
                            last = nc.tensor.matmul(flat(buf)[0:r, n0:n0 + w], a[0:rowsK, h, P * i:P * i + r],
                                                    b[0:rowsK, h, n0:n0 + w], start=True, stop=(n != bank))
                            if n == bank:
                                last = nc.tensor.matmul(flat(buf)[0:r, P * i:P * i + r], eye16[0:r, 0:r],
                                                        mask16[0:r, 0:r], start=False, stop=True)
                    elif kind == "maxt":
                        pe.wait_ge(dve, C.value(it, "dve", ("max", H2 - 1, 4)))
                        for i, r in TILES:
                            last = nc.tensor.transpose(flat(buf)[0:H2, P * i:P * i + r], mx[0:r, i, :], ident[0:r, 0:r])
                    elif kind == "pv":
                        h = step[1]
                        pe.wait_ge(act, C.value(it, "act", ("exp", h, 4)))
                        pe.wait_ge(dve, C.value(it, "dve", ("norm", (h - 1) % H2), turns_back=int(h == 0)))
                        for n0, w in COLS:
                            for i, r in TILES:
                                last = nc.tensor.matmul(flat(acc)[:, n0:n0 + w], vals[0:r, i, h, :],
                                                        probs[h % 2][0:r, i, n0:n0 + w], start=(i == 0), stop=(i == 4))
                    elif kind == "wo":
                        if step[1] == 0:
                            pe.wait_ge(dve, C.value(it, "dve", ("norm", H2 - 1)))
                        for n, i in enumerate(WO_JOBS[step[1]]):
                            r = TILES[i][1]
                            for k in range(6):
                                last = nc.tensor.matmul(buf[0:r, n, 0:D], oT[:, k, P * i:P * i + r], wo[:, k, :],
                                                        start=(k == 0), stop=(k == 5))
                    last.then_inc(mm, 1)

        @block.scalar
        def _(sc):
            sc.sem_inc(act, BASE)
            sc.wait_ge(fixed_in, 96)
            with sc.Fori(0, B) as it:
                for step in C.steps:
                    kind = step[0]
                    if kind not in on_act:
                        continue
                    buf = ring[C.buffer(step)]
                    sc.wait_ge(mm, C.value(it, "mm", step))
                    if kind == "t":
                        nc.scalar.activation(xT[:, step[1], :], flat(buf)[0:KC, 0:N], ACT.Copy).then_inc(act, 1)
                    elif kind == "qk_q":
                        for r in range(2):
                            h = 2 * step[1] + r
                            ins = nc.scalar.activation(qT[0:DH, h, :], flat(buf)[64 * r:64 * r + DH, 0:N], ACT.Copy,
                                                       scale=scale[64 * r:64 * r + DH, h:h + 1])
                        ins.then_inc(act, 1)
                    elif kind == "maxt":
                        nc.scalar.activation(nmax[:, :], flat(buf)[0:H2, 0:N], ACT.Copy, scale=-1.0).then_inc(act, 1)
                    elif kind == "exp":
                        h, i = step[1:]
                        r = TILES[i][1]
                        if i == 0 and h >= 2:
                            sc.wait_ge(mm, C.value(it, "mm", ("pv", h - 2)))
                        nc.scalar.activation(probs[h % 2][0:r, i, :], flat(buf)[0:r, 0:N], ACT.Exp).then_inc(act, 1)

        @block.vector
        def _(v):
            nc.vector.memset(kT[:, :, :], 1.0)
            nc.vector.memset(vals[:, :, :, :], 1.0).then_inc(ready, 1)
            nc.vector.memset(mv[:, :, :], 1.0)
            for s in (mm, dve, ln, stored):
                v.sem_inc(s, BASE)
            v.wait_ge(fixed_in, 96)
            v.wait_ge(ready, 1)
            nc.vector.tensor_copy(eye16[:, :], ident[:, :]).then_inc(ready, 1)
            nc.vector.tensor_scalar(mask16[:, :], ident[:, :], -BIG, None, ALU.mult).then_inc(ready, 1)
            v.wait_ge(ready, 3)
            with v.Fori(0, B) as it:
                v.wait_ge(loaded, it * 32 + 32)
                for i, r in TILES:
                    nc.vector.bn_stats(stats[0:r, i, :], h_in[0:r, i, :]).then_inc(ln, 1)
                v.wait_ge(ln, it * N_LN + (BASE + 5))
                v.sem_inc(tick, 1)
                for i, r in TILES:
                    nc.vector.bn_aggr(mv[0:r, i, :], stats[0:r, i, :]).then_inc(ln, 1)
                v.wait_ge(pool, it * N_POOL + (BASE + 4))
                for i, r in TILES:
                    nc.vector.tensor_scalar(xn[0:r, i, :], h_in[0:r, i, :], mv[0:r, i, 0:1], rstd[0:r, i:i + 1],
                                            ALU.subtract, ALU.mult).then_inc(ln, 1)
                for step in C.steps:
                    kind = step[0]
                    if kind not in on_dve:
                        continue
                    if kind == "norm":
                        h = step[1]
                        v.wait_ge(mm, C.value(it, "mm", ("pv", h)))
                        nc.vector.reciprocal(sums[:, :], flat(acc)[DH:2 * DH, 0:N]).then_inc(ln, 1)
                        v.wait_ge(ln, it * N_LN + (BASE + 16 + h))
                        r0 = DH * (h % 2)
                        nc.vector.tensor_tensor(oT[r0:r0 + DH, h // 2, :], flat(acc)[0:DH, 0:N], sums[:, :],
                                                ALU.mult).then_inc(dve, 1)
                        continue
                    buf = ring[C.buffer(step)]
                    v.wait_ge(mm, C.value(it, "mm", step))
                    if kind == "qk_k":
                        for r in range(2):
                            h = 2 * (step[1] - 6) + r
                            ins = nc.vector.tensor_copy(kT[0:DH, h, :], flat(buf)[64 * r:64 * r + DH, 0:N])
                        ins.then_inc(dve, 1)
                    elif kind == "v":
                        i = step[1]
                        r = TILES[i][1]
                        nc.vector.tensor_copy(vals[0:r, i, :, 0:DH].rearrange("p (a h) d -> p a h d", a=2),
                                              buf[0:r, :, 0:H2 * DH // 2].rearrange("p a (h d) -> p a h d", d=DH)).then_inc(dve, 1)
                    elif kind == "max":
                        h, i = step[1:]
                        r = TILES[i][1]
                        nc.vector.tensor_reduce(mx[0:r, i, h:h + 1], flat(buf)[0:r, 0:N], AX, ALU.max).then_inc(dve, 1)
                    elif kind == "wo":
                        if step[1] == 0:
                            v.wait_ge(stored, it * 32 + BASE)
                        tiles = WO_JOBS[step[1]]
                        r, i = TILES[tiles[0]][1], tiles[0]
                        nc.vector.tensor_tensor(out[0:r, i:i + len(tiles), :], buf[0:r, 0:len(tiles), 0:D],
                                                res[0:r, i:i + len(tiles), :], ALU.add).then_inc(dve, 1)


JOBS3 = ("t", "gate", "ct", "bd", "up", "down")
ON_ACT3 = ("t", "ct", "up")
ON_DVE3 = ("gate", "bd", "down")


def expert_steps():
    out = [("t", 0), ("t", 1), ("gate",), ("ct",)] + [("bd", n) for n in range(4)]
    for e in range(EXPERTS):
        out += [("up", e, m) for m in range(6)]
        if e:
            out.insert(-4, ("down", e - 1, 0))
            out.insert(-4, ("down", e - 1, 1))
    return out + [("down", EXPERTS - 1, 0), ("down", EXPERTS - 1, 1)]


def experts_phase(nc, dram, fused, out_dram):
    C = Counts(expert_steps(), JOBS3, ON_ACT3, ON_DVE3)
    C.looped = True
    assert len(C.jobs) % RING == 0, len(C.jobs)
    E = EXPERTS
    with ExitStack() as ctx:
        sb = lambda n, s, d=F32: ctx.enter_context(nc.sbuf_tensor(n, s, d))
        sem = lambda n: ctx.enter_context(nc.semaphore(n))
        ident = sb("e_ident", [P, P])
        gate_w = sb("gate_w", [KC, 2, E])
        wup = sb("wup", [KC, 2, E, FF])
        bup = sb("bup", [P, E, 6])
        wdown = sb("wdown", [P, 6, E, D])
        bdown = sb("bdown", [E, D])
        tri = sb("tri", [P, 2, E, E])
        h_in = sb("e_h", [P, 5, D])
        xn = sb("e_xn", [P, 5, D])
        xT = sb("e_xT", [KC, 2, N])
        logits = sb("logits", [P, 5, E])
        top = sb("top", [P, 5])
        ex = sb("ex", [P, 5, E])
        total = sb("total", [P, 5])
        pr = sb("pr", [P, 5, E])
        ge = sb("ge", [P, 5, E, E])
        gt = sb("gt", [P, 5, E, E])
        rank = sb("rank", [P, 5, E])
        comb = sb("comb", [P, 5, E])
        combT = sb("combT", [E, N])
        hid = [sb(f"hid{i}", [P, 6, N]) for i in range(2)]
        acc = sb("e_acc", [P, 5, D])
        stats = sb("e_stats", [P, 5, 6])
        mv = sb("e_mv", [P, 5, 2])
        rstd = sb("e_rstd", [P, 5])
        var_eps = sb("e_var_eps", [P, 5])
        half = sb("e_half", [P, 5])
        ring = [ctx.enter_context(nc.psum_tensor(f"e_ring{i}", [P, 2, 512], F32)) for i in range(RING)]
        fixed_in, ready, loaded, mm, act, dve, ln, pool, gate_exp, stored = (sem("e_" + n) for n in (
            "fixed_in", "ready", "loaded", "mm", "act", "dve", "ln", "pool", "gate_exp", "stored"))
        tick = sem("e_tick")
        sems = {"mm": mm, "act": act, "dve": dve}
        N_LN, N_POOL = 15 + 11, 2
        block = ctx.enter_context(nc.Block())

        @block.sync
        def _(sp):
            for dst, src in ((ident[:, :], dram["ident"]), (gate_w[:, :, :], dram["gate_w"]), (wup[:, :, :, :], dram["wup"]),
                             (bup[:, :, :], dram["bup"]), (wdown[:, :, :, :], dram["wdown"]), (bdown[:, :], dram["bdown"]),
                             (tri[:, :, :, :], dram["tri"].partition_broadcast(P))):
                sp.dma_start(dst, src).then_inc(fixed_in, 16)
            with sp.Fori(0, B) as it:
                sp.wait_ge(dve, it * C.total("dve") + BASE)
                full, rest = rows_of(fused, it)
                sp.dma_start(h_in[:, 0:4, :], full).then_inc(loaded, 16)
                sp.dma_start(h_in[0:N - 4 * P, 4, :], rest).then_inc(loaded, 16)
                sp.wait_ge(dve, C.value(it, "dve", ("down", E - 1, 1)))
                full, rest = rows_of(out_dram, it)
                sp.dma_start(full, acc[:, 0:4, :]).then_inc(stored, 16)
                sp.dma_start(rest, acc[0:N - 4 * P, 4, :]).then_inc(stored, 16)
            sp.wait_ge(stored, 32 * B + BASE)

        @block.gpsimd
        def _(g):
            nc.gpsimd.memset(half[:, :], -0.5)
            g.sem_inc(pool, BASE)
            with g.Fori(0, B) as it:
                g.wait_ge(ln, it * N_LN + (BASE + 10))
                rsqrt_steps(nc, g, tick, rstd[:, :], mv[:, :, 1], var_eps[:, :], half[:, :], pool, it * N_POOL + (BASE + 1))

        @block.tensor
        def _(pe):
            pe.wait_ge(fixed_in, 112)
            with pe.Fori(0, B) as it:
                for step in C.steps:
                    kind = step[0]
                    buf = ring[C.buffer(step)]
                    name, value = C.freed(it, step)
                    pe.wait_ge(sems[name], value)
                    if kind == "t":
                        c = step[1]
                        pe.wait_ge(ln, it * N_LN + (BASE + 15))
                        for i, r in TILES:
                            last = nc.tensor.transpose(flat(buf)[0:KC, P * i:P * i + r], xn[0:r, i, KC * c:KC * c + KC],
                                                       ident[0:r, 0:r])
                    elif kind == "gate":
                        pe.wait_ge(act, C.value(it, "act", ("t", 1)))
                        for i, r in TILES:
                            for c in range(2):
                                last = nc.tensor.matmul(buf[0:r, 0, E * i:E * i + E], xT[:, c, P * i:P * i + r], gate_w[:, c, :],
                                                        start=(c == 0), stop=(c == 1))
                    elif kind == "ct":
                        pe.wait_ge(ln, it * N_LN + (BASE + N_LN))
                        for i, r in TILES:
                            last = nc.tensor.transpose(flat(buf)[0:E, P * i:P * i + r], comb[0:r, i, :], ident[0:r, 0:r])
                    elif kind == "bd":
                        if step[1] == 0:
                            pe.wait_ge(act, C.value(it, "act", ("ct",)))
                        for n, i in enumerate(WO_JOBS[step[1]]):
                            r = TILES[i][1]
                            last = nc.tensor.matmul(buf[0:r, n, 0:D], combT[:, P * i:P * i + r], bdown[:, :], start=True, stop=True)
                    elif kind == "up":
                        e, m = step[1:]
                        for n0, n in COLS:
                            for c in range(2):
                                last = nc.tensor.matmul(flat(buf)[:, n0:n0 + n], wup[:, c, e, P * m:P * m + P],
                                                        xT[:, c, n0:n0 + n], start=(c == 0), stop=(c == 1))
                    elif kind == "down":
                        e, part = step[1:]
                        if part == 0:
                            pe.wait_ge(act, C.value(it, "act", ("up", e, 5)))
                        for i in (range(4) if part == 0 else (4,)):
                            r = TILES[i][1]
                            for k in range(6):
                                last = nc.tensor.matmul(buf[0:r, (i % 4) // 2, D * (i % 2):D * (i % 2) + D],
                                                        hid[e % 2][:, k, P * i:P * i + r], wdown[:, k, e, :],
                                                        start=(k == 0), stop=(k == 5))
                    last.then_inc(mm, 1)

        @block.scalar
        def _(sc):
            sc.sem_inc(act, BASE)
            sc.wait_ge(fixed_in, 112)
            with sc.Fori(0, B) as it:
                for step in C.steps:
                    kind = step[0]
                    if kind == "gate":
                        sc.wait_ge(ln, it * N_LN + (BASE + 17))
                        nc.scalar.activation(ex[:, :, :], logits[:, :, :], ACT.Exp).then_inc(gate_exp, 1)
                    if kind not in ON_ACT3:
                        continue
                    buf = ring[C.buffer(step)]
                    sc.wait_ge(mm, C.value(it, "mm", step))
                    if kind == "t":
                        nc.scalar.activation(xT[:, step[1], :], flat(buf)[0:KC, 0:N], ACT.Copy).then_inc(act, 1)
                    elif kind == "ct":
                        nc.scalar.activation(combT[:, :], flat(buf)[0:E, 0:N], ACT.Copy).then_inc(act, 1)
                    elif kind == "up":
                        e, m = step[1:]
                        if m == 0 and e >= 2:
                            sc.wait_ge(mm, C.value(it, "mm", ("down", e - 2, 1)))
                        nc.scalar.activation(hid[e % 2][:, m, :], flat(buf)[:, 0:N], ACT.Gelu, bias=bup[:, e, m:m + 1]).then_inc(act, 1)

        @block.vector
        def _(v):
            nc.vector.memset(mv[:, :, :], 1.0)
            nc.vector.memset(logits[:, :, :], 0.0)
            for s in (mm, dve, ln, stored):
                v.sem_inc(s, BASE)
            v.wait_ge(fixed_in, 112)
            with v.Fori(0, B) as it:
                at = [0]

                def link(ins):
                    at[0] += 1
                    ins.then_inc(ln, 1)
                    v.wait_ge(ln, it * N_LN + (BASE + at[0]))

                v.wait_ge(loaded, it * 32 + 32)
                for i, r in TILES:
                    nc.vector.bn_stats(stats[0:r, i, :], h_in[0:r, i, :]).then_inc(ln, 1)
                v.wait_ge(ln, it * N_LN + (BASE + 5))
                v.sem_inc(tick, 1)
                for i, r in TILES:
                    nc.vector.bn_aggr(mv[0:r, i, :], stats[0:r, i, :]).then_inc(ln, 1)
                v.wait_ge(pool, it * N_POOL + (BASE + 2))
                for i, r in TILES:
                    nc.vector.tensor_scalar(xn[0:r, i, :], h_in[0:r, i, :], mv[0:r, i, 0:1], rstd[0:r, i:i + 1],
                                            ALU.subtract, ALU.mult).then_inc(ln, 1)
                at[0] = 15
                for step in C.steps:
                    kind = step[0]
                    if kind not in ON_DVE3:
                        continue
                    buf = ring[C.buffer(step)]
                    v.wait_ge(mm, C.value(it, "mm", step))
                    if kind == "gate":
                        R = N - 4 * P
                        nc.vector.tensor_copy(logits[:, 0:4, :], buf[:, 0, 0:4 * E].rearrange("p (i e) -> p i e", e=E))
                        ins = nc.vector.tensor_copy(logits[0:R, 4:5, :], buf[0:R, 0, 4 * E:5 * E].rearrange("p (i e) -> p i e", e=E))
                        ins.then_inc(dve, 1)
                        v.wait_ge(dve, C.value(it, "dve", step))
                        link(nc.vector.tensor_reduce(top[:, :], logits[:, :, :], AX, ALU.max))
                        wide = lambda t: t[:, :].rearrange("p (i a) -> p i a", a=1).to_broadcast([P, 5, E])
                        link(nc.vector.tensor_tensor(logits[:, :, :], logits[:, :, :], wide(top), ALU.subtract))
                        v.wait_ge(gate_exp, it + 1)
                        link(nc.vector.tensor_reduce(total[:, :], ex[:, :, :], AX, ALU.add))
                        link(nc.vector.reciprocal(total[:, :], total[:, :]))
                        link(nc.vector.tensor_tensor(pr[:, :, :], ex[:, :, :], wide(total), ALU.mult))
                        for n in range(5):
                            mine = pr[:, n, :].rearrange("p (e a) -> p e a", a=1).to_broadcast([P, E, E])
                            other = pr[:, n, :].rearrange("p (a e) -> p a e", a=1).to_broadcast([P, E, E])
                            nc.vector.tensor_tensor(ge[:, n, :, :], other, mine, ALU.is_ge)
                            ins = nc.vector.tensor_tensor(gt[:, n, :, :], other, mine, ALU.is_gt)
                        link(ins)
                        masked = lambda k: tri[:, k, :, :].rearrange("p (i e) f -> p i (e f)", i=1).to_broadcast([P, 5, E * E])
                        both = lambda t: t[:, :, :, :].rearrange("p i e f -> p i (e f)")
                        nc.vector.tensor_tensor(both(ge), both(ge), masked(0), ALU.mult)
                        link(nc.vector.tensor_tensor(both(gt), both(gt), masked(1), ALU.mult))
                        link(nc.vector.tensor_tensor(both(ge), both(ge), both(gt), ALU.add))
                        link(nc.vector.tensor_reduce(rank[:, :, :], ge[:, :, :, :], AX, ALU.add))
                        link(nc.vector.tensor_scalar(rank[:, :, :], rank[:, :, :], 2.0, None, ALU.is_lt))
                        link(nc.vector.tensor_tensor(comb[:, :, :], pr[:, :, :], rank[:, :, :], ALU.mult))
                    elif kind == "bd":
                        if step[1] == 0:
                            v.wait_ge(stored, it * 32 + BASE)
                        tiles = WO_JOBS[step[1]]
                        r, i = TILES[tiles[0]][1], tiles[0]
                        nc.vector.tensor_tensor(acc[0:r, i:i + len(tiles), :], buf[0:r, 0:len(tiles), 0:D],
                                                h_in[0:r, i:i + len(tiles), :], ALU.add).then_inc(dve, 1)
                    elif kind == "down":
                        e, part = step[1:]
                        before = ("bd", 3) if e == 0 else ("down", e - 1, 1)
                        v.wait_ge(dve, C.value(it, "dve", before))
                        for i in (range(4) if part == 0 else (4,)):
                            r = TILES[i][1]
                            ins = nc.vector.scalar_tensor_tensor(
                                acc[0:r, i, :], buf[0:r, (i % 4) // 2, D * (i % 2):D * (i % 2) + D], comb[0:r, i, e:e + 1],
                                acc[0:r, i, :], ALU.mult, ALU.add)
                        ins.then_inc(dve, 1)
                assert at[0] == N_LN, at[0]


def build(nc, dram, out):
    tokens = nc.dram_tensor("tokens", [B * N, D], F32, kind="Internal").ap()
    fused = nc.dram_tensor("fused", [B * N, D], F32, kind="Internal").ap()
    embed_phase(nc, dram, tokens)
    encoder_phase(nc, dram, tokens)
    attention_phase(nc, dram, tokens, fused)
    experts_phase(nc, dram, fused, out.rearrange("b n d -> (b n) d"))


def kernel(**inputs):
    import concourse.bacc as _bacc
    from concourse.bass_utils import run_bass_kernel_spmd as _run

    a = {k: np.asarray(v) for k, v in inputs.items()}
    con = np.ascontiguousarray
    laid = {}
    x = a["x"].reshape(B, 3, 7, 16, 7, 16).transpose(0, 2, 4, 1, 3, 5).reshape(B * IMG, 768)
    laid["patches"] = x.T.reshape(6, P, B * IMG).transpose(1, 0, 2)
    laid["wproj"] = a["L0_tok_W_proj"].T.reshape(6, P, D).transpose(1, 0, 2)
    laid["tok_rows"] = np.stack([a["L0_tok_b_proj"], a["L0_tok_gamma"], a["L0_tok_beta"]])
    laid["ids"] = a["x_txt"].reshape(B * TXT // P, P).T
    laid["emb"] = a["L0_txt_emb"]
    pe = np.zeros((TXT, D), np.float32)
    where = np.arange(TXT, dtype=np.float32)[:, None]
    div = np.exp(np.arange(0, D, 2, dtype=np.float32) * (-np.log(10000.0) / D))
    pe[:, 0::2] = np.sin(where * div)
    pe[:, 1::2] = np.cos(where * div)
    laid["pos"] = pe.reshape(4, P, D).transpose(1, 0, 2)
    laid["ident"] = np.eye(P, dtype=np.float32)
    chunks = lambda w: w.reshape(w.shape[:-2] + (2, KC, w.shape[-1])).swapaxes(-3, -2)
    laid["wqk"] = chunks(np.concatenate([a["L0_txt_Wq"], a["L0_txt_Wk"]], axis=2))
    laid["wv"] = chunks(a["L0_txt_Wv"])
    laid["bqk"] = np.concatenate([a["L0_txt_bq"], a["L0_txt_bk"]], axis=1).reshape(LAYERS, 3, P).swapaxes(1, 2)
    laid["bv2"] = np.concatenate([a["L0_txt_bv"], a["L0_txt_bv"]], axis=1)
    wo = np.zeros((LAYERS, 3, 4, 32, D), np.float32)
    wo[:, :, :, 0:DK, :] = a["L0_txt_Wo"].reshape(LAYERS, 3, 4, DK, D)
    laid["wo"] = wo.reshape(LAYERS, 3, P, D).swapaxes(1, 2)
    laid["w1"] = chunks(a["L0_txt_W1"])
    laid["b1"] = a["L0_txt_bw1"].reshape(LAYERS, 6, P).swapaxes(1, 2)
    laid["w2"] = a["L0_txt_W2"].reshape(LAYERS, 6, P, D).swapaxes(1, 2)
    laid["enc_rows"] = np.stack([a["L0_txt_" + n] for n in ("bo", "g1", "bn1", "bw2", "g2", "bn2")], axis=1)
    w = a["L0_attn_W_qkv"].T
    laid["a_wqk"] = chunks(w[:, 0:2 * H2 * DH])
    laid["a_wv"] = chunks(w[:, 2 * H2 * DH:])
    laid["a_wo"] = a["L0_attn_W_out"].T.reshape(6, P, D).transpose(1, 0, 2)
    laid["a_scale"] = a["L0_attn_scale"]
    laid["a_bout"] = a["L0_attn_b_out"].reshape(1, D)
    laid["gate_w"] = chunks(a["L0_ffn_gate_w"])
    laid["wup"] = chunks(a["L0_ffn_w_up"]).transpose(1, 2, 0, 3)
    laid["bup"] = a["L0_ffn_b_up"].reshape(EXPERTS, 6, P).transpose(2, 0, 1)
    laid["wdown"] = a["L0_ffn_w_down"].reshape(EXPERTS, 6, P, D).transpose(2, 1, 0, 3)
    laid["bdown"] = a["L0_ffn_b_down"]
    laid["tri"] = np.stack([np.tril(np.ones((EXPERTS, EXPERTS), np.float32), -1),
                            np.triu(np.ones((EXPERTS, EXPERTS), np.float32), 1)])
    nc = _bacc.Bacc("TRN2", target_bir_lowering=False, num_devices=1)
    arrays, dram = {}, {}
    for name, value in laid.items():
        arrays[f"in_{name}"] = con(value)
        dram[name] = nc.dram_tensor(f"in_{name}", value.shape, mybir.dt.from_np(value.dtype), kind="ExternalInput").ap()
    out = nc.dram_tensor("out", (B, N, D), F32, kind="ExternalOutput").ap()
    build(nc, dram, out)
    r = _run(nc, [arrays], core_ids=[0])
    return r.results[0]["out"]
```

```python
import numpy as np
import concourse.bass as bass
from concourse import mybir
from contextlib import ExitStack

F32 = mybir.dt.float32
F32R = mybir.dt.float32r
BF16 = mybir.dt.bfloat16
I32 = mybir.dt.int32
U32 = mybir.dt.uint32
ALU = mybir.AluOpType
ACT = mybir.ActivationFunctionType
AX = mybir.AxisListType.X

B, IMG, TXT, D = 8, 49, 512, 192
N = IMG + TXT
P = 128
KC = 96
EPS = 1e-5
LAYERS, H1, DK = 4, 12, 16
FF = 768
H2, DH = 12, 64
EXPERTS = 8
VOCAB = 8000
BIG = 987654321.0
BASE = 16


def rsqrt_steps(nc, g, tick, rstd, mv, var_eps, half, pool, count):
    g.sem_inc(tick, 1)
    nc.gpsimd.tensor_scalar(var_eps, mv, EPS, None, ALU.add).then_inc(pool, 1)
    g.wait_ge(pool, count)
    nc.gpsimd.tensor_tensor(rstd, var_eps, half, ALU.pow).then_inc(pool, 1)


def embed_phase(nc, dram, tokens):
    TILES = B * TXT // P
    IT = B * IMG // 98
    KT = 768 // P
    with ExitStack() as ctx:
        sb = lambda n, s, d=F32: ctx.enter_context(nc.sbuf_tensor(n, s, d))
        sem = lambda n: ctx.enter_context(nc.semaphore(n))
        ids = sb("ids", [P, TILES], I32)
        idf = sb("idf", [P, TILES])
        neg = sb("neg", [P, TILES])
        idu = sb("idu", [P, TILES], U32)
        words = sb("words", [P, TILES, D])
        pos = sb("pos", [P, 4, D])
        patches = sb("patches", [P, KT, B * IMG])
        wproj = sb("wproj", [P, KT, D])
        rows = sb("tok_rows", [P, 3, D])
        y = sb("tok_y", [P, IT, D])
        z = sb("tok_z", [P, IT, D])
        zero = sb("zero_rows", [P, D])
        stats = sb("tok_stats", [P, IT, 6])
        mv = sb("tok_mv", [P, IT, 2])
        rstd = sb("tok_rstd", [P, IT])
        var_eps = sb("tok_var_eps", [P, IT])
        half = sb("tok_half", [P, IT])
        ps = [ctx.enter_context(nc.psum_tensor(f"tok_ps{i}", [P, 512], F32)) for i in range(IT)]
        ids_in, loaded, gathered, mm, dve, pool, stored = (
            sem(n) for n in ("ids_in", "tok_loaded", "gathered", "tok_mm", "tok_dve", "tok_pool", "tok_stored"))
        tick = sem("tok_tick")
        block = ctx.enter_context(nc.Block())

        @block.sync
        def _(sp):
            sp.dma_start(ids[:, :], dram["ids"]).then_inc(ids_in, 16)
            sp.dma_start(patches[:, :, :], dram["patches"]).then_inc(loaded, 16)
            sp.dma_start(wproj[:, :, :], dram["wproj"]).then_inc(loaded, 16)
            sp.dma_start(rows[:, :, :], dram["tok_rows"].partition_broadcast(P)).then_inc(loaded, 16)
            sp.dma_start(pos[:, :, :], dram["pos"]).then_inc(loaded, 16)
            sp.wait_ge(pool, 7)
            for b in range(B):
                sp.dma_start(tokens[b * N + IMG:(b + 1) * N, :].rearrange("(i p) d -> p i d", p=P),
                             words[:, 4 * b:4 * b + 4, :]).then_inc(stored, 16)
            sp.wait_ge(dve, 6 + 4 * IT)
            for b in range(B):
                p0 = IMG * (b % 2)
                sp.dma_start(tokens[b * N:b * N + IMG, :], z[p0:p0 + IMG, b // 2, :]).then_inc(stored, 16)
            sp.wait_ge(stored, 16 * 2 * B)

        @block.gpsimd
        def _(g):
            g.wait_ge(dve, 4)
            for i in range(TILES):
                g.indirect_dma_start(words[:, i, :], None, dram["emb"],
                                     bass.IndirectOffsetOnAxis(ap=idu[:, i:i + 1], axis=0)).then_inc(gathered, 16)
            g.wait_ge(dve, 4 + 3 * IT)
            nc.gpsimd.memset(half[:, :], -0.5).then_inc(pool, 1)
            g.wait_ge(pool, 1)
            rsqrt_steps(nc, g, tick, rstd[0:98, :], mv[0:98, :, 1], var_eps[0:98, :], half[0:98, :], pool, 2)
            g.wait_ge(gathered, 16 * TILES)
            g.wait_ge(loaded, 64)
            for i in range(4):
                v = words[:, :, :].rearrange("p (b i) d -> p i b d", i=4)[:, i, :, :]
                nc.gpsimd.tensor_tensor(v, v, pos[:, i:i + 1, :].to_broadcast([P, B, D]), ALU.add).then_inc(pool, 1)

        @block.tensor
        def _(pe):
            pe.wait_ge(loaded, 64)
            for i in range(IT):
                for k in range(KT):
                    last = nc.tensor.matmul(ps[i][0:98, 0:D], patches[:, k, 98 * i:98 * i + 98], wproj[:, k, :],
                                            start=(k == 0), stop=(k == KT - 1))
                last.then_inc(mm, 1)

        @block.vector
        def _(v):
            v.wait_ge(ids_in, 16)
            nc.vector.tensor_copy(idf[:, :], ids[:, :]).then_inc(dve, 1)
            v.wait_ge(dve, 1)
            nc.vector.tensor_scalar(neg[:, :], idf[:, :], 0.0, float(VOCAB), ALU.is_lt, ALU.mult).then_inc(dve, 1)
            v.wait_ge(dve, 2)
            nc.vector.tensor_tensor(idf[:, :], idf[:, :], neg[:, :], ALU.add).then_inc(dve, 1)
            v.wait_ge(dve, 3)
            nc.vector.tensor_scalar(idu[:, :], idf[:, :], 0.0, float(VOCAB - 1), ALU.max, ALU.min).then_inc(dve, 1)
            for i in range(IT):
                v.wait_ge(mm, i + 1)
                nc.vector.tensor_tensor(y[0:98, i, :], ps[i][0:98, 0:D], rows[0:98, 0, :], ALU.add).then_inc(dve, 1)
                v.wait_ge(dve, 5 + 3 * i)
                nc.vector.bn_stats(stats[0:98, i, :], y[0:98, i, :]).then_inc(dve, 1)
                v.wait_ge(dve, 6 + 3 * i)
                nc.vector.bn_aggr(mv[0:98, i, :], stats[0:98, i, :]).then_inc(dve, 1)
            v.wait_ge(pool, 3)
            for i in range(IT):
                nc.vector.tensor_scalar(z[0:98, i, :], y[0:98, i, :], mv[0:98, i, 0:1], rstd[0:98, i:i + 1],
                                        ALU.subtract, ALU.mult).then_inc(dve, 1)
            c = 4 + 4 * IT
            v.wait_ge(dve, c)
            nc.vector.tensor_tensor(y[0:98, :, :], z[0:98, :, :], rows[0:98, 1:2, :].to_broadcast([98, IT, D]), ALU.mult).then_inc(dve, 1)
            v.wait_ge(dve, c + 1)
            nc.vector.tensor_tensor(z[0:98, :, :], y[0:98, :, :], rows[0:98, 2:3, :].to_broadcast([98, IT, D]), ALU.add).then_inc(dve, 1)


RING = 3
JOBS = ("tx", "qk", "v", "max", "maxt", "exp", "wo", "ft", "f1", "f2")
ON_ACT = ("tx", "qk", "maxt", "exp", "ft", "f1")
ON_DVE = ("qk", "v", "max", "norm", "wo", "f2")


def spread(main, side):
    out, done = [], 0
    for i, step in enumerate(main):
        out.append(step)
        due = len(side) * (i + 1) // len(main)
        out, done = out + side[done:due], due
    return out


def attend_steps(s):
    out, due, pieces = [], [], []
    for n in range(6):
        for hh in range(4):
            out.append(("exp", s, n, hh))
            out, pieces = out + pieces[:1], pieces[1:]
            due = [(left - 1, step) for left, step in due]
            if due and due[0][0] == 0:
                out.append(due.pop(0)[1])
                if n % 2 == 0:
                    pieces = [("norm", s, n // 2 - 1, p) for p in range(PIECES + 1)]
        due.append((2, ("pv", s, n)))
    return out + [step for _, step in due] + [("norm", s, 2, p) for p in range(PIECES + 1)]


def project_steps(s):
    return [("tx", s), ("qk", s, 0), ("qk", s, 1), ("qk", s, 2), ("v", s)]


def max_steps(s):
    return [("max", s, h, a) for h in range(H1) for a in range(2)]


PIECES = 4
M0, M1 = max_steps(0) + [("maxt", 0)], max_steps(1) + [("maxt", 1)]
EXP0, EXP1 = attend_steps(0), attend_steps(1)
SIDE = ([("wo", 0)] + project_steps(0) + [("ft", 0), ("f1", 0, 0), ("f1", 0, 1)] + M0[0:4] + [("f1", 0, 2)] + M0[4:8]
        + [("f2", 0)] + M0[8:12])
TAIL = ([("tx", 1), M0[12], ("qk", 1, 0), M0[13], ("qk", 1, 1), ("qk", 1, 2), ("wo", 1), ("v", 1)] + M0[14:20]
        + [("ft", 1)] + M0[20:22] + [("f1", 1, 0)] + M0[22:25] + [("f1", 1, 1), ("f1", 1, 2), ("f2", 1)])
BODY = spread(EXP0[:-8], M1) + EXP0[-8:] + spread(EXP1, SIDE) + TAIL
AHEAD = project_steps(0) + project_steps(1) + M0


class Counts:

    def __init__(self, steps, jobs, on_act, on_dve, start=None, first_job=0):
        self.steps, self.on_dve, self.first_job = steps, on_dve, first_job
        number = lambda kinds: {s: n for n, s in enumerate(x for x in steps if x[0] in kinds)}
        self.jobs = number(jobs)
        self.tables = {"mm": number(jobs + ("pv",)), "act": number(on_act), "dve": number(on_dve)}
        self.start = start or {"mm": BASE, "act": BASE, "dve": BASE}

    def total(self, name):
        return len(self.tables[name])

    def end(self):
        return {name: self.start[name] + self.total(name) for name in self.tables}

    def value(self, turn, name, step, turns_back=0):
        fixed = self.start[name] + self.tables[name][step] + 1 - turns_back * self.total(name)
        return turn * self.total(name) + fixed if self.looped else fixed

    looped = False

    def buffer(self, step):
        return (self.jobs[step] + self.first_job) % RING

    def freed(self, turn, step):
        j, order = self.jobs[step], list(self.jobs)
        if j < RING and not self.looped:
            return None
        before = order[j - RING]
        name = "dve" if before[0] in self.on_dve else "act"
        return name, self.value(turn, name, before, turns_back=1 if j < RING else 0)


def encoder_phase(nc, dram, tokens):
    ahead_jobs = sum(x[0] in JOBS for x in AHEAD)
    PRO = Counts(AHEAD, JOBS, ON_ACT, ON_DVE, first_job=-ahead_jobs % RING)
    LOOP = Counts(BODY, JOBS, ON_ACT, ON_DVE, start=PRO.end())
    LOOP.looped = True
    assert len(LOOP.jobs) % RING == 0
    TURNS = LAYERS * B // 2
    with ExitStack() as ctx:
        sb = lambda n, s, d=F32: ctx.enter_context(nc.sbuf_tensor(n, s, d))
        sem = lambda n: ctx.enter_context(nc.semaphore(n))
        two = lambda n, s, d=F32: [sb(f"{n}{i}", s, d) for i in range(2)]
        ident = sb("ident", [P, P])
        wqk = sb("wqk", [KC, 2, 2 * D])
        wv = sb("wv", [KC, 2, D])
        bqk = sb("bqk", [P, 3])
        bv = sb("bv_rows", [P, 2 * D])
        wo = sb("wo", [P, 3, D])
        w1 = sb("w1", [KC, 2, FF])
        b1 = sb("b1", [P, 6])
        w2 = sb("w2", [P, 6, D])
        rows = sb("enc_rows", [P, 6, D])
        h_in = two("h_in", [P, 4, D])
        res = two("res", [P, 4, D])
        hT = sb("hT", [KC, 2, TXT])
        qk_hi = sb("qk_hi", [P, 3, TXT], F32R)
        qk_lo = sb("qk_lo", [P, 3, TXT], F32R)
        q_st = two("q_stack", [P, 2, H1 // 2, TXT], F32R)
        k_st = two("k_stack", [P, H1 // 2, TXT], F32R)
        vals = two("vals", [P, 4, H1, 32])
        mx = two("mx", [P, 4, H1])
        nmax = sb("nmax", [H1, TXT], F32R)
        probs = two("probs", [P, 4, 2, TXT])
        sums = sb("sums", [P, TXT])
        oT = sb("oT", [P, 3, TXT])
        h1 = sb("h1", [P, 4, D])
        h1T = sb("h1T", [KC, 2, TXT])
        relu = sb("relu", [P, 6, TXT])
        y = sb("y", [P, 4, D])
        yn = sb("yn", [P, 4, D])
        h_out = sb("h_out", [P, 4, D])
        stats = sb("stats", [P, 4, 6])
        mv = sb("mv", [P, 4, 2])
        rstd = sb("rstd", [P, 4])
        var_eps = sb("var_eps", [P, 4])
        half = sb("half", [P, 4])
        ring = [ctx.enter_context(nc.psum_tensor(f"ring{i}", [P, 2, 512], F32)) for i in range(RING)]
        acc = [ctx.enter_context(nc.psum_tensor(f"acc{i}", [P, 512], F32)) for i in range(2)]
        qk_dram = [nc.dram_tensor(f"qk_scratch{s}", [2, 2 * D, TXT], F32, kind="Internal").ap() for s in range(2)]

        fixed_in, mm, act, dve, ln, pool = (sem(n) for n in ("fixed_in", "mm", "act", "dve", "ln", "pool"))
        wx_in, wf_in = sem("wx_in"), sem("wf_in")
        h_loaded, spilled, stacked, max_in, stored = ([sem(f"{n}{s}") for s in range(2)] for n in
                                                      ("h_loaded", "spilled", "stacked", "max_in", "stored"))
        ones_set, tick = sem("ones_set"), sem("tick")
        h_dram = tokens[0:B * N, :].rearrange("(b n) d -> b n d", n=N)[:, IMG:N, :].rearrange(
            "b (i p) d -> b p i d", p=P)
        pool_at, count = {("res", 0): 1, ("res", 1): 2}, 2
        ln_at, links = {}, 0
        for step in BODY:
            if step[0] == "norm" and step[3]:
                links += 1
            elif step[0] in ("wo", "f2"):
                which = 1 if step[0] == "wo" else 2
                pool_at[("rstd", step[1], which)] = count + 2
                pool_at[("ln", step[1], which)] = count + 4
                count += 4
                if which == 1:
                    count += 1
                    pool_at[("res2", step[1])] = count
                ln_at[(step[1], which)] = (links + 8, links + 12)
                links += 12
        N_POOL, N_LN = count, links
        POOL_BASE = N_POOL

        def pool_value(it, *piece, turns_back=0):
            return it * N_POOL + (POOL_BASE + pool_at[piece] - turns_back * N_POOL)

        sems = {"mm": mm, "act": act, "dve": dve}
        block = ctx.enter_context(nc.Block())

        @block.tensor
        def _(pe):
            pe.wait_ge(fixed_in, 16)

            def steps(counts, it):
                k = it if counts is LOOP else 0
                loads = 1 if counts is LOOP else 0
                for step in counts.steps:
                    kind, s = step[0], step[1]
                    if kind == "norm":
                        continue
                    if kind != "pv":
                        buf = ring[counts.buffer(step)]
                        freed = counts.freed(it, step)
                        if freed:
                            pe.wait_ge(sems[freed[0]], freed[1])
                    if kind == "tx":
                        pe.wait_ge(h_loaded[s], k * 16 + 16 * (1 + loads))
                        for c in range(2):
                            for i in range(4):
                                last = nc.tensor.transpose(buf[0:KC, c, P * i:P * i + P], h_in[s][:, i, KC * c:KC * c + KC],
                                                           ident[:, :])
                    elif kind == "qk":
                        m = step[2]
                        if m == 0:
                            pe.wait_ge(act, counts.value(it, "act", ("tx", s)))
                            pe.wait_ge(wx_in, k * 64 + 64 * (1 + loads))
                        for c in range(2):
                            last = nc.tensor.matmul(buf[:, 0, :], wqk[:, c, P * m:P * m + P], hT[:, c, :],
                                                    start=(c == 0), stop=(c == 1))
                    elif kind == "v":
                        for i in range(4):
                            for c in range(2):
                                last = nc.tensor.matmul(buf[:, i // 2, D * (i % 2):D * (i % 2) + D],
                                                        hT[:, c, P * i:P * i + P], wv[:, c, :],
                                                        start=(c == 0), stop=(c == 1))
                    elif kind == "max":
                        h, a = step[2:]
                        r, t = h % 2, h // 2
                        if h == 0 and a == 0:
                            ahead = loads if s == 0 else 0
                            pe.wait_ge(stacked[s], k * 224 + 224 * (1 + ahead))
                            pe.wait_ge(ones_set, 1)
                        for i in (2 * a, 2 * a + 1):
                            last = nc.tensor.matmul(buf[:, i % 2, :], q_st[s][:, r, t, P * i:P * i + P],
                                                    k_st[s][:, t, :], start=True, stop=True)
                    elif kind == "maxt":
                        pe.wait_ge(dve, counts.value(it, "dve", ("max", s, H1 - 1, 1)))
                        for i in range(4):
                            last = nc.tensor.transpose(buf[0:H1, 0, P * i:P * i + P], mx[s][:, i, :], ident[:, :])
                    elif kind == "exp":
                        n, hh = step[2:]
                        h = 4 * (n // 2) + hh
                        r, t = h % 2, h // 2
                        if n == 0 and hh == 0:
                            pe.wait_ge(max_in[s], k * 32 + 32)
                        for j in range(2):
                            kt = 2 * (n % 2) + j
                            last = nc.tensor.matmul(buf[:, j, :], k_st[s][:, t, P * kt:P * kt + P],
                                                    q_st[s][:, r, t, :], start=True, stop=True)
                    elif kind == "pv":
                        n = step[2]
                        g = 3 * s + n // 2
                        pe.wait_ge(act, counts.value(it, "act", ("exp", s, n, 3)))
                        if n % 2 == 0:
                            back = (g - 2) % 6
                            pe.wait_ge(dve, counts.value(it, "dve", ("norm", back // 3, back % 3, PIECES),
                                                               turns_back=int(g < 2)))
                        for j in range(2):
                            kt = 2 * (n % 2) + j
                            for hh in range(4):
                                last = nc.tensor.matmul(acc[g % 2][32 * hh:32 * hh + 32, :],
                                                        vals[s][:, kt, 4 * (n // 2) + hh, :], probs[n % 2][:, hh, j, :],
                                                        start=(n % 2 == 0 and j == 0), stop=(n % 2 == 1 and j == 1),
                                                        tile_position=(0, 32 * hh), skip_group_check=True)
                    elif kind == "wo":
                        pe.wait_ge(wf_in, k * 80 + 80)
                        for i in range(4):
                            pe.wait_ge(dve, counts.value(it, "dve", ("norm", s, 2, 1 + i)))
                            for g in range(3):
                                last = nc.tensor.matmul(buf[:, i // 2, D * (i % 2):D * (i % 2) + D],
                                                        oT[:, g, P * i:P * i + P], wo[:, g, :],
                                                        start=(g == 0), stop=(g == 2))
                    elif kind == "ft":
                        pe.wait_ge(pool, pool_value(it, "ln", s, 1))
                        for c in range(2):
                            for i in range(4):
                                last = nc.tensor.transpose(buf[0:KC, c, P * i:P * i + P], h1[:, i, KC * c:KC * c + KC],
                                                           ident[:, :])
                    elif kind == "f1":
                        m = step[2]
                        if m == 0:
                            pe.wait_ge(act, counts.value(it, "act", ("ft", s)))
                        for j in range(2):
                            for c in range(2):
                                f = P * (2 * m + j)
                                last = nc.tensor.matmul(buf[:, j, :], w1[:, c, f:f + P], h1T[:, c, :],
                                                        start=(c == 0), stop=(c == 1))
                    elif kind == "f2":
                        pe.wait_ge(act, counts.value(it, "act", ("f1", s, 2)))
                        for i in range(4):
                            for k2 in range(6):
                                last = nc.tensor.matmul(buf[:, i // 2, D * (i % 2):D * (i % 2) + D],
                                                        relu[:, k2, P * i:P * i + P], w2[:, k2, :],
                                                        start=(k2 == 0), stop=(k2 == 5))
                    last.then_inc(mm, 1)

            steps(PRO, 0)
            with pe.Fori(0, TURNS) as it:
                steps(LOOP, it)

        @block.scalar
        def _(sc):
            def steps(counts, it):
                for step in counts.steps:
                    kind, s = step[0], step[1]
                    if kind not in ON_ACT:
                        continue
                    buf = ring[counts.buffer(step)]
                    sc.wait_ge(mm, counts.value(it, "mm", step))
                    if kind == "tx":
                        nc.scalar.activation(hT[:, :, :], buf[0:KC, :, :], ACT.Copy).then_inc(act, 1)
                    elif kind == "qk":
                        m = step[2]
                        if m == 0:
                            if counts is LOOP:
                                sc.wait_ge(spilled[1 - s], it * 32 + (32 if s == 0 else 64))
                            elif s == 1:
                                sc.wait_ge(spilled[0], 32)
                        nc.scalar.activation(qk_hi[:, m, :], buf[:, 0, :], ACT.Identity, bias=bqk[:, m:m + 1]).then_inc(act, 1)
                    elif kind == "maxt":
                        nc.scalar.activation(nmax[:, :], buf[0:H1, 0, :], ACT.Copy, scale=-1.0).then_inc(act, 1)
                    elif kind == "exp":
                        n, hh = step[2:]
                        if hh == 0:
                            back = 6 * s + n - 2
                            if back >= 0:
                                sc.wait_ge(mm, counts.value(it, "mm", ("pv", back // 6, back % 6)))
                        nc.scalar.activation(probs[n % 2][:, hh, :, :], buf[:, :, :], ACT.Exp,
                                             scale=DK ** -0.5).then_inc(act, 1)
                    elif kind == "ft":
                        nc.scalar.activation(h1T[:, :, :], buf[0:KC, :, :], ACT.Copy).then_inc(act, 1)
                    elif kind == "f1":
                        m = step[2]
                        nc.scalar.activation(relu[:, 2 * m, :], buf[:, 0, :], ACT.Relu, bias=b1[:, 2 * m:2 * m + 1])
                        nc.scalar.activation(relu[:, 2 * m + 1, :], buf[:, 1, :], ACT.Relu,
                                             bias=b1[:, 2 * m + 1:2 * m + 2]).then_inc(act, 1)

            sc.sem_inc(act, BASE)
            sc.wait_ge(wx_in, 64)
            steps(PRO, 0)
            with sc.Fori(0, TURNS) as it:
                steps(LOOP, it)

        @block.vector
        def _(v):
            def steps(counts, it):
                link_at = [0]

                def link(ins):
                    link_at[0] += 1
                    ins.then_inc(ln, 1)
                    v.wait_ge(ln, it * N_LN + (BASE + link_at[0]))

                def layer_norm(s, which):
                    for i in range(4):
                        last = nc.vector.bn_stats(stats[:, i, :], y[:, i, :])
                        if i < 3:
                            last.then_inc(ln, 1)
                            link_at[0] += 1
                    link(last)
                    v.sem_inc(tick, 1)
                    for i in range(4):
                        last = nc.vector.bn_aggr(mv[:, i, :], stats[:, i, :])
                        last.then_inc(ln, 1)
                        link_at[0] += 1
                    v.wait_ge(pool, pool_value(it, "rstd", s, which))
                    for i in range(4):
                        nc.vector.tensor_scalar(yn[:, i, :], y[:, i, :], mv[:, i, 0:1], rstd[:, i:i + 1],
                                                ALU.subtract, ALU.mult).then_inc(ln, 1)
                        link_at[0] += 1

                for step in counts.steps:
                    kind, s = step[0], step[1]
                    if kind not in ON_DVE:
                        continue
                    if kind == "norm":
                        g, p = step[2:]
                        a, back = acc[(3 * s + g) % 2], (3 * s + g - 1) % 6
                        if p == 0:
                            v.wait_ge(mm, counts.value(it, "mm", ("pv", s, 2 * g + 1)))
                            v.wait_ge(dve, counts.value(it, "dve", ("norm", back // 3, back % 3, PIECES),
                                                        turns_back=int(3 * s + g < 1)))
                            v.sem_inc(tick, 1)
                            nc.vector.stream_shuffle(sums[:, :], a[:, :], [16 + i % 16 for i in range(32)]).then_inc(dve, 1)
                        else:
                            if p == 1:
                                v.wait_ge(dve, counts.value(it, "dve", ("norm", s, g, 0)))
                            t = slice(P * (p - 1), P * p)
                            link(nc.vector.reciprocal(sums[:, t], sums[:, t]))
                            nc.vector.tensor_tensor(oT[:, g, t], a[:, t], sums[:, t], ALU.mult).then_inc(dve, 1)
                        continue
                    buf = ring[counts.buffer(step)]
                    if kind == "qk":
                        m = step[2]
                        v.wait_ge(act, counts.value(it, "act", step))
                        nc.vector.scalar_tensor_tensor(qk_lo[:, m, :], buf[:, 0, :], bqk[:, m:m + 1],
                                                       qk_hi[:, m, :].bitcast(F32), ALU.add, ALU.subtract).then_inc(dve, 1)
                        continue
                    v.wait_ge(mm, counts.value(it, "mm", step))
                    if kind == "v":
                        nc.vector.tensor_tensor(
                            vals[s][:, :, :, 0:DK].rearrange("p (a b) h d -> p a (b h) d", a=2),
                            buf[:, :, 0:2 * D].rearrange("p a (h d) -> p a h d", d=DK),
                            bv[:, :].rearrange("p (a h d) -> p a h d", a=1, d=DK).to_broadcast([P, 2, 2 * H1, DK]),
                            ALU.add).then_inc(dve, 1)
                    elif kind == "max":
                        h, a = step[2:]
                        row = (h % 2) * 6 + h // 2
                        nc.vector.tensor_reduce(mx[s][:, 2 * a:2 * a + 2, row], buf[:, :, :], AX, ALU.max).then_inc(dve, 1)
                    elif kind in ("wo", "f2"):
                        if kind == "wo":
                            v.wait_ge(pool, pool_value(it, "res", s))
                        if kind == "f2":
                            v.wait_ge(pool, pool_value(it, "res2", s))
                        r = res[s]
                        v.wait_ge(ln, it * N_LN + (BASE + link_at[0]))
                        link_y = nc.vector.tensor_tensor(y[:, :, :].rearrange("p (a b) d -> p a (b d)", a=2), buf[:, :, 0:2 * D],
                                                         r[:, :, :].rearrange("p (a b) d -> p a (b d)", a=2), ALU.add)
                        link_y.then_inc(dve, 1)
                        v.wait_ge(dve, counts.value(it, "dve", step))
                        layer_norm(s, 1 if kind == "wo" else 2)
                return link_at[0]

            for s in range(2):
                nc.vector.memset(k_st[s][:, :, :].bitcast(F32), 1.0)
                nc.vector.memset(q_st[s][:, :, :, :].bitcast(F32), 0.0)
                last = nc.vector.memset(vals[s][:, :, :, :], 1.0)
            last.then_inc(ones_set, 1)
            v.sem_inc(mm, BASE)
            v.sem_inc(dve, BASE)
            v.sem_inc(ln, BASE)
            v.wait_ge(wx_in, 64)
            v.wait_ge(ones_set, 1)
            steps(PRO, 0)
            with v.Fori(0, TURNS) as it:
                links = steps(LOOP, it)
            assert links == N_LN, links

        @block.gpsimd
        def _(g):
            def lane(name):
                return {"bo": 0, "g1": 1, "bn1": 2, "bw2": 3, "g2": 4, "bn2": 5}[name]

            wide = lambda name: rows[:, lane(name):lane(name) + 1, :].to_broadcast([P, 4, D])
            nc.gpsimd.memset(half[:, :], -0.5)
            g.sem_inc(pool, POOL_BASE)
            with g.Fori(0, TURNS) as it:
                g.wait_ge(wf_in, it * 80 + 80)
                g.wait_ge(dve, it * LOOP.total("dve") + LOOP.start["dve"])
                for s in range(2):
                    g.wait_ge(h_loaded[s], it * 16 + 16)
                    nc.gpsimd.tensor_tensor(res[s][:, :, :], h_in[s][:, :, :], wide("bo"), ALU.add).then_inc(pool, 1)
                for step in LOOP.steps:
                    kind, s = step[0], step[1]
                    if kind in ("wo", "f2"):
                        which = 1 if kind == "wo" else 2
                        moments, normed = ln_at[(s, which)]
                        g.wait_ge(ln, it * N_LN + (BASE + moments))
                        rsqrt_steps(nc, g, tick, rstd[:, :], mv[:, :, 1], var_eps[:, :], half[:, :], pool,
                                    pool_value(it, "rstd", s, which) - 1)
                        g.wait_ge(ln, it * N_LN + (BASE + normed))
                        out = h1 if which == 1 else h_out
                        if which == 2:
                            g.wait_ge(stored[1 - s], it * 16 + 16 * (1 + s))
                        nc.gpsimd.tensor_tensor(out[:, :, :], yn[:, :, :], wide("g1" if which == 1 else "g2"),
                                                ALU.mult).then_inc(pool, 1)
                        g.wait_ge(pool, pool_value(it, "ln", s, which) - 1)
                        nc.gpsimd.tensor_tensor(out[:, :, :], out[:, :, :], wide("bn1" if which == 1 else "bn2"),
                                                ALU.add).then_inc(pool, 1)
                        g.wait_ge(pool, pool_value(it, "ln", s, which))
                        if which == 1:
                            nc.gpsimd.tensor_tensor(res[s][:, :, :], out[:, :, :], wide("bw2"), ALU.add).then_inc(pool, 1)

        @block.sync
        def _(sp):
            def load_project_weights(layer):
                sp.dma_start(wqk[:, :, :], dram["wqk"][layer]).then_inc(wx_in, 16)
                sp.dma_start(wv[:, :, :], dram["wv"][layer]).then_inc(wx_in, 16)
                sp.dma_start(bqk[:, :], dram["bqk"][layer]).then_inc(wx_in, 16)
                sp.dma_start(bv[:, :], dram["bv2"][layer].partition_broadcast(P)).then_inc(wx_in, 16)

            def spill_and_stack(counts, it, s, before_count):
                sp.wait_ge(act, counts.value(it, "act", ("qk", s, 2)))
                sp.sem_inc(tick, 1)
                sp.wait_ge(dve, counts.value(it, "dve", ("qk", s, 2)))
                for part, t in ((0, qk_hi), (1, qk_lo)):
                    sp.dma_start(qk_dram[s][part].rearrange("(m p) n -> p m n", p=P),
                                 t[:, :, :].bitcast(F32)).then_inc(spilled[s], 16)
                sp.wait_ge(spilled[s], before_count)
                for r in range(2):
                    for st, first, parts in ((q_st, 0, (0, 1, 0)), (k_st, D, (0, 0, 1))):
                        for c, part in enumerate(parts):
                            src = qk_dram[s][part][first:first + D, :].rearrange("(t r d) n -> r d t n", r=2, d=DK)
                            p0 = 64 * r + DK * c
                            dst = st[s][p0:p0 + DK, r, :, :] if st is q_st else st[s][p0:p0 + DK, :, :]
                            sp.dma_start(dst.bitcast(F32), src[r]).then_inc(stacked[s], 16)
                    p0, other = 64 * r + 3 * DK, 64 * (1 - r) + 3 * DK
                    sp.dma_start(q_st[s][p0:p0 + 1, r, :, :].bitcast(F32),
                                 q_st[s][other:other + 1, r, :, :].bitcast(F32)).then_inc(stacked[s], 16)

            def max_row(counts, it, s):
                sp.wait_ge(act, counts.value(it, "act", ("maxt", s)))
                for r in range(2):
                    p0 = 64 * r + 3 * DK
                    sp.dma_start(q_st[s][p0:p0 + 1, r, :, :].bitcast(F32),
                                 nmax[6 * r:6 * r + 6, :].bitcast(F32)).then_inc(max_in[s], 16)

            def store(it, s):
                sp.wait_ge(pool, pool_value(it, "ln", s, 2))
                sp.sem_inc(tick, 1)
                sp.dma_start(h_dram[(it % 4) * 2 + s], h_out[:, :, :]).then_inc(stored[s], 16)

            for s in range(2):
                sp.sem_inc(stored[s], 16)
            sp.dma_start(ident[:, :], dram["ident"]).then_inc(fixed_in, 16)
            load_project_weights(0)
            for s in range(2):
                sp.dma_start(h_in[s][:, :, :], h_dram[s]).then_inc(h_loaded[s], 16)
            sp.wait_ge(ones_set, 1)
            for s in range(2):
                spill_and_stack(PRO, 0, s, 32)
            max_row(PRO, 0, 0)
            with sp.Fori(0, TURNS) as it:
                nxt = (it + 1) % TURNS
                sp.wait_ge(dve, it * LOOP.total("dve") + LOOP.start["dve"])
                sp.sem_inc(tick, 1)
                load_project_weights(nxt // 4)
                sp.wait_ge(pool, it * N_POOL + POOL_BASE)
                sp.sem_inc(tick, 1)
                layer = it // 4
                sp.dma_start(wo[:, :, :], dram["wo"][layer]).then_inc(wf_in, 16)
                sp.dma_start(w1[:, :, :], dram["w1"][layer]).then_inc(wf_in, 16)
                sp.dma_start(b1[:, :], dram["b1"][layer]).then_inc(wf_in, 16)
                sp.dma_start(w2[:, :, :], dram["w2"][layer]).then_inc(wf_in, 16)
                sp.dma_start(rows[:, :, :], dram["enc_rows"][layer].partition_broadcast(P)).then_inc(wf_in, 16)
                for s in range(2):
                    sp.wait_ge(pool, pool_value(it, "res", s))
                    sp.wait_ge(stored[s], it * 16 + 16)
                    sp.sem_inc(tick, 1)
                    sp.dma_start(h_in[s][:, :, :], h_dram[(nxt % 4) * 2 + s]).then_inc(h_loaded[s], 16)
                max_row(LOOP, it, 1)
                spill_and_stack(LOOP, it, 0, it * 32 + 64)
                store(it, 0)
                spill_and_stack(LOOP, it, 1, it * 32 + 64)
                max_row(LOOP, it, 0)
                store(it, 1)
            for s in range(2):
                sp.wait_ge(stored[s], 16 * TURNS + 16)
                sp.wait_ge(stacked[s], 224 * (TURNS + 1))
                sp.wait_ge(max_in[s], 32 * (TURNS + 1 - s))


TILES = [(i, min(P, N - P * i)) for i in range((N + P - 1) // P)]
WO_JOBS = ((0, 1), (2,), (3,), (4,))
NE = N + N % 2
COLS = ((0, 2 * P), (2 * P, N - 2 * P))
COLS_E = ((0, 2 * P), (2 * P, NE - 2 * P))


GH = 4
GROUPS = H2 // GH
LAST = 6


def scores_steps(g):
    heads = range(GH * g, GH * g + GH)
    out = [("qk", x, h) for h in heads if h % 2 == 0 for x in ("q", "k")]
    if g == 0:
        out += [("v", i) for i, _ in TILES]
    return out + [("max", h, i) for h in heads for i, _ in TILES] + [("maxt", g)]


def weigh_steps(g):
    out = []
    for h in range(GH * g, GH * g + GH):
        after = {0: [("norm", h - 2, 3)], 1: [("norm", h - 2, 4), ("pv", h - 1), ("take", h - 1)],
                 2: [("norm", h - 1, 0)], 3: [("norm", h - 1, 1)], 4: [("norm", h - 1, 2)]}
        for kt, _ in TILES:
            out += [("exp", h, kt)] + [x for x in after[kt] if x[1] >= 0]
            if (h, kt) in ((GH * (GROUPS - 1) + 1, 0), (GH * GROUPS - 1, 0)):
                out.append(("ln", 0 if kt or h < GH * GROUPS - 1 else 1))
    return out


def fused_steps():
    out = [("t", 0), ("t", 1)] + scores_steps(0)
    for g in range(GROUPS):
        main, side = weigh_steps(g), scores_steps(g + 1) if g + 1 < GROUPS else []
        out += spread(main[:-LAST], side) + main[-LAST:]
    out += [("norm", H2 - 2, 3), ("norm", H2 - 2, 4), ("pv", H2 - 1), ("take", H2 - 1)]
    return out + [("norm", H2 - 1, i) for i, _ in TILES] + [("wo", i) for i, _ in TILES]


def slot(h):
    return h % (2 * GH)


def flat(buf):
    return buf[:, :, :].rearrange("p a b -> p (a b)")[:, 512 - 2 * P:1024]


def rows_of(t, b):
    v = t[:, :].rearrange("(b n) d -> b n d", n=N)
    return (v[:, 0:4 * P, :].rearrange("b (i p) d -> b p i d", p=P)[b], v[:, 4 * P:N, :][b])


def attention_phase(nc, dram, tokens, fused):
    steps_list = fused_steps()
    on_act, on_dve = ("t", "qk", "maxt", "exp", "take"), ("qk", "v", "max", "norm", "wo")
    C = Counts(steps_list, ("t", "qk", "v", "max", "maxt", "exp", "wo"), on_act, on_dve)
    C.looped = True
    assert len(C.jobs) % RING == 0, len(C.jobs)
    with ExitStack() as ctx:
        sb = lambda n, s, d=F32: ctx.enter_context(nc.sbuf_tensor(n, s, d))
        sem = lambda n: ctx.enter_context(nc.semaphore(n))
        ident = sb("a_ident", [P, P])
        eye16 = sb("eye16", [P, P], BF16)
        mask16 = sb("mask16", [P, P], BF16)
        wqk = sb("a_wqk", [KC, 2, 2 * H2 * DH])
        wv = sb("a_wv", [KC, 2, H2 * DH])
        wo = sb("a_wo", [P, 6, D])
        scale = sb("a_scale", [P, H2])
        b_out = sb("a_bout", [P, 1, D])
        h_in = sb("a_h", [P, 5, D])
        res = sb("a_res", [P, 5, D])
        xn = sb("a_xn", [P, 5, D])
        xT = sb("a_xT", [KC, 2, N])
        q_hl = sb("a_q_hl", [P, 2 * GH, NE], F32R)
        k_hh = sb("a_k_hh", [P, 2 * GH, NE], F32R)
        q_hm = sb("a_q_hm", [P, 2 * GH, NE], F32R)
        k_l1 = sb("a_k_l1", [P, 2 * GH, NE], F32R)
        vals = sb("a_vals", [P, 5, H2, 2 * DH])
        mx = sb("a_mx", [P, 5, H2])
        nmax = sb("a_nmax", [GH, N], F32R)
        zeros = sb("a_zeros", [2 * GH, NE])
        probs = [sb(f"a_probs{i}", [P, 5, N]) for i in range(2)]
        taken = [sb(f"a_taken{i}", [P, N]) for i in range(2)]
        oT = sb("a_oT", [P, 6, N])
        stats = sb("a_stats", [P, 5, 6])
        mv = sb("a_mv", [P, 5, 2])
        rstd = sb("a_rstd", [P, 5])
        var_eps = sb("a_var_eps", [P, 5])
        half = sb("a_half", [P, 5])
        ring = [ctx.enter_context(nc.psum_tensor(f"a_ring{i}", [P, 2, 512], F32)) for i in range(RING)]
        acc = ctx.enter_context(nc.psum_tensor("a_acc", [P, 2, 512], F32))
        fixed_in, ready, loaded, mm, act, dve, ln, pool, max_in, stored = (sem("a_" + n) for n in (
            "fixed_in", "ready", "loaded", "mm", "act", "dve", "ln", "pool", "max_in", "stored"))
        zeroed, copied, recip, pool_res = sem("a_zeroed"), sem("a_copied"), sem("a_recip"), sem("a_pool_res")
        tick = sem("a_tick")
        sems = {"mm": mm, "act": act, "dve": dve}
        block = ctx.enter_context(nc.Block())

        @block.sync
        def _(sp):
            def load(b):
                full, rest = rows_of(tokens, b)
                sp.dma_start(h_in[:, 0:4, :], full).then_inc(loaded, 16)
                sp.dma_start(h_in[0:N - 4 * P, 4, :], rest).then_inc(loaded, 16)

            for dst, src in ((ident[:, :], dram["ident"]), (wqk[:, :, :], dram["a_wqk"]), (wv[:, :, :], dram["a_wv"]),
                             (wo[:, :, :], dram["a_wo"]), (scale[:, :], dram["a_scale"].partition_broadcast(P)),
                             (b_out[:, :, :], dram["a_bout"].partition_broadcast(P))):
                sp.dma_start(dst, src).then_inc(fixed_in, 16)
            load(0)
            sp.dma_start(tokens[B * N:(B + 1) * N, :], tokens[0:N, :]).then_inc(copied, 16)
            sp.wait_ge(copied, 16)
            sp.wait_ge(ready, 3)
            with sp.Fori(0, B) as it:
                for g in range(GROUPS):
                    if g == 0:
                        sp.wait_ge(mm, C.value(it, "mm", ("exp", H2 - 1, 4), turns_back=1))
                        sp.dma_start(q_hm[DH:DH + 1, :, :].bitcast(F32), zeros[:, :]).then_inc(zeroed, 16)
                    elif g == 1:
                        sp.wait_ge(ln, it * 15 + (BASE + 15))
                        sp.wait_ge(pool_res, it * 2 + (BASE + 2))
                        load(it + 1)
                    elif g == 2:
                        sp.wait_ge(mm, C.value(it, "mm", ("exp", GH - 1, 4)))
                        sp.dma_start(q_hm[DH:DH + 1, 0:GH, :].bitcast(F32), zeros[0:GH, :]).then_inc(zeroed, 16)
                    sp.wait_ge(act, C.value(it, "act", ("maxt", g)))
                    sp.dma_start(q_hm[DH:DH + 1, slot(GH * g):slot(GH * g) + GH, 0:N].bitcast(F32),
                                 nmax[:, :].bitcast(F32)).then_inc(max_in, 16)
                sp.wait_ge(dve, C.value(it, "dve", ("wo", 4)))
                full, rest = rows_of(fused, it)
                sp.dma_start(full, res[:, 0:4, :]).then_inc(stored, 16)
                sp.dma_start(rest, res[0:N - 4 * P, 4, :]).then_inc(stored, 16)
            sp.wait_ge(stored, 32 * B + BASE)
            sp.wait_ge(max_in, 16 * GROUPS * B)
            sp.wait_ge(zeroed, 32 * B)

        @block.gpsimd
        def _(g):
            nc.gpsimd.memset(half[:, :], -0.5)
            g.sem_inc(pool, BASE)
            g.sem_inc(pool_res, BASE)
            g.wait_ge(fixed_in, 96)

            def moments_to_rstd(b):
                g.wait_ge(ln, b * 15 + (BASE + 10))
                rsqrt_steps(nc, g, tick, rstd[:, :], mv[:, :, 1], var_eps[:, :], half[:, :], pool, b * 2 + (BASE + 1))

            moments_to_rstd(0)
            with g.Fori(0, B) as it:
                g.wait_ge(loaded, it * 32 + 32)
                g.wait_ge(stored, it * 32 + BASE)
                for t, r in ((slice(0, 4), P), (slice(4, 5), N - 4 * P)):
                    nt = t.stop - t.start
                    nc.gpsimd.tensor_tensor(res[0:r, t, :], h_in[0:r, t, :], b_out[0:r, :, :].to_broadcast([r, nt, D]),
                                            ALU.add).then_inc(pool_res, 1)
                moments_to_rstd(it + 1)

        @block.tensor
        def _(pe):
            pe.wait_ge(fixed_in, 96)
            pe.wait_ge(ready, 5)
            with pe.Fori(0, B) as it:
                for step in C.steps:
                    kind = step[0]
                    if kind in ("take", "norm", "ln"):
                        continue
                    if kind != "pv":
                        buf = ring[C.buffer(step)]
                        name, value = C.freed(it, step)
                        pe.wait_ge(sems[name], value)
                    if kind == "t":
                        c = step[1]
                        pe.wait_ge(ln, it * 15 + (BASE + 15))
                        for i, r in TILES:
                            last = nc.tensor.transpose(flat(buf)[0:KC, P * i:P * i + r], xn[0:r, i, KC * c:KC * c + KC],
                                                       ident[0:r, 0:r])
                    elif kind == "qk":
                        j = step[2] // 2 + (6 if step[1] == "k" else 0)
                        if step[1:] == ("q", 0):
                            pe.wait_ge(act, C.value(it, "act", ("t", 1)))
                        for n0, n in COLS:
                            for c in range(2):
                                last = nc.tensor.matmul(flat(buf)[:, n0:n0 + n], wqk[:, c, P * j:P * j + P],
                                                        xT[:, c, n0:n0 + n], start=(c == 0), stop=(c == 1))
                    elif kind == "v":
                        i = step[1]
                        r = TILES[i][1]
                        for half in range(2):
                            w = H2 * DH // 2
                            for c in range(2):
                                last = nc.tensor.matmul(buf[0:r, half, 0:w], xT[:, c, P * i:P * i + r],
                                                        wv[:, c, half * w:half * w + w], start=(c == 0), stop=(c == 1))
                    elif kind in ("max", "exp"):
                        h, i = step[1:]
                        r = TILES[i][1]
                        s = slot(h)
                        if kind == "max" and i == 0:
                            pe.wait_ge(dve, C.value(it, "dve", ("qk", "k", h - h % 2)))
                            pe.wait_ge(zeroed, it * 32 + (16 if h < 2 * GH else 32))
                        if kind == "exp" and h % GH == 0 and i == 0:
                            pe.wait_ge(max_in, it * (16 * GROUPS) + 16 * (h // GH + 1))
                        rows = slice(P * i, P * i + r)
                        if kind == "max":
                            pairs = ((q_hl[:, s, rows], k_hh[:, s, :]), (q_hm[:, s, rows], k_l1[:, s, :]))
                        else:
                            pairs = ((k_hh[:, s, rows], q_hl[:, s, :]), (k_l1[:, s, rows], q_hm[:, s, :]))
                        if i == 4:
                            pe.sem_inc(tick, 1)
                        bank = 0 if i < 2 else 1
                        for n, (n0, w) in enumerate(COLS_E):
                            for m, (a, b) in enumerate(pairs):
                                last = nc.tensor.matmul(flat(buf)[0:r, n0:n0 + w], a, b[:, n0:n0 + w],
                                                        start=(m == 0), stop=(m == 1 and n != bank))
                            if n == bank:
                                last = nc.tensor.matmul(flat(buf)[0:r, P * i:P * i + r], eye16[0:r, 0:r],
                                                        mask16[0:r, 0:r], start=False, stop=True)
                    elif kind == "maxt":
                        h = GH * step[1]
                        pe.wait_ge(dve, C.value(it, "dve", ("max", h + GH - 1, 4)))
                        for i, r in TILES:
                            last = nc.tensor.transpose(flat(buf)[0:GH, P * i:P * i + r], mx[0:r, i, h:h + GH], ident[0:r, 0:r])
                    elif kind == "pv":
                        h = step[1]
                        pe.wait_ge(act, C.value(it, "act", ("exp", h, 4)))
                        pe.wait_ge(act, C.value(it, "act", ("take", (h - 1) % H2), turns_back=int(h == 0)))
                        for n0, w in COLS:
                            for i, r in TILES:
                                last = nc.tensor.matmul(flat(acc)[:, n0:n0 + w], vals[0:r, i, h, :],
                                                        probs[h % 2][0:r, i, n0:n0 + w], start=(i == 0), stop=(i == 4))
                    elif kind == "wo":
                        pe.wait_ge(dve, C.value(it, "dve", ("norm", H2 - 1, step[1])))
                        i, r = TILES[step[1]]
                        for k in range(6):
                            last = nc.tensor.matmul(buf[0:r, 0, 0:D], oT[:, k, P * i:P * i + r], wo[:, k, :],
                                                    start=(k == 0), stop=(k == 5))
                    last.then_inc(mm, 1)

        @block.scalar
        def _(sc):
            sc.sem_inc(act, BASE)
            sc.wait_ge(fixed_in, 96)
            with sc.Fori(0, B) as it:
                for step in C.steps:
                    kind = step[0]
                    if kind not in on_act:
                        continue
                    if kind == "take":
                        h = step[1]
                        sc.wait_ge(mm, C.value(it, "mm", ("pv", h)))
                        sc.wait_ge(dve, C.value(it, "dve", ("norm", (h - 2) % H2, 4), turns_back=int(h < 2)))
                        nc.scalar.activation(taken[h % 2][:, :], flat(acc)[:, 0:N], ACT.Copy).then_inc(act, 1)
                        continue
                    buf = ring[C.buffer(step)]
                    sc.wait_ge(mm, C.value(it, "mm", step))
                    if kind == "t":
                        nc.scalar.activation(xT[:, step[1], :], flat(buf)[0:KC, 0:N], ACT.Copy).then_inc(act, 1)
                    elif kind == "qk":
                        for r in range(2):
                            src = flat(buf)[DH * r:DH * r + DH, 0:N]
                            h = step[2] + r
                            if step[1] == "q":
                                for dst in (q_hm[0:DH], q_hl[0:DH]):
                                    ins = nc.scalar.activation(dst[:, slot(h), 0:N], src, ACT.Copy,
                                                               scale=scale[DH * r:DH * r + DH, h:h + 1])
                            else:
                                for dst in (k_hh[DH:P], k_hh[0:DH]):
                                    ins = nc.scalar.activation(dst[:, slot(h), 0:N], src, ACT.Copy)
                        ins.then_inc(act, 1)
                    elif kind == "maxt":
                        nc.scalar.activation(nmax[:, :], flat(buf)[0:GH, 0:N], ACT.Copy, scale=-1.0).then_inc(act, 1)
                    elif kind == "exp":
                        h, i = step[1:]
                        r = TILES[i][1]
                        if i == 0 and h >= 2:
                            sc.wait_ge(mm, C.value(it, "mm", ("pv", h - 2)))
                        nc.scalar.activation(probs[h % 2][0:r, i, :], flat(buf)[0:r, 0:N], ACT.Exp).then_inc(act, 1)

        @block.vector
        def _(v):
            nc.vector.memset(zeros[:, :], 0.0)
            for t in (q_hm, k_l1):
                nc.vector.memset(t[:, :, :].bitcast(F32), 0.0).then_inc(ready, 1)
            for t in (q_hl, k_hh):
                nc.vector.memset(t[:, :, N:NE].bitcast(F32), 0.0)
            v.wait_ge(ready, 2)
            nc.vector.memset(k_l1[DH:DH + 1, :, :].bitcast(F32), 1.0)
            nc.vector.memset(vals[:, :, :, :], 1.0).then_inc(ready, 1)
            nc.vector.memset(mv[:, :, :], 1.0)
            for s in (mm, dve, ln, recip, stored):
                v.sem_inc(s, BASE)
            v.wait_ge(fixed_in, 96)
            v.wait_ge(ready, 3)
            nc.vector.tensor_copy(eye16[:, :], ident[:, :]).then_inc(ready, 1)
            nc.vector.tensor_scalar(mask16[:, :], ident[:, :], -BIG, None, ALU.mult).then_inc(ready, 1)
            v.wait_ge(ready, 5)

            def moments(b):
                v.wait_ge(loaded, b * 32 + 32)
                for i, r in TILES:
                    nc.vector.bn_stats(stats[0:r, i, :], h_in[0:r, i, :]).then_inc(ln, 1)
                v.wait_ge(ln, b * 15 + (BASE + 5))
                v.sem_inc(tick, 1)
                for i, r in TILES:
                    nc.vector.bn_aggr(mv[0:r, i, :], stats[0:r, i, :]).then_inc(ln, 1)

            def normalise(b):
                v.wait_ge(pool, b * 2 + (BASE + 2))
                for i, r in TILES:
                    nc.vector.tensor_scalar(xn[0:r, i, :], h_in[0:r, i, :], mv[0:r, i, 0:1], rstd[0:r, i:i + 1],
                                            ALU.subtract, ALU.mult).then_inc(ln, 1)

            moments(0)
            normalise(0)
            with v.Fori(0, B) as it:
                for step in C.steps:
                    kind = step[0]
                    if kind == "ln":
                        (moments, normalise)[step[1]](it + 1)
                    if kind not in on_dve:
                        continue
                    if kind == "norm":
                        h, i = step[1:]
                        r0, t = DH * (h % 2), slice(P * i, P * i + TILES[i][1])
                        v.wait_ge(act, C.value(it, "act", ("take", h)))
                        nc.vector.reciprocal(taken[h % 2][DH:2 * DH, t], taken[h % 2][DH:2 * DH, t]).then_inc(recip, 1)
                        v.wait_ge(recip, it * (5 * H2) + (BASE + 1 + 5 * h + i))
                        nc.vector.tensor_tensor(oT[r0:r0 + DH, h // 2, t], taken[h % 2][0:DH, t],
                                                taken[h % 2][DH:2 * DH, t], ALU.mult).then_inc(dve, 1)
                        continue
                    buf = ring[C.buffer(step)]
                    if kind == "qk":
                        v.wait_ge(act, C.value(it, "act", step))
                        for r in range(2):
                            h, s = step[2] + r, slot(step[2] + r)
                            src = flat(buf)[DH * r:DH * r + DH, 0:N]
                            if step[1] == "q":
                                ins = nc.vector.scalar_tensor_tensor(q_hl[DH:P, s, 0:N], src, scale[DH * r:DH * r + DH, h:h + 1],
                                                               q_hl[0:DH, s, 0:N].bitcast(F32), ALU.mult, ALU.subtract)
                            else:
                                ins = nc.vector.tensor_tensor(k_l1[0:DH, s, 0:N], src, k_hh[0:DH, s, 0:N].bitcast(F32), ALU.subtract)
                        ins.then_inc(dve, 1)
                        continue
                    v.wait_ge(mm, C.value(it, "mm", step))
                    if kind == "v":
                        i = step[1]
                        r = TILES[i][1]
                        nc.vector.tensor_copy(vals[0:r, i, :, 0:DH].rearrange("p (a h) d -> p a h d", a=2),
                                              buf[0:r, :, 0:H2 * DH // 2].rearrange("p a (h d) -> p a h d", d=DH)).then_inc(dve, 1)
                    elif kind == "max":
                        h, i = step[1:]
                        r = TILES[i][1]
                        nc.vector.tensor_reduce(mx[0:r, i, h:h + 1], flat(buf)[0:r, 0:N], AX, ALU.max).then_inc(dve, 1)
                    elif kind == "wo":
                        i, r = TILES[step[1]]
                        if i == 0:
                            v.wait_ge(pool_res, it * 2 + (BASE + 2))
                        nc.vector.tensor_tensor(res[0:r, i, :], buf[0:r, 0, 0:D], res[0:r, i, :], ALU.add).then_inc(dve, 1)


JOBS3 = ("t", "gate", "ct", "bd", "up", "down")
ON_ACT3 = ("t", "ct", "up")
ON_DVE3 = ("gate", "bd", "down")


def expert_steps():
    out = [("t", 0), ("t", 1), ("gate",), ("ct",)] + [("bd", n) for n in range(4)]
    for e in range(EXPERTS):
        out += [("up", e, m) for m in range(6)]
        if e:
            out.insert(-4, ("down", e - 1, 0))
            out.insert(-4, ("down", e - 1, 1))
    return out + [("down", EXPERTS - 1, 0), ("down", EXPERTS - 1, 1)]


def experts_phase(nc, dram, fused, out_dram):
    C = Counts(expert_steps(), JOBS3, ON_ACT3, ON_DVE3)
    C.looped = True
    assert len(C.jobs) % RING == 0, len(C.jobs)
    E = EXPERTS
    with ExitStack() as ctx:
        sb = lambda n, s, d=F32: ctx.enter_context(nc.sbuf_tensor(n, s, d))
        sem = lambda n: ctx.enter_context(nc.semaphore(n))
        ident = sb("e_ident", [P, P])
        gate_w = sb("gate_w", [KC, 2, E])
        wup = sb("wup", [KC, 2, E, FF])
        bup = sb("bup", [P, E, 6])
        wdown = sb("wdown", [P, 6, E, D])
        bdown = sb("bdown", [E, D])
        tri = sb("tri", [P, 2, E, E])
        h_in = sb("e_h", [P, 5, D])
        xn = sb("e_xn", [P, 5, D])
        xT = sb("e_xT", [KC, 2, N])
        logits = sb("logits", [P, 5, E])
        top = sb("top", [P, 5])
        ex = sb("ex", [P, 5, E])
        total = sb("total", [P, 5])
        pr = sb("pr", [P, 5, E])
        ge = sb("ge", [P, 5, E, E])
        gt = sb("gt", [P, 5, E, E])
        rank = sb("rank", [P, 5, E])
        comb = sb("comb", [P, 5, E])
        combT = sb("combT", [E, N])
        hid = [sb(f"hid{i}", [P, 6, N]) for i in range(2)]
        acc = sb("e_acc", [P, 5, D])
        stats = sb("e_stats", [P, 5, 6])
        mv = sb("e_mv", [P, 5, 2])
        rstd = sb("e_rstd", [P, 5])
        var_eps = sb("e_var_eps", [P, 5])
        half = sb("e_half", [P, 5])
        ring = [ctx.enter_context(nc.psum_tensor(f"e_ring{i}", [P, 2, 512], F32)) for i in range(RING)]
        fixed_in, ready, loaded, mm, act, dve, ln, pool, gate_exp, stored = (sem("e_" + n) for n in (
            "fixed_in", "ready", "loaded", "mm", "act", "dve", "ln", "pool", "gate_exp", "stored"))
        tick = sem("e_tick")
        sems = {"mm": mm, "act": act, "dve": dve}
        N_LN, N_POOL = 15 + 11, 2
        block = ctx.enter_context(nc.Block())

        @block.sync
        def _(sp):
            for dst, src in ((ident[:, :], dram["ident"]), (gate_w[:, :, :], dram["gate_w"]), (wup[:, :, :, :], dram["wup"]),
                             (bup[:, :, :], dram["bup"]), (wdown[:, :, :, :], dram["wdown"]), (bdown[:, :], dram["bdown"]),
                             (tri[:, :, :, :], dram["tri"].partition_broadcast(P))):
                sp.dma_start(dst, src).then_inc(fixed_in, 16)
            with sp.Fori(0, B) as it:
                sp.wait_ge(dve, it * C.total("dve") + BASE)
                full, rest = rows_of(fused, it)
                sp.dma_start(h_in[:, 0:4, :], full).then_inc(loaded, 16)
                sp.dma_start(h_in[0:N - 4 * P, 4, :], rest).then_inc(loaded, 16)
                sp.wait_ge(dve, C.value(it, "dve", ("down", E - 1, 1)))
                full, rest = rows_of(out_dram, it)
                sp.dma_start(full, acc[:, 0:4, :]).then_inc(stored, 16)
                sp.dma_start(rest, acc[0:N - 4 * P, 4, :]).then_inc(stored, 16)
            sp.wait_ge(stored, 32 * B + BASE)

        @block.gpsimd
        def _(g):
            nc.gpsimd.memset(half[:, :], -0.5)
            g.sem_inc(pool, BASE)
            with g.Fori(0, B) as it:
                g.wait_ge(ln, it * N_LN + (BASE + 10))
                rsqrt_steps(nc, g, tick, rstd[:, :], mv[:, :, 1], var_eps[:, :], half[:, :], pool, it * N_POOL + (BASE + 1))

        @block.tensor
        def _(pe):
            pe.wait_ge(fixed_in, 112)
            with pe.Fori(0, B) as it:
                for step in C.steps:
                    kind = step[0]
                    buf = ring[C.buffer(step)]
                    name, value = C.freed(it, step)
                    pe.wait_ge(sems[name], value)
                    if kind == "t":
                        c = step[1]
                        pe.wait_ge(ln, it * N_LN + (BASE + 15))
                        for i, r in TILES:
                            last = nc.tensor.transpose(flat(buf)[0:KC, P * i:P * i + r], xn[0:r, i, KC * c:KC * c + KC],
                                                       ident[0:r, 0:r])
                    elif kind == "gate":
                        pe.wait_ge(act, C.value(it, "act", ("t", 1)))
                        for i, r in TILES:
                            for c in range(2):
                                last = nc.tensor.matmul(buf[0:r, 0, E * i:E * i + E], xT[:, c, P * i:P * i + r], gate_w[:, c, :],
                                                        start=(c == 0), stop=(c == 1))
                    elif kind == "ct":
                        pe.wait_ge(ln, it * N_LN + (BASE + N_LN))
                        for i, r in TILES:
                            last = nc.tensor.transpose(flat(buf)[0:E, P * i:P * i + r], comb[0:r, i, :], ident[0:r, 0:r])
                    elif kind == "bd":
                        if step[1] == 0:
                            pe.wait_ge(act, C.value(it, "act", ("ct",)))
                        for n, i in enumerate(WO_JOBS[step[1]]):
                            r = TILES[i][1]
                            last = nc.tensor.matmul(buf[0:r, n, 0:D], combT[:, P * i:P * i + r], bdown[:, :], start=True, stop=True)
                    elif kind == "up":
                        e, m = step[1:]
                        for n0, n in COLS:
                            for c in range(2):
                                last = nc.tensor.matmul(flat(buf)[:, n0:n0 + n], wup[:, c, e, P * m:P * m + P],
                                                        xT[:, c, n0:n0 + n], start=(c == 0), stop=(c == 1))
                    elif kind == "down":
                        e, part = step[1:]
                        if part == 0:
                            pe.wait_ge(act, C.value(it, "act", ("up", e, 5)))
                        for i in (range(4) if part == 0 else (4,)):
                            r = TILES[i][1]
                            for k in range(6):
                                last = nc.tensor.matmul(buf[0:r, (i % 4) // 2, D * (i % 2):D * (i % 2) + D],
                                                        hid[e % 2][:, k, P * i:P * i + r], wdown[:, k, e, :],
                                                        start=(k == 0), stop=(k == 5))
                    last.then_inc(mm, 1)

        @block.scalar
        def _(sc):
            sc.sem_inc(act, BASE)
            sc.wait_ge(fixed_in, 112)
            with sc.Fori(0, B) as it:
                for step in C.steps:
                    kind = step[0]
                    if kind == "gate":
                        sc.wait_ge(ln, it * N_LN + (BASE + 17))
                        nc.scalar.activation(ex[:, :, :], logits[:, :, :], ACT.Exp).then_inc(gate_exp, 1)
                    if kind not in ON_ACT3:
                        continue
                    buf = ring[C.buffer(step)]
                    sc.wait_ge(mm, C.value(it, "mm", step))
                    if kind == "t":
                        nc.scalar.activation(xT[:, step[1], :], flat(buf)[0:KC, 0:N], ACT.Copy).then_inc(act, 1)
                    elif kind == "ct":
                        nc.scalar.activation(combT[:, :], flat(buf)[0:E, 0:N], ACT.Copy).then_inc(act, 1)
                    elif kind == "up":
                        e, m = step[1:]
                        if m == 0 and e >= 2:
                            sc.wait_ge(mm, C.value(it, "mm", ("down", e - 2, 1)))
                        nc.scalar.activation(hid[e % 2][:, m, :], flat(buf)[:, 0:N], ACT.Gelu, bias=bup[:, e, m:m + 1]).then_inc(act, 1)

        @block.vector
        def _(v):
            nc.vector.memset(mv[:, :, :], 1.0)
            nc.vector.memset(logits[:, :, :], 0.0)
            for s in (mm, dve, ln, stored):
                v.sem_inc(s, BASE)
            v.wait_ge(fixed_in, 112)
            with v.Fori(0, B) as it:
                at = [0]

                def link(ins):
                    at[0] += 1
                    ins.then_inc(ln, 1)
                    v.wait_ge(ln, it * N_LN + (BASE + at[0]))

                v.wait_ge(loaded, it * 32 + 32)
                for i, r in TILES:
                    nc.vector.bn_stats(stats[0:r, i, :], h_in[0:r, i, :]).then_inc(ln, 1)
                v.wait_ge(ln, it * N_LN + (BASE + 5))
                v.sem_inc(tick, 1)
                for i, r in TILES:
                    nc.vector.bn_aggr(mv[0:r, i, :], stats[0:r, i, :]).then_inc(ln, 1)
                v.wait_ge(pool, it * N_POOL + (BASE + 2))
                for i, r in TILES:
                    nc.vector.tensor_scalar(xn[0:r, i, :], h_in[0:r, i, :], mv[0:r, i, 0:1], rstd[0:r, i:i + 1],
                                            ALU.subtract, ALU.mult).then_inc(ln, 1)
                at[0] = 15
                for step in C.steps:
                    kind = step[0]
                    if kind not in ON_DVE3:
                        continue
                    buf = ring[C.buffer(step)]
                    v.wait_ge(mm, C.value(it, "mm", step))
                    if kind == "gate":
                        R = N - 4 * P
                        nc.vector.tensor_copy(logits[:, 0:4, :], buf[:, 0, 0:4 * E].rearrange("p (i e) -> p i e", e=E))
                        ins = nc.vector.tensor_copy(logits[0:R, 4:5, :], buf[0:R, 0, 4 * E:5 * E].rearrange("p (i e) -> p i e", e=E))
                        ins.then_inc(dve, 1)
                        v.wait_ge(dve, C.value(it, "dve", step))
                        link(nc.vector.tensor_reduce(top[:, :], logits[:, :, :], AX, ALU.max))
                        wide = lambda t: t[:, :].rearrange("p (i a) -> p i a", a=1).to_broadcast([P, 5, E])
                        link(nc.vector.tensor_tensor(logits[:, :, :], logits[:, :, :], wide(top), ALU.subtract))
                        v.wait_ge(gate_exp, it + 1)
                        link(nc.vector.tensor_reduce(total[:, :], ex[:, :, :], AX, ALU.add))
                        link(nc.vector.reciprocal(total[:, :], total[:, :]))
                        link(nc.vector.tensor_tensor(pr[:, :, :], ex[:, :, :], wide(total), ALU.mult))
                        for n in range(5):
                            mine = pr[:, n, :].rearrange("p (e a) -> p e a", a=1).to_broadcast([P, E, E])
                            other = pr[:, n, :].rearrange("p (a e) -> p a e", a=1).to_broadcast([P, E, E])
                            nc.vector.tensor_tensor(ge[:, n, :, :], other, mine, ALU.is_ge)
                            ins = nc.vector.tensor_tensor(gt[:, n, :, :], other, mine, ALU.is_gt)
                        link(ins)
                        masked = lambda k: tri[:, k, :, :].rearrange("p (i e) f -> p i (e f)", i=1).to_broadcast([P, 5, E * E])
                        both = lambda t: t[:, :, :, :].rearrange("p i e f -> p i (e f)")
                        nc.vector.tensor_tensor(both(ge), both(ge), masked(0), ALU.mult)
                        link(nc.vector.tensor_tensor(both(gt), both(gt), masked(1), ALU.mult))
                        link(nc.vector.tensor_tensor(both(ge), both(ge), both(gt), ALU.add))
                        link(nc.vector.tensor_reduce(rank[:, :, :], ge[:, :, :, :], AX, ALU.add))
                        link(nc.vector.tensor_scalar(rank[:, :, :], rank[:, :, :], 2.0, None, ALU.is_lt))
                        link(nc.vector.tensor_tensor(comb[:, :, :], pr[:, :, :], rank[:, :, :], ALU.mult))
                    elif kind == "bd":
                        if step[1] == 0:
                            v.wait_ge(stored, it * 32 + BASE)
                        tiles = WO_JOBS[step[1]]
                        r, i = TILES[tiles[0]][1], tiles[0]
                        nc.vector.tensor_tensor(acc[0:r, i:i + len(tiles), :], buf[0:r, 0:len(tiles), 0:D],
                                                h_in[0:r, i:i + len(tiles), :], ALU.add).then_inc(dve, 1)
                    elif kind == "down":
                        e, part = step[1:]
                        before = ("bd", 3) if e == 0 else ("down", e - 1, 1)
                        v.wait_ge(dve, C.value(it, "dve", before))
                        for i in (range(4) if part == 0 else (4,)):
                            r = TILES[i][1]
                            ins = nc.vector.scalar_tensor_tensor(
                                acc[0:r, i, :], buf[0:r, (i % 4) // 2, D * (i % 2):D * (i % 2) + D], comb[0:r, i, e:e + 1],
                                acc[0:r, i, :], ALU.mult, ALU.add)
                        ins.then_inc(dve, 1)
                assert at[0] == N_LN, at[0]


def build(nc, dram, out):
    tokens = nc.dram_tensor("tokens", [(B + 1) * N, D], F32, kind="Internal").ap()
    fused = nc.dram_tensor("fused", [B * N, D], F32, kind="Internal").ap()
    embed_phase(nc, dram, tokens)
    encoder_phase(nc, dram, tokens)
    attention_phase(nc, dram, tokens, fused)
    experts_phase(nc, dram, fused, out.rearrange("b n d -> (b n) d"))


def kernel(**inputs):
    import concourse.bacc as _bacc
    from concourse.bass_utils import run_bass_kernel_spmd as _run

    a = {k: np.asarray(v) for k, v in inputs.items()}
    con = np.ascontiguousarray
    laid = {}
    x = a["x"].reshape(B, 3, 7, 16, 7, 16).transpose(0, 2, 4, 1, 3, 5).reshape(B * IMG, 768)
    laid["patches"] = x.T.reshape(6, P, B * IMG).transpose(1, 0, 2)
    laid["wproj"] = a["L0_tok_W_proj"].T.reshape(6, P, D).transpose(1, 0, 2)
    laid["tok_rows"] = np.stack([a["L0_tok_b_proj"], a["L0_tok_gamma"], a["L0_tok_beta"]])
    laid["ids"] = a["x_txt"].reshape(B * TXT // P, P).T
    laid["emb"] = a["L0_txt_emb"]
    pe = np.zeros((TXT, D), np.float32)
    where = np.arange(TXT, dtype=np.float32)[:, None]
    div = np.exp(np.arange(0, D, 2, dtype=np.float32) * (-np.log(10000.0) / D))
    pe[:, 0::2] = np.sin(where * div)
    pe[:, 1::2] = np.cos(where * div)
    laid["pos"] = pe.reshape(4, P, D).transpose(1, 0, 2)
    laid["ident"] = np.eye(P, dtype=np.float32)
    chunks = lambda w: w.reshape(w.shape[:-2] + (2, KC, w.shape[-1])).swapaxes(-3, -2)
    laid["wqk"] = chunks(np.concatenate([a["L0_txt_Wq"], a["L0_txt_Wk"]], axis=2))
    laid["wv"] = chunks(a["L0_txt_Wv"])
    laid["bqk"] = np.concatenate([a["L0_txt_bq"], a["L0_txt_bk"]], axis=1).reshape(LAYERS, 3, P).swapaxes(1, 2)
    laid["bv2"] = np.concatenate([a["L0_txt_bv"], a["L0_txt_bv"]], axis=1)
    wo = np.zeros((LAYERS, 3, 4, 32, D), np.float32)
    wo[:, :, :, 0:DK, :] = a["L0_txt_Wo"].reshape(LAYERS, 3, 4, DK, D)
    laid["wo"] = wo.reshape(LAYERS, 3, P, D).swapaxes(1, 2)
    laid["w1"] = chunks(a["L0_txt_W1"])
    laid["b1"] = a["L0_txt_bw1"].reshape(LAYERS, 6, P).swapaxes(1, 2)
    laid["w2"] = a["L0_txt_W2"].reshape(LAYERS, 6, P, D).swapaxes(1, 2)
    laid["enc_rows"] = np.stack([a["L0_txt_" + n] for n in ("bo", "g1", "bn1", "bw2", "g2", "bn2")], axis=1)
    w = a["L0_attn_W_qkv"].T
    laid["a_wqk"] = chunks(w[:, 0:2 * H2 * DH])
    laid["a_wv"] = chunks(w[:, 2 * H2 * DH:])
    laid["a_wo"] = a["L0_attn_W_out"].T.reshape(6, P, D).transpose(1, 0, 2)
    laid["a_scale"] = a["L0_attn_scale"]
    laid["a_bout"] = a["L0_attn_b_out"].reshape(1, D)
    laid["gate_w"] = chunks(a["L0_ffn_gate_w"])
    laid["wup"] = chunks(a["L0_ffn_w_up"]).transpose(1, 2, 0, 3)
    laid["bup"] = a["L0_ffn_b_up"].reshape(EXPERTS, 6, P).transpose(2, 0, 1)
    laid["wdown"] = a["L0_ffn_w_down"].reshape(EXPERTS, 6, P, D).transpose(2, 1, 0, 3)
    laid["bdown"] = a["L0_ffn_b_down"]
    laid["tri"] = np.stack([np.tril(np.ones((EXPERTS, EXPERTS), np.float32), -1),
                            np.triu(np.ones((EXPERTS, EXPERTS), np.float32), 1)])
    nc = _bacc.Bacc("TRN2", target_bir_lowering=False, num_devices=1)
    arrays, dram = {}, {}
    for name, value in laid.items():
        arrays[f"in_{name}"] = con(value)
        dram[name] = nc.dram_tensor(f"in_{name}", value.shape, mybir.dt.from_np(value.dtype), kind="ExternalInput").ap()
    out = nc.dram_tensor("out", (B, N, D), F32, kind="ExternalOutput").ap()
    build(nc, dram, out)
    r = _run(nc, [arrays], core_ids=[0])
    return r.results[0]["out"]
```

```python
import numpy as np
import concourse.bass as bass
from concourse import mybir
from contextlib import ExitStack

F32 = mybir.dt.float32
F32R = mybir.dt.float32r
BF16 = mybir.dt.bfloat16
I32 = mybir.dt.int32
U32 = mybir.dt.uint32
ALU = mybir.AluOpType
ACT = mybir.ActivationFunctionType
AX = mybir.AxisListType.X

B, IMG, TXT, D = 8, 49, 512, 192
N = IMG + TXT
P = 128
KC = 96
EPS = 1e-5
LAYERS, H1, DK = 4, 12, 16
FF = 768
H2, DH = 12, 64
EXPERTS = 8
VOCAB = 8000
BIG = 987654321.0
BASE = 16


def rsqrt_steps(nc, g, tick, rstd, mv, var_eps, half, pool, count):
    g.sem_inc(tick, 1)
    nc.gpsimd.tensor_scalar(var_eps, mv, EPS, None, ALU.add).then_inc(pool, 1)
    g.wait_ge(pool, count)
    nc.gpsimd.tensor_tensor(rstd, var_eps, half, ALU.pow).then_inc(pool, 1)


def embed_phase(nc, dram, tokens):
    TILES = B * TXT // P
    IT = B * IMG // 98
    KT = 768 // P
    with ExitStack() as ctx:
        sb = lambda n, s, d=F32: ctx.enter_context(nc.sbuf_tensor(n, s, d))
        sem = lambda n: ctx.enter_context(nc.semaphore(n))
        ids = sb("ids", [P, TILES], I32)
        idf = sb("idf", [P, TILES])
        neg = sb("neg", [P, TILES])
        idu = sb("idu", [P, TILES], U32)
        words = sb("words", [P, TILES, D])
        pos = sb("pos", [P, 4, D])
        patches = sb("patches", [P, KT, B * IMG])
        wproj = sb("wproj", [P, KT, D])
        rows = sb("tok_rows", [P, 3, D])
        y = sb("tok_y", [P, IT, D])
        z = sb("tok_z", [P, IT, D])
        zero = sb("zero_rows", [P, D])
        stats = sb("tok_stats", [P, IT, 6])
        mv = sb("tok_mv", [P, IT, 2])
        rstd = sb("tok_rstd", [P, IT])
        var_eps = sb("tok_var_eps", [P, IT])
        half = sb("tok_half", [P, IT])
        ps = [ctx.enter_context(nc.psum_tensor(f"tok_ps{i}", [P, 512], F32)) for i in range(IT)]
        ids_in, loaded, gathered, mm, dve, pool, stored = (
            sem(n) for n in ("ids_in", "tok_loaded", "gathered", "tok_mm", "tok_dve", "tok_pool", "tok_stored"))
        tick = sem("tok_tick")
        block = ctx.enter_context(nc.Block())

        @block.sync
        def _(sp):
            sp.dma_start(ids[:, :], dram["ids"]).then_inc(ids_in, 16)
            sp.dma_start(patches[:, :, :], dram["patches"]).then_inc(loaded, 16)
            sp.dma_start(wproj[:, :, :], dram["wproj"]).then_inc(loaded, 16)
            sp.dma_start(rows[:, :, :], dram["tok_rows"].partition_broadcast(P)).then_inc(loaded, 16)
            sp.dma_start(pos[:, :, :], dram["pos"]).then_inc(loaded, 16)
            sp.wait_ge(pool, 7)
            for b in range(B):
                sp.dma_start(tokens[b * N + IMG:(b + 1) * N, :].rearrange("(i p) d -> p i d", p=P),
                             words[:, 4 * b:4 * b + 4, :]).then_inc(stored, 16)
            sp.wait_ge(dve, 6 + 4 * IT)
            for b in range(B):
                p0 = IMG * (b % 2)
                sp.dma_start(tokens[b * N:b * N + IMG, :], z[p0:p0 + IMG, b // 2, :]).then_inc(stored, 16)
            sp.wait_ge(stored, 16 * 2 * B)

        @block.gpsimd
        def _(g):
            g.wait_ge(dve, 4)
            for i in range(TILES):
                g.indirect_dma_start(words[:, i, :], None, dram["emb"],
                                     bass.IndirectOffsetOnAxis(ap=idu[:, i:i + 1], axis=0)).then_inc(gathered, 16)
            g.wait_ge(dve, 4 + 3 * IT)
            nc.gpsimd.memset(half[:, :], -0.5).then_inc(pool, 1)
            g.wait_ge(pool, 1)
            rsqrt_steps(nc, g, tick, rstd[0:98, :], mv[0:98, :, 1], var_eps[0:98, :], half[0:98, :], pool, 2)
            g.wait_ge(gathered, 16 * TILES)
            g.wait_ge(loaded, 64)
            for i in range(4):
                v = words[:, :, :].rearrange("p (b i) d -> p i b d", i=4)[:, i, :, :]
                nc.gpsimd.tensor_tensor(v, v, pos[:, i:i + 1, :].to_broadcast([P, B, D]), ALU.add).then_inc(pool, 1)

        @block.tensor
        def _(pe):
            pe.wait_ge(loaded, 64)
            for i in range(IT):
                for k in range(KT):
                    last = nc.tensor.matmul(ps[i][0:98, 0:D], patches[:, k, 98 * i:98 * i + 98], wproj[:, k, :],
                                            start=(k == 0), stop=(k == KT - 1))
                last.then_inc(mm, 1)

        @block.vector
        def _(v):
            v.wait_ge(ids_in, 16)
            nc.vector.tensor_copy(idf[:, :], ids[:, :]).then_inc(dve, 1)
            v.wait_ge(dve, 1)
            nc.vector.tensor_scalar(neg[:, :], idf[:, :], 0.0, float(VOCAB), ALU.is_lt, ALU.mult).then_inc(dve, 1)
            v.wait_ge(dve, 2)
            nc.vector.tensor_tensor(idf[:, :], idf[:, :], neg[:, :], ALU.add).then_inc(dve, 1)
            v.wait_ge(dve, 3)
            nc.vector.tensor_scalar(idu[:, :], idf[:, :], 0.0, float(VOCAB - 1), ALU.max, ALU.min).then_inc(dve, 1)
            for i in range(IT):
                v.wait_ge(mm, i + 1)
                nc.vector.tensor_tensor(y[0:98, i, :], ps[i][0:98, 0:D], rows[0:98, 0, :], ALU.add).then_inc(dve, 1)
                v.wait_ge(dve, 5 + 3 * i)
                nc.vector.bn_stats(stats[0:98, i, :], y[0:98, i, :]).then_inc(dve, 1)
                v.wait_ge(dve, 6 + 3 * i)
                nc.vector.bn_aggr(mv[0:98, i, :], stats[0:98, i, :]).then_inc(dve, 1)
            v.wait_ge(pool, 3)
            for i in range(IT):
                nc.vector.tensor_scalar(z[0:98, i, :], y[0:98, i, :], mv[0:98, i, 0:1], rstd[0:98, i:i + 1],
                                        ALU.subtract, ALU.mult).then_inc(dve, 1)
            c = 4 + 4 * IT
            v.wait_ge(dve, c)
            nc.vector.tensor_tensor(y[0:98, :, :], z[0:98, :, :], rows[0:98, 1:2, :].to_broadcast([98, IT, D]), ALU.mult).then_inc(dve, 1)
            v.wait_ge(dve, c + 1)
            nc.vector.tensor_tensor(z[0:98, :, :], y[0:98, :, :], rows[0:98, 2:3, :].to_broadcast([98, IT, D]), ALU.add).then_inc(dve, 1)


RING = 3
JOBS = ("tx", "qk", "v", "max", "maxt", "exp", "wo", "ft", "f1", "f2")
ON_ACT = ("tx", "qk", "maxt", "exp", "ft", "f1")
ON_DVE = ("qk", "v", "max", "norm", "wo", "f2")


def spread(main, side):
    out, done = [], 0
    for i, step in enumerate(main):
        out.append(step)
        due = len(side) * (i + 1) // len(main)
        out, done = out + side[done:due], due
    return out


def normalise_later(steps):
    out, due = [], []
    for step in steps:
        out.append(step)
        if step[0] in ON_DVE:
            due = [(left - 1, late) for left, late in due]
            while due and due[0][0] == 0:
                out.append(due.pop(0)[1])
        if step[0] in ("wo", "f2"):
            due.append((1, ("ln", step[1], 1)) if step[0] == "wo" else (3, ("ln", step[1], 2)))
            due.sort()
    return out + [late for _, late in due]


def attend_steps(s):
    out, due, pieces = [], [], []
    for n in range(6):
        for hh in range(4):
            out.append(("exp", s, n, hh))
            out, pieces = out + pieces[:1], pieces[1:]
            due = [(left - 1, step) for left, step in due]
            if due and due[0][0] == 0:
                out.append(due.pop(0)[1])
                if n % 2 == 0:
                    pieces = [("norm", s, n // 2 - 1, p) for p in range(PIECES + 1)]
        due.append((2, ("pv", s, n)))
    return out + [step for _, step in due] + [("norm", s, 2, p) for p in range(PIECES + 1)]


def project_steps(s):
    return [("tx", s), ("qk", s, 0), ("qk", s, 1), ("qk", s, 2), ("v", s)]


def max_steps(s):
    return [("max", s, h, a) for h in range(H1) for a in range(2)]


PIECES = 4
M0, M1 = max_steps(0) + [("maxt", 0)], max_steps(1) + [("maxt", 1)]
EXP0, EXP1 = attend_steps(0), attend_steps(1)
SIDE = ([("wo", 0)] + project_steps(0) + [("ft", 0), ("f1", 0, 0), ("f1", 0, 1)] + M0[0:4] + [("f1", 0, 2)] + M0[4:8]
        + [("f2", 0)] + M0[8:12])
TAIL = ([("tx", 1), M0[12], ("qk", 1, 0), M0[13], ("qk", 1, 1), ("qk", 1, 2), ("wo", 1), ("v", 1)] + M0[14:20]
        + [("ft", 1)] + M0[20:22] + [("f1", 1, 0)] + M0[22:25] + [("f1", 1, 1), ("f1", 1, 2), ("f2", 1)])
BODY = normalise_later(spread(EXP0[:-8], M1) + EXP0[-8:] + spread(EXP1, SIDE) + TAIL)
AHEAD = project_steps(0) + project_steps(1) + M0


class Counts:

    def __init__(self, steps, jobs, on_act, on_dve, start=None, first_job=0):
        self.steps, self.on_dve, self.first_job = steps, on_dve, first_job
        number = lambda kinds: {s: n for n, s in enumerate(x for x in steps if x[0] in kinds)}
        self.jobs = number(jobs)
        self.tables = {"mm": number(jobs + ("pv",)), "act": number(on_act), "dve": number(on_dve)}
        self.start = start or {"mm": BASE, "act": BASE, "dve": BASE}

    def total(self, name):
        return len(self.tables[name])

    def end(self):
        return {name: self.start[name] + self.total(name) for name in self.tables}

    def value(self, turn, name, step, turns_back=0):
        fixed = self.start[name] + self.tables[name][step] + 1 - turns_back * self.total(name)
        return turn * self.total(name) + fixed if self.looped else fixed

    looped = False

    def buffer(self, step):
        return (self.jobs[step] + self.first_job) % RING

    def freed(self, turn, step):
        j, order = self.jobs[step], list(self.jobs)
        if j < RING and not self.looped:
            return None
        before = order[j - RING]
        name = "dve" if before[0] in self.on_dve else "act"
        return name, self.value(turn, name, before, turns_back=1 if j < RING else 0)


def encoder_phase(nc, dram, tokens):
    ahead_jobs = sum(x[0] in JOBS for x in AHEAD)
    PRO = Counts(AHEAD, JOBS, ON_ACT, ON_DVE, first_job=-ahead_jobs % RING)
    LOOP = Counts(BODY, JOBS, ON_ACT, ON_DVE, start=PRO.end())
    LOOP.looped = True
    assert len(LOOP.jobs) % RING == 0
    TURNS = LAYERS * B // 2
    with ExitStack() as ctx:
        sb = lambda n, s, d=F32: ctx.enter_context(nc.sbuf_tensor(n, s, d))
        sem = lambda n: ctx.enter_context(nc.semaphore(n))
        two = lambda n, s, d=F32: [sb(f"{n}{i}", s, d) for i in range(2)]
        ident = sb("ident", [P, P])
        wqk = sb("wqk", [KC, 2, 2 * D])
        wv = sb("wv", [KC, 2, D])
        bqk = sb("bqk", [P, 3])
        bv = sb("bv_rows", [P, 2 * D])
        wo = sb("wo", [P, 3, D])
        w1 = sb("w1", [KC, 2, FF])
        b1 = sb("b1", [P, 6])
        w2 = sb("w2", [P, 6, D])
        rows = sb("enc_rows", [P, 6, D])
        h_in = two("h_in", [P, 4, D])
        res = two("res", [P, 4, D])
        hT = sb("hT", [KC, 2, TXT])
        qk_hi = sb("qk_hi", [P, 3, TXT], F32R)
        qk_lo = sb("qk_lo", [P, 3, TXT], F32R)
        q_st = two("q_stack", [P, 2, H1 // 2, TXT], F32R)
        k_st = two("k_stack", [P, H1 // 2, TXT], F32R)
        vals = two("vals", [P, 4, H1, 32])
        mx = two("mx", [P, 4, H1])
        nmax = sb("nmax", [H1, TXT], F32R)
        probs = two("probs", [P, 4, 2, TXT])
        sums = sb("sums", [P, TXT])
        oT = sb("oT", [P, 3, TXT])
        h1 = sb("h1", [P, 4, D])
        h1T = sb("h1T", [KC, 2, TXT])
        relu = sb("relu", [P, 6, TXT])
        y = sb("y", [P, 4, D])
        yn = sb("yn", [P, 4, D])
        h_out = sb("h_out", [P, 4, D])
        stats = sb("stats", [P, 4, 6])
        mv = sb("mv", [P, 4, 2])
        rstd = sb("rstd", [P, 4])
        var_eps = sb("var_eps", [P, 4])
        half = sb("half", [P, 4])
        ring = [ctx.enter_context(nc.psum_tensor(f"ring{i}", [P, 2, 512], F32)) for i in range(RING)]
        acc = [ctx.enter_context(nc.psum_tensor(f"acc{i}", [P, 512], F32)) for i in range(2)]
        qk_dram = [nc.dram_tensor(f"qk_scratch{s}", [2, 2 * D, TXT], F32, kind="Internal").ap() for s in range(2)]

        fixed_in, mm, act, dve, ln, pool = (sem(n) for n in ("fixed_in", "mm", "act", "dve", "ln", "pool"))
        wx_in, wf_in = sem("wx_in"), sem("wf_in")
        h_loaded, spilled, stacked, max_in, stored = ([sem(f"{n}{s}") for s in range(2)] for n in
                                                      ("h_loaded", "spilled", "stacked", "max_in", "stored"))
        ones_set, tick = sem("ones_set"), sem("tick")
        h_dram = tokens[0:B * N, :].rearrange("(b n) d -> b n d", n=N)[:, IMG:N, :].rearrange(
            "b (i p) d -> b p i d", p=P)
        pool_at, count = {("res", 0): 1, ("res", 1): 2}, 2
        ln_at, links = {}, 0
        for step in BODY:
            if step[0] == "norm" and step[3]:
                links += 1
            elif step[0] in ("wo", "f2"):
                which = 1 if step[0] == "wo" else 2
                pool_at[("rstd", step[1], which)] = count + 2
                pool_at[("ln", step[1], which)] = count + 4
                count += 4
                if which == 1:
                    count += 1
                    pool_at[("res2", step[1])] = count
                links += 8
                ln_at[(step[1], which)] = (links,)
            elif step[0] == "ln":
                links += 4
                ln_at[step[1:]] += (links,)
        N_POOL, N_LN = count, links
        POOL_BASE = N_POOL

        def pool_value(it, *piece, turns_back=0):
            return it * N_POOL + (POOL_BASE + pool_at[piece] - turns_back * N_POOL)

        sems = {"mm": mm, "act": act, "dve": dve}
        block = ctx.enter_context(nc.Block())

        @block.tensor
        def _(pe):
            pe.wait_ge(fixed_in, 16)

            def steps(counts, it):
                k = it if counts is LOOP else 0
                loads = 1 if counts is LOOP else 0
                for step in counts.steps:
                    kind, s = step[0], step[1]
                    if kind in ("norm", "ln"):
                        continue
                    if kind != "pv":
                        buf = ring[counts.buffer(step)]
                        freed = counts.freed(it, step)
                        if freed:
                            pe.wait_ge(sems[freed[0]], freed[1])
                    if kind == "tx":
                        pe.wait_ge(h_loaded[s], k * 16 + 16 * (1 + loads))
                        for c in range(2):
                            for i in range(4):
                                last = nc.tensor.transpose(buf[0:KC, c, P * i:P * i + P], h_in[s][:, i, KC * c:KC * c + KC],
                                                           ident[:, :])
                    elif kind == "qk":
                        m = step[2]
                        if m == 0:
                            pe.wait_ge(act, counts.value(it, "act", ("tx", s)))
                            pe.wait_ge(wx_in, k * 64 + 64 * (1 + loads))
                        for c in range(2):
                            last = nc.tensor.matmul(buf[:, 0, :], wqk[:, c, P * m:P * m + P], hT[:, c, :],
                                                    start=(c == 0), stop=(c == 1))
                    elif kind == "v":
                        for i in range(4):
                            for c in range(2):
                                last = nc.tensor.matmul(buf[:, i // 2, D * (i % 2):D * (i % 2) + D],
                                                        hT[:, c, P * i:P * i + P], wv[:, c, :],
                                                        start=(c == 0), stop=(c == 1))
                    elif kind == "max":
                        h, a = step[2:]
                        r, t = h % 2, h // 2
                        if h == 0 and a == 0:
                            ahead = loads if s == 0 else 0
                            pe.wait_ge(stacked[s], k * 224 + 224 * (1 + ahead))
                            pe.wait_ge(ones_set, 1)
                        for i in (2 * a, 2 * a + 1):
                            last = nc.tensor.matmul(buf[:, i % 2, :], q_st[s][:, r, t, P * i:P * i + P],
                                                    k_st[s][:, t, :], start=True, stop=True)
                    elif kind == "maxt":
                        pe.wait_ge(dve, counts.value(it, "dve", ("max", s, H1 - 1, 1)))
                        for i in range(4):
                            last = nc.tensor.transpose(buf[0:H1, 0, P * i:P * i + P], mx[s][:, i, :], ident[:, :])
                    elif kind == "exp":
                        n, hh = step[2:]
                        h = 4 * (n // 2) + hh
                        r, t = h % 2, h // 2
                        if n == 0 and hh == 0:
                            pe.wait_ge(max_in[s], k * 32 + 32)
                        for j in range(2):
                            kt = 2 * (n % 2) + j
                            last = nc.tensor.matmul(buf[:, j, :], k_st[s][:, t, P * kt:P * kt + P],
                                                    q_st[s][:, r, t, :], start=True, stop=True)
                    elif kind == "pv":
                        n = step[2]
                        g = 3 * s + n // 2
                        pe.wait_ge(act, counts.value(it, "act", ("exp", s, n, 3)))
                        if n % 2 == 0:
                            back = (g - 2) % 6
                            pe.wait_ge(dve, counts.value(it, "dve", ("norm", back // 3, back % 3, PIECES),
                                                               turns_back=int(g < 2)))
                        for j in range(2):
                            kt = 2 * (n % 2) + j
                            for hh in range(4):
                                last = nc.tensor.matmul(acc[g % 2][32 * hh:32 * hh + 32, :],
                                                        vals[s][:, kt, 4 * (n // 2) + hh, :], probs[n % 2][:, hh, j, :],
                                                        start=(n % 2 == 0 and j == 0), stop=(n % 2 == 1 and j == 1),
                                                        tile_position=(0, 32 * hh), skip_group_check=True)
                    elif kind == "wo":
                        pe.wait_ge(wf_in, k * 80 + 80)
                        for i in range(4):
                            pe.wait_ge(dve, counts.value(it, "dve", ("norm", s, 2, 1 + i)))
                            for g in range(3):
                                last = nc.tensor.matmul(buf[:, i // 2, D * (i % 2):D * (i % 2) + D],
                                                        oT[:, g, P * i:P * i + P], wo[:, g, :],
                                                        start=(g == 0), stop=(g == 2))
                    elif kind == "ft":
                        pe.wait_ge(pool, pool_value(it, "ln", s, 1))
                        for c in range(2):
                            for i in range(4):
                                last = nc.tensor.transpose(buf[0:KC, c, P * i:P * i + P], h1[:, i, KC * c:KC * c + KC],
                                                           ident[:, :])
                    elif kind == "f1":
                        m = step[2]
                        if m == 0:
                            pe.wait_ge(act, counts.value(it, "act", ("ft", s)))
                        for j in range(2):
                            for c in range(2):
                                f = P * (2 * m + j)
                                last = nc.tensor.matmul(buf[:, j, :], w1[:, c, f:f + P], h1T[:, c, :],
                                                        start=(c == 0), stop=(c == 1))
                    elif kind == "f2":
                        pe.wait_ge(act, counts.value(it, "act", ("f1", s, 2)))
                        for i in range(4):
                            for k2 in range(6):
                                last = nc.tensor.matmul(buf[:, i // 2, D * (i % 2):D * (i % 2) + D],
                                                        relu[:, k2, P * i:P * i + P], w2[:, k2, :],
                                                        start=(k2 == 0), stop=(k2 == 5))
                    last.then_inc(mm, 1)

            steps(PRO, 0)
            with pe.Fori(0, TURNS) as it:
                steps(LOOP, it)

        @block.scalar
        def _(sc):
            def steps(counts, it):
                for step in counts.steps:
                    kind, s = step[0], step[1]
                    if kind not in ON_ACT:
                        continue
                    buf = ring[counts.buffer(step)]
                    sc.wait_ge(mm, counts.value(it, "mm", step))
                    if kind == "tx":
                        nc.scalar.activation(hT[:, :, :], buf[0:KC, :, :], ACT.Copy).then_inc(act, 1)
                    elif kind == "qk":
                        m = step[2]
                        if m == 0:
                            if counts is LOOP:
                                sc.wait_ge(spilled[1 - s], it * 32 + (32 if s == 0 else 64))
                            elif s == 1:
                                sc.wait_ge(spilled[0], 32)
                        nc.scalar.activation(qk_hi[:, m, :], buf[:, 0, :], ACT.Identity, bias=bqk[:, m:m + 1]).then_inc(act, 1)
                    elif kind == "maxt":
                        nc.scalar.activation(nmax[:, :], buf[0:H1, 0, :], ACT.Copy, scale=-1.0).then_inc(act, 1)
                    elif kind == "exp":
                        n, hh = step[2:]
                        if hh == 0:
                            back = 6 * s + n - 2
                            if back >= 0:
                                sc.wait_ge(mm, counts.value(it, "mm", ("pv", back // 6, back % 6)))
                        nc.scalar.activation(probs[n % 2][:, hh, :, :], buf[:, :, :], ACT.Exp,
                                             scale=DK ** -0.5).then_inc(act, 1)
                    elif kind == "ft":
                        nc.scalar.activation(h1T[:, :, :], buf[0:KC, :, :], ACT.Copy).then_inc(act, 1)
                    elif kind == "f1":
                        m = step[2]
                        nc.scalar.activation(relu[:, 2 * m, :], buf[:, 0, :], ACT.Relu, bias=b1[:, 2 * m:2 * m + 1])
                        nc.scalar.activation(relu[:, 2 * m + 1, :], buf[:, 1, :], ACT.Relu,
                                             bias=b1[:, 2 * m + 1:2 * m + 2]).then_inc(act, 1)

            sc.sem_inc(act, BASE)
            sc.wait_ge(wx_in, 64)
            steps(PRO, 0)
            with sc.Fori(0, TURNS) as it:
                steps(LOOP, it)

        @block.vector
        def _(v):
            def steps(counts, it):
                link_at = [0]

                def link(ins):
                    link_at[0] += 1
                    ins.then_inc(ln, 1)
                    v.wait_ge(ln, it * N_LN + (BASE + link_at[0]))

                def moments():
                    for i in range(4):
                        last = nc.vector.bn_stats(stats[:, i, :], y[:, i, :])
                        if i < 3:
                            last.then_inc(ln, 1)
                            link_at[0] += 1
                    link(last)
                    v.sem_inc(tick, 1)
                    for i in range(4):
                        last = nc.vector.bn_aggr(mv[:, i, :], stats[:, i, :])
                        last.then_inc(ln, 1)
                        link_at[0] += 1

                def normalise(s, which):
                    v.wait_ge(pool, pool_value(it, "rstd", s, which))
                    for i in range(4):
                        nc.vector.tensor_scalar(yn[:, i, :], y[:, i, :], mv[:, i, 0:1], rstd[:, i:i + 1],
                                                ALU.subtract, ALU.mult).then_inc(ln, 1)
                        link_at[0] += 1

                for step in counts.steps:
                    kind, s = step[0], step[1]
                    if kind == "ln":
                        normalise(s, step[2])
                    if kind not in ON_DVE:
                        continue
                    if kind == "norm":
                        g, p = step[2:]
                        a, back = acc[(3 * s + g) % 2], (3 * s + g - 1) % 6
                        if p == 0:
                            v.wait_ge(mm, counts.value(it, "mm", ("pv", s, 2 * g + 1)))
                            v.wait_ge(dve, counts.value(it, "dve", ("norm", back // 3, back % 3, PIECES),
                                                        turns_back=int(3 * s + g < 1)))
                            v.sem_inc(tick, 1)
                            nc.vector.stream_shuffle(sums[:, :], a[:, :], [16 + i % 16 for i in range(32)]).then_inc(dve, 1)
                        else:
                            if p == 1:
                                v.wait_ge(dve, counts.value(it, "dve", ("norm", s, g, 0)))
                            t = slice(P * (p - 1), P * p)
                            link(nc.vector.reciprocal(sums[:, t], sums[:, t]))
                            nc.vector.tensor_tensor(oT[:, g, t], a[:, t], sums[:, t], ALU.mult).then_inc(dve, 1)
                        continue
                    buf = ring[counts.buffer(step)]
                    if kind == "qk":
                        m = step[2]
                        v.wait_ge(act, counts.value(it, "act", step))
                        nc.vector.scalar_tensor_tensor(qk_lo[:, m, :], buf[:, 0, :], bqk[:, m:m + 1],
                                                       qk_hi[:, m, :].bitcast(F32), ALU.add, ALU.subtract).then_inc(dve, 1)
                        continue
                    v.wait_ge(mm, counts.value(it, "mm", step))
                    if kind == "v":
                        nc.vector.tensor_tensor(
                            vals[s][:, :, :, 0:DK].rearrange("p (a b) h d -> p a (b h) d", a=2),
                            buf[:, :, 0:2 * D].rearrange("p a (h d) -> p a h d", d=DK),
                            bv[:, :].rearrange("p (a h d) -> p a h d", a=1, d=DK).to_broadcast([P, 2, 2 * H1, DK]),
                            ALU.add).then_inc(dve, 1)
                    elif kind == "max":
                        h, a = step[2:]
                        row = (h % 2) * 6 + h // 2
                        nc.vector.tensor_reduce(mx[s][:, 2 * a:2 * a + 2, row], buf[:, :, :], AX, ALU.max).then_inc(dve, 1)
                    elif kind in ("wo", "f2"):
                        if kind == "wo":
                            v.wait_ge(pool, pool_value(it, "res", s))
                        if kind == "f2":
                            v.wait_ge(pool, pool_value(it, "res2", s))
                        r = res[s]
                        v.wait_ge(ln, it * N_LN + (BASE + link_at[0]))
                        link_y = nc.vector.tensor_tensor(y[:, :, :].rearrange("p (a b) d -> p a (b d)", a=2), buf[:, :, 0:2 * D],
                                                         r[:, :, :].rearrange("p (a b) d -> p a (b d)", a=2), ALU.add)
                        link_y.then_inc(dve, 1)
                        v.wait_ge(dve, counts.value(it, "dve", step))
                        moments()
                return link_at[0]

            for s in range(2):
                nc.vector.memset(k_st[s][:, :, :].bitcast(F32), 1.0)
                nc.vector.memset(q_st[s][:, :, :, :].bitcast(F32), 0.0)
                last = nc.vector.memset(vals[s][:, :, :, :], 1.0)
            last.then_inc(ones_set, 1)
            v.sem_inc(mm, BASE)
            v.sem_inc(dve, BASE)
            v.sem_inc(ln, BASE)
            v.wait_ge(wx_in, 64)
            v.wait_ge(ones_set, 1)
            steps(PRO, 0)
            with v.Fori(0, TURNS) as it:
                links = steps(LOOP, it)
            assert links == N_LN, links

        @block.gpsimd
        def _(g):
            def lane(name):
                return {"bo": 0, "g1": 1, "bn1": 2, "bw2": 3, "g2": 4, "bn2": 5}[name]

            wide = lambda name: rows[:, lane(name):lane(name) + 1, :].to_broadcast([P, 4, D])
            nc.gpsimd.memset(half[:, :], -0.5)
            g.sem_inc(pool, POOL_BASE)
            with g.Fori(0, TURNS) as it:
                g.wait_ge(wf_in, it * 80 + 80)
                g.wait_ge(dve, it * LOOP.total("dve") + LOOP.start["dve"])
                for s in range(2):
                    g.wait_ge(h_loaded[s], it * 16 + 16)
                    nc.gpsimd.tensor_tensor(res[s][:, :, :], h_in[s][:, :, :], wide("bo"), ALU.add).then_inc(pool, 1)
                for step in LOOP.steps:
                    kind, s = step[0], step[1]
                    if kind in ("wo", "f2"):
                        which = 1 if kind == "wo" else 2
                        moments, normed = ln_at[(s, which)]
                        g.wait_ge(ln, it * N_LN + (BASE + moments))
                        rsqrt_steps(nc, g, tick, rstd[:, :], mv[:, :, 1], var_eps[:, :], half[:, :], pool,
                                    pool_value(it, "rstd", s, which) - 1)
                        g.wait_ge(ln, it * N_LN + (BASE + normed))
                        out = h1 if which == 1 else h_out
                        if which == 2:
                            g.wait_ge(stored[1 - s], it * 16 + 16 * (1 + s))
                        nc.gpsimd.tensor_tensor(out[:, :, :], yn[:, :, :], wide("g1" if which == 1 else "g2"),
                                                ALU.mult).then_inc(pool, 1)
                        g.wait_ge(pool, pool_value(it, "ln", s, which) - 1)
                        nc.gpsimd.tensor_tensor(out[:, :, :], out[:, :, :], wide("bn1" if which == 1 else "bn2"),
                                                ALU.add).then_inc(pool, 1)
                        g.wait_ge(pool, pool_value(it, "ln", s, which))
                        if which == 1:
                            nc.gpsimd.tensor_tensor(res[s][:, :, :], out[:, :, :], wide("bw2"), ALU.add).then_inc(pool, 1)

        @block.sync
        def _(sp):
            def load_project_weights(layer):
                sp.dma_start(wqk[:, :, :], dram["wqk"][layer]).then_inc(wx_in, 16)
                sp.dma_start(wv[:, :, :], dram["wv"][layer]).then_inc(wx_in, 16)
                sp.dma_start(bqk[:, :], dram["bqk"][layer]).then_inc(wx_in, 16)
                sp.dma_start(bv[:, :], dram["bv2"][layer].partition_broadcast(P)).then_inc(wx_in, 16)

            def spill_and_stack(counts, it, s, before_count):
                sp.wait_ge(act, counts.value(it, "act", ("qk", s, 2)))
                sp.sem_inc(tick, 1)
                sp.wait_ge(dve, counts.value(it, "dve", ("qk", s, 2)))
                for part, t in ((0, qk_hi), (1, qk_lo)):
                    sp.dma_start(qk_dram[s][part].rearrange("(m p) n -> p m n", p=P),
                                 t[:, :, :].bitcast(F32)).then_inc(spilled[s], 16)
                sp.wait_ge(spilled[s], before_count)
                for r in range(2):
                    for st, first, parts in ((q_st, 0, (0, 1, 0)), (k_st, D, (0, 0, 1))):
                        for c, part in enumerate(parts):
                            src = qk_dram[s][part][first:first + D, :].rearrange("(t r d) n -> r d t n", r=2, d=DK)
                            p0 = 64 * r + DK * c
                            dst = st[s][p0:p0 + DK, r, :, :] if st is q_st else st[s][p0:p0 + DK, :, :]
                            sp.dma_start(dst.bitcast(F32), src[r]).then_inc(stacked[s], 16)
                    p0, other = 64 * r + 3 * DK, 64 * (1 - r) + 3 * DK
                    sp.dma_start(q_st[s][p0:p0 + 1, r, :, :].bitcast(F32),
                                 q_st[s][other:other + 1, r, :, :].bitcast(F32)).then_inc(stacked[s], 16)

            def max_row(counts, it, s):
                sp.wait_ge(act, counts.value(it, "act", ("maxt", s)))
                for r in range(2):
                    p0 = 64 * r + 3 * DK
                    sp.dma_start(q_st[s][p0:p0 + 1, r, :, :].bitcast(F32),
                                 nmax[6 * r:6 * r + 6, :].bitcast(F32)).then_inc(max_in[s], 16)

            def store(it, s):
                sp.wait_ge(pool, pool_value(it, "ln", s, 2))
                sp.sem_inc(tick, 1)
                sp.dma_start(h_dram[(it % 4) * 2 + s], h_out[:, :, :]).then_inc(stored[s], 16)

            for s in range(2):
                sp.sem_inc(stored[s], 16)
            sp.dma_start(ident[:, :], dram["ident"]).then_inc(fixed_in, 16)
            load_project_weights(0)
            for s in range(2):
                sp.dma_start(h_in[s][:, :, :], h_dram[s]).then_inc(h_loaded[s], 16)
            sp.wait_ge(ones_set, 1)
            for s in range(2):
                spill_and_stack(PRO, 0, s, 32)
            max_row(PRO, 0, 0)
            with sp.Fori(0, TURNS) as it:
                nxt = (it + 1) % TURNS
                sp.wait_ge(dve, it * LOOP.total("dve") + LOOP.start["dve"])
                sp.sem_inc(tick, 1)
                load_project_weights(nxt // 4)
                sp.wait_ge(pool, it * N_POOL + POOL_BASE)
                sp.sem_inc(tick, 1)
                layer = it // 4
                sp.dma_start(wo[:, :, :], dram["wo"][layer]).then_inc(wf_in, 16)
                sp.dma_start(w1[:, :, :], dram["w1"][layer]).then_inc(wf_in, 16)
                sp.dma_start(b1[:, :], dram["b1"][layer]).then_inc(wf_in, 16)
                sp.dma_start(w2[:, :, :], dram["w2"][layer]).then_inc(wf_in, 16)
                sp.dma_start(rows[:, :, :], dram["enc_rows"][layer].partition_broadcast(P)).then_inc(wf_in, 16)
                for s in range(2):
                    sp.wait_ge(pool, pool_value(it, "res", s))
                    sp.wait_ge(stored[s], it * 16 + 16)
                    sp.sem_inc(tick, 1)
                    sp.dma_start(h_in[s][:, :, :], h_dram[(nxt % 4) * 2 + s]).then_inc(h_loaded[s], 16)
                max_row(LOOP, it, 1)
                spill_and_stack(LOOP, it, 0, it * 32 + 64)
                store(it, 0)
                spill_and_stack(LOOP, it, 1, it * 32 + 64)
                max_row(LOOP, it, 0)
                store(it, 1)
            for s in range(2):
                sp.wait_ge(stored[s], 16 * TURNS + 16)
                sp.wait_ge(stacked[s], 224 * (TURNS + 1))
                sp.wait_ge(max_in[s], 32 * (TURNS + 1 - s))


TILES = [(i, min(P, N - P * i)) for i in range((N + P - 1) // P)]
NE = N + N % 2
COLS = ((0, 2 * P), (2 * P, N - 2 * P))
COLS_E = ((0, 2 * P), (2 * P, NE - 2 * P))


GH = 4
GROUPS = H2 // GH
LAST = 6


def scores_steps(g):
    heads = range(GH * g, GH * g + GH)
    out = [("qk", x, h) for h in heads if h % 2 == 0 for x in ("q", "k")]
    if g == 0:
        out += [("v", i) for i, _ in TILES]
    return out + [("max", h, i) for h in heads for i, _ in TILES] + [("maxt", g)]


def weigh_steps(g):
    out = []
    for h in range(GH * g, GH * g + GH):
        after = {0: [("norm", h - 2, 3)], 1: [("norm", h - 2, 4), ("pv", h - 1), ("take", h - 1)],
                 2: [("norm", h - 1, 0)], 3: [("norm", h - 1, 1)], 4: [("norm", h - 1, 2)]}
        for kt, _ in TILES:
            out += [("exp", h, kt)] + [x for x in after[kt] if x[1] >= 0]
            if (h, kt) in ((GH * (GROUPS - 1) + 1, 0), (GH * GROUPS - 1, 0)):
                out.append(("ln", 0 if kt or h < GH * GROUPS - 1 else 1))
    return out


def fused_steps():
    out = [("t", 0), ("t", 1)] + scores_steps(0)
    for g in range(GROUPS):
        main, side = weigh_steps(g), scores_steps(g + 1) if g + 1 < GROUPS else []
        out += spread(main[:-LAST], side) + main[-LAST:]
    out += [("norm", H2 - 2, 3), ("norm", H2 - 2, 4), ("pv", H2 - 1), ("take", H2 - 1)]
    return out + [("norm", H2 - 1, i) for i, _ in TILES] + [("wo", i) for i, _ in TILES]


def slot(h):
    return h % (2 * GH)


def flat(buf):
    return buf[:, :, :].rearrange("p a b -> p (a b)")[:, 512 - 2 * P:1024]


def rows_of(t, b):
    v = t[0:t.shape[0] // N * N, :].rearrange("(b n) d -> b n d", n=N)
    return (v[:, 0:4 * P, :].rearrange("b (i p) d -> b p i d", p=P)[b], v[:, 4 * P:N, :][b])


def attention_phase(nc, dram, tokens, fused):
    steps_list = fused_steps()
    on_act, on_dve = ("t", "qk", "maxt", "exp", "take"), ("qk", "v", "max", "norm", "wo")
    C = Counts(steps_list, ("t", "qk", "v", "max", "maxt", "exp", "wo"), on_act, on_dve)
    C.looped = True
    assert len(C.jobs) % RING == 0, len(C.jobs)
    with ExitStack() as ctx:
        sb = lambda n, s, d=F32: ctx.enter_context(nc.sbuf_tensor(n, s, d))
        sem = lambda n: ctx.enter_context(nc.semaphore(n))
        ident = sb("a_ident", [P, P])
        eye16 = sb("eye16", [P, P], BF16)
        mask16 = sb("mask16", [P, P], BF16)
        wqk = sb("a_wqk", [KC, 2, 2 * H2 * DH])
        wv = sb("a_wv", [KC, 2, H2 * DH])
        wo = sb("a_wo", [P, 6, D])
        scale = sb("a_scale", [P, H2])
        b_out = sb("a_bout", [P, 1, D])
        h_in = sb("a_h", [P, 5, D])
        res = sb("a_res", [P, 5, D])
        xn = sb("a_xn", [P, 5, D])
        xT = sb("a_xT", [KC, 2, N])
        q_hl = sb("a_q_hl", [P, 2 * GH, NE], F32R)
        k_hh = sb("a_k_hh", [P, 2 * GH, NE], F32R)
        q_hm = sb("a_q_hm", [P, 2 * GH, NE], F32R)
        k_l1 = sb("a_k_l1", [P, 2 * GH, NE], F32R)
        vals = sb("a_vals", [P, 5, H2, 2 * DH])
        mx = sb("a_mx", [P, 5, H2])
        nmax = sb("a_nmax", [GH, N], F32R)
        zeros = sb("a_zeros", [2 * GH, NE])
        probs = [sb(f"a_probs{i}", [P, 5, N]) for i in range(2)]
        taken = [sb(f"a_taken{i}", [P, N]) for i in range(2)]
        oT = sb("a_oT", [P, 6, N])
        stats = sb("a_stats", [P, 5, 6])
        mv = sb("a_mv", [P, 5, 2])
        rstd = sb("a_rstd", [P, 5])
        var_eps = sb("a_var_eps", [P, 5])
        half = sb("a_half", [P, 5])
        ring = [ctx.enter_context(nc.psum_tensor(f"a_ring{i}", [P, 2, 512], F32)) for i in range(RING)]
        acc = ctx.enter_context(nc.psum_tensor("a_acc", [P, 2, 512], F32))
        fixed_in, ready, loaded, mm, act, dve, ln, pool, max_in, stored = (sem("a_" + n) for n in (
            "fixed_in", "ready", "loaded", "mm", "act", "dve", "ln", "pool", "max_in", "stored"))
        zeroed, copied, recip, pool_res = sem("a_zeroed"), sem("a_copied"), sem("a_recip"), sem("a_pool_res")
        tick = sem("a_tick")
        sems = {"mm": mm, "act": act, "dve": dve}
        block = ctx.enter_context(nc.Block())

        @block.sync
        def _(sp):
            def load(b):
                full, rest = rows_of(tokens, b)
                sp.dma_start(h_in[:, 0:4, :], full).then_inc(loaded, 16)
                sp.dma_start(h_in[0:N - 4 * P, 4, :], rest).then_inc(loaded, 16)

            for dst, src in ((ident[:, :], dram["ident"]), (wqk[:, :, :], dram["a_wqk"]), (wv[:, :, :], dram["a_wv"]),
                             (wo[:, :, :], dram["a_wo"]), (scale[:, :], dram["a_scale"].partition_broadcast(P)),
                             (b_out[:, :, :], dram["a_bout"].partition_broadcast(P))):
                sp.dma_start(dst, src).then_inc(fixed_in, 16)
            load(0)
            sp.dma_start(tokens[B * N:(B + 1) * N, :], tokens[0:N, :]).then_inc(copied, 16)
            sp.wait_ge(copied, 16)
            sp.wait_ge(ready, 3)
            with sp.Fori(0, B) as it:
                for g in range(GROUPS):
                    if g == 0:
                        sp.wait_ge(mm, C.value(it, "mm", ("exp", H2 - 1, 4), turns_back=1))
                        sp.dma_start(q_hm[DH:DH + 1, :, :].bitcast(F32), zeros[:, :]).then_inc(zeroed, 16)
                    elif g == 1:
                        sp.wait_ge(ln, it * 15 + (BASE + 15))
                        sp.wait_ge(pool_res, it * 2 + (BASE + 2))
                        load(it + 1)
                    elif g == 2:
                        sp.wait_ge(mm, C.value(it, "mm", ("exp", GH - 1, 4)))
                        sp.dma_start(q_hm[DH:DH + 1, 0:GH, :].bitcast(F32), zeros[0:GH, :]).then_inc(zeroed, 16)
                    sp.wait_ge(act, C.value(it, "act", ("maxt", g)))
                    sp.dma_start(q_hm[DH:DH + 1, slot(GH * g):slot(GH * g) + GH, 0:N].bitcast(F32),
                                 nmax[:, :].bitcast(F32)).then_inc(max_in, 16)
                sp.wait_ge(dve, C.value(it, "dve", ("wo", 4)))
                full, rest = rows_of(fused, it)
                sp.dma_start(full, res[:, 0:4, :]).then_inc(stored, 16)
                sp.dma_start(rest, res[0:N - 4 * P, 4, :]).then_inc(stored, 16)
            sp.wait_ge(stored, 32 * B + BASE)
            sp.wait_ge(max_in, 16 * GROUPS * B)
            sp.wait_ge(zeroed, 32 * B)

        @block.gpsimd
        def _(g):
            nc.gpsimd.memset(half[:, :], -0.5)
            g.sem_inc(pool, BASE)
            g.sem_inc(pool_res, BASE)
            g.wait_ge(fixed_in, 96)

            def moments_to_rstd(b):
                g.wait_ge(ln, b * 15 + (BASE + 10))
                rsqrt_steps(nc, g, tick, rstd[:, :], mv[:, :, 1], var_eps[:, :], half[:, :], pool, b * 2 + (BASE + 1))

            moments_to_rstd(0)
            with g.Fori(0, B) as it:
                g.wait_ge(loaded, it * 32 + 32)
                g.wait_ge(stored, it * 32 + BASE)
                for t, r in ((slice(0, 4), P), (slice(4, 5), N - 4 * P)):
                    nt = t.stop - t.start
                    nc.gpsimd.tensor_tensor(res[0:r, t, :], h_in[0:r, t, :], b_out[0:r, :, :].to_broadcast([r, nt, D]),
                                            ALU.add).then_inc(pool_res, 1)
                moments_to_rstd(it + 1)

        @block.tensor
        def _(pe):
            pe.wait_ge(fixed_in, 96)
            pe.wait_ge(ready, 5)
            with pe.Fori(0, B) as it:
                for step in C.steps:
                    kind = step[0]
                    if kind in ("take", "norm", "ln"):
                        continue
                    if kind != "pv":
                        buf = ring[C.buffer(step)]
                        name, value = C.freed(it, step)
                        pe.wait_ge(sems[name], value)
                    if kind == "t":
                        c = step[1]
                        pe.wait_ge(ln, it * 15 + (BASE + 15))
                        for i, r in TILES:
                            last = nc.tensor.transpose(flat(buf)[0:KC, P * i:P * i + r], xn[0:r, i, KC * c:KC * c + KC],
                                                       ident[0:r, 0:r])
                    elif kind == "qk":
                        j = step[2] // 2 + (6 if step[1] == "k" else 0)
                        if step[1:] == ("q", 0):
                            pe.wait_ge(act, C.value(it, "act", ("t", 1)))
                        for n0, n in COLS:
                            for c in range(2):
                                last = nc.tensor.matmul(flat(buf)[:, n0:n0 + n], wqk[:, c, P * j:P * j + P],
                                                        xT[:, c, n0:n0 + n], start=(c == 0), stop=(c == 1))
                    elif kind == "v":
                        i = step[1]
                        r = TILES[i][1]
                        for half in range(2):
                            w = H2 * DH // 2
                            for c in range(2):
                                last = nc.tensor.matmul(buf[0:r, half, 0:w], xT[:, c, P * i:P * i + r],
                                                        wv[:, c, half * w:half * w + w], start=(c == 0), stop=(c == 1))
                    elif kind in ("max", "exp"):
                        h, i = step[1:]
                        r = TILES[i][1]
                        s = slot(h)
                        if kind == "max" and i == 0:
                            pe.wait_ge(dve, C.value(it, "dve", ("qk", "k", h - h % 2)))
                            pe.wait_ge(zeroed, it * 32 + (16 if h < 2 * GH else 32))
                        if kind == "exp" and h % GH == 0 and i == 0:
                            pe.wait_ge(max_in, it * (16 * GROUPS) + 16 * (h // GH + 1))
                        rows = slice(P * i, P * i + r)
                        if kind == "max":
                            pairs = ((q_hl[:, s, rows], k_hh[:, s, :]), (q_hm[:, s, rows], k_l1[:, s, :]))
                        else:
                            pairs = ((k_hh[:, s, rows], q_hl[:, s, :]), (k_l1[:, s, rows], q_hm[:, s, :]))
                        if i == 4:
                            pe.sem_inc(tick, 1)
                        bank = 0 if i < 2 else 1
                        for n, (n0, w) in enumerate(COLS_E):
                            for m, (a, b) in enumerate(pairs):
                                last = nc.tensor.matmul(flat(buf)[0:r, n0:n0 + w], a, b[:, n0:n0 + w],
                                                        start=(m == 0), stop=(m == 1 and n != bank))
                            if n == bank:
                                last = nc.tensor.matmul(flat(buf)[0:r, P * i:P * i + r], eye16[0:r, 0:r],
                                                        mask16[0:r, 0:r], start=False, stop=True)
                    elif kind == "maxt":
                        h = GH * step[1]
                        pe.wait_ge(dve, C.value(it, "dve", ("max", h + GH - 1, 4)))
                        for i, r in TILES:
                            last = nc.tensor.transpose(flat(buf)[0:GH, P * i:P * i + r], mx[0:r, i, h:h + GH], ident[0:r, 0:r])
                    elif kind == "pv":
                        h = step[1]
                        pe.wait_ge(act, C.value(it, "act", ("exp", h, 4)))
                        pe.wait_ge(act, C.value(it, "act", ("take", (h - 1) % H2), turns_back=int(h == 0)))
                        for n0, w in COLS:
                            for i, r in TILES:
                                last = nc.tensor.matmul(flat(acc)[:, n0:n0 + w], vals[0:r, i, h, :],
                                                        probs[h % 2][0:r, i, n0:n0 + w], start=(i == 0), stop=(i == 4))
                    elif kind == "wo":
                        pe.wait_ge(dve, C.value(it, "dve", ("norm", H2 - 1, step[1])))
                        i, r = TILES[step[1]]
                        for k in range(6):
                            last = nc.tensor.matmul(buf[0:r, 0, 0:D], oT[:, k, P * i:P * i + r], wo[:, k, :],
                                                    start=(k == 0), stop=(k == 5))
                    last.then_inc(mm, 1)

        @block.scalar
        def _(sc):
            sc.sem_inc(act, BASE)
            sc.wait_ge(fixed_in, 96)
            with sc.Fori(0, B) as it:
                for step in C.steps:
                    kind = step[0]
                    if kind not in on_act:
                        continue
                    if kind == "take":
                        h = step[1]
                        sc.wait_ge(mm, C.value(it, "mm", ("pv", h)))
                        sc.wait_ge(dve, C.value(it, "dve", ("norm", (h - 2) % H2, 4), turns_back=int(h < 2)))
                        nc.scalar.activation(taken[h % 2][:, :], flat(acc)[:, 0:N], ACT.Copy).then_inc(act, 1)
                        continue
                    buf = ring[C.buffer(step)]
                    sc.wait_ge(mm, C.value(it, "mm", step))
                    if kind == "t":
                        nc.scalar.activation(xT[:, step[1], :], flat(buf)[0:KC, 0:N], ACT.Copy).then_inc(act, 1)
                    elif kind == "qk":
                        for r in range(2):
                            src = flat(buf)[DH * r:DH * r + DH, 0:N]
                            h = step[2] + r
                            if step[1] == "q":
                                for dst in (q_hm[0:DH], q_hl[0:DH]):
                                    ins = nc.scalar.activation(dst[:, slot(h), 0:N], src, ACT.Copy,
                                                               scale=scale[DH * r:DH * r + DH, h:h + 1])
                            else:
                                for dst in (k_hh[DH:P], k_hh[0:DH]):
                                    ins = nc.scalar.activation(dst[:, slot(h), 0:N], src, ACT.Copy)
                        ins.then_inc(act, 1)
                    elif kind == "maxt":
                        nc.scalar.activation(nmax[:, :], flat(buf)[0:GH, 0:N], ACT.Copy, scale=-1.0).then_inc(act, 1)
                    elif kind == "exp":
                        h, i = step[1:]
                        r = TILES[i][1]
                        if i == 0 and h >= 2:
                            sc.wait_ge(mm, C.value(it, "mm", ("pv", h - 2)))
                        nc.scalar.activation(probs[h % 2][0:r, i, :], flat(buf)[0:r, 0:N], ACT.Exp).then_inc(act, 1)

        @block.vector
        def _(v):
            nc.vector.memset(zeros[:, :], 0.0)
            for t in (q_hm, k_l1):
                nc.vector.memset(t[:, :, :].bitcast(F32), 0.0).then_inc(ready, 1)
            for t in (q_hl, k_hh):
                nc.vector.memset(t[:, :, N:NE].bitcast(F32), 0.0)
            v.wait_ge(ready, 2)
            nc.vector.memset(k_l1[DH:DH + 1, :, :].bitcast(F32), 1.0)
            nc.vector.memset(vals[:, :, :, :], 1.0).then_inc(ready, 1)
            nc.vector.memset(mv[:, :, :], 1.0)
            for s in (mm, dve, ln, recip, stored):
                v.sem_inc(s, BASE)
            v.wait_ge(fixed_in, 96)
            v.wait_ge(ready, 3)
            nc.vector.tensor_copy(eye16[:, :], ident[:, :]).then_inc(ready, 1)
            nc.vector.tensor_scalar(mask16[:, :], ident[:, :], -BIG, None, ALU.mult).then_inc(ready, 1)
            v.wait_ge(ready, 5)

            def moments(b):
                v.wait_ge(loaded, b * 32 + 32)
                for i, r in TILES:
                    nc.vector.bn_stats(stats[0:r, i, :], h_in[0:r, i, :]).then_inc(ln, 1)
                v.wait_ge(ln, b * 15 + (BASE + 5))
                v.sem_inc(tick, 1)
                for i, r in TILES:
                    nc.vector.bn_aggr(mv[0:r, i, :], stats[0:r, i, :]).then_inc(ln, 1)

            def normalise(b):
                v.wait_ge(pool, b * 2 + (BASE + 2))
                for i, r in TILES:
                    nc.vector.tensor_scalar(xn[0:r, i, :], h_in[0:r, i, :], mv[0:r, i, 0:1], rstd[0:r, i:i + 1],
                                            ALU.subtract, ALU.mult).then_inc(ln, 1)

            moments(0)
            normalise(0)
            with v.Fori(0, B) as it:
                for step in C.steps:
                    kind = step[0]
                    if kind == "ln":
                        (moments, normalise)[step[1]](it + 1)
                    if kind not in on_dve:
                        continue
                    if kind == "norm":
                        h, i = step[1:]
                        r0, t = DH * (h % 2), slice(P * i, P * i + TILES[i][1])
                        v.wait_ge(act, C.value(it, "act", ("take", h)))
                        nc.vector.reciprocal(taken[h % 2][DH:2 * DH, t], taken[h % 2][DH:2 * DH, t]).then_inc(recip, 1)
                        v.wait_ge(recip, it * (5 * H2) + (BASE + 1 + 5 * h + i))
                        nc.vector.tensor_tensor(oT[r0:r0 + DH, h // 2, t], taken[h % 2][0:DH, t],
                                                taken[h % 2][DH:2 * DH, t], ALU.mult).then_inc(dve, 1)
                        continue
                    buf = ring[C.buffer(step)]
                    if kind == "qk":
                        v.wait_ge(act, C.value(it, "act", step))
                        for r in range(2):
                            h, s = step[2] + r, slot(step[2] + r)
                            src = flat(buf)[DH * r:DH * r + DH, 0:N]
                            if step[1] == "q":
                                ins = nc.vector.scalar_tensor_tensor(q_hl[DH:P, s, 0:N], src, scale[DH * r:DH * r + DH, h:h + 1],
                                                               q_hl[0:DH, s, 0:N].bitcast(F32), ALU.mult, ALU.subtract)
                            else:
                                ins = nc.vector.tensor_tensor(k_l1[0:DH, s, 0:N], src, k_hh[0:DH, s, 0:N].bitcast(F32), ALU.subtract)
                        ins.then_inc(dve, 1)
                        continue
                    v.wait_ge(mm, C.value(it, "mm", step))
                    if kind == "v":
                        i = step[1]
                        r = TILES[i][1]
                        nc.vector.tensor_copy(vals[0:r, i, :, 0:DH].rearrange("p (a h) d -> p a h d", a=2),
                                              buf[0:r, :, 0:H2 * DH // 2].rearrange("p a (h d) -> p a h d", d=DH)).then_inc(dve, 1)
                    elif kind == "max":
                        h, i = step[1:]
                        r = TILES[i][1]
                        nc.vector.tensor_reduce(mx[0:r, i, h:h + 1], flat(buf)[0:r, 0:N], AX, ALU.max).then_inc(dve, 1)
                    elif kind == "wo":
                        i, r = TILES[step[1]]
                        if i == 0:
                            v.wait_ge(pool_res, it * 2 + (BASE + 2))
                        nc.vector.tensor_tensor(res[0:r, i, :], buf[0:r, 0, 0:D], res[0:r, i, :], ALU.add).then_inc(dve, 1)


T_ALL = (B * N + P - 1) // P
R_LAST = B * N - P * (T_ALL - 1)
GT = 12
BLOCK = 2 * P
NBLOCKS = (2 * B * N + EXPERTS * (BLOCK - 1)) // BLOCK
PLACES = 4
NBLOCKS += -NBLOCKS % PLACES
MOST = (B * N + BLOCK - 1) // BLOCK


def route_phase(nc, dram, fused, normed, logits_dram, slots_in):
    turns = T_ALL // GT
    assert turns * GT == T_ALL
    with ExitStack() as ctx:
        sb = lambda n, s, d=F32: ctx.enter_context(nc.sbuf_tensor(n, s, d))
        sem = lambda n: ctx.enter_context(nc.semaphore("r_" + n))
        ident = sb("r_ident", [P, P])
        gate_w = sb("r_gate_w", [KC, 2, EXPERTS])
        zeros = sb("r_zeros", [P, 1, D])
        h = sb("r_h", [P, GT, D])
        xn = sb("r_xn", [P, GT, D])
        xT = sb("r_xT", [KC, 2, GT * P])
        logits = sb("r_logits", [P, GT, EXPERTS])
        stats = sb("r_stats", [P, GT, 6])
        mv = sb("r_mv", [P, GT, 2])
        rstd = sb("r_rstd", [P, GT])
        var_eps = sb("r_var_eps", [P, GT])
        half = sb("r_half", [P, GT])
        ps_t = ctx.enter_context(nc.psum_tensor("r_ps_t", [P, 2, GT * P], F32))
        ps_g = ctx.enter_context(nc.psum_tensor("r_ps_g", [P, 512], F32))
        fixed_in, zeroed, padded, filled, loaded, ln, rst, mm_t, mm_g, xt_done, lg_done, kept, tick = (
            sem(n) for n in ("fixed_in", "zeroed", "padded", "filled", "loaded", "ln", "rst", "mm_t", "mm_g", "xt", "lg",
                             "kept", "tick"))
        rows = lambda t, k: t[:, :].rearrange("(g i p) d -> g p i d", p=P, i=GT)[k]
        block = ctx.enter_context(nc.Block())

        @block.sync
        def _(sp):
            sp.dma_start(ident[:, :], dram["ident"]).then_inc(fixed_in, 16)
            sp.dma_start(gate_w[:, :, :], dram["gate_w"]).then_inc(fixed_in, 16)
            sp.wait_ge(zeroed, 1)
            sp.dma_start(fused[B * N:P * T_ALL, :], zeros[0:P - R_LAST, 0, :]).then_inc(padded, 16)
            sp.wait_ge(padded, 16)
            with sp.Fori(0, turns) as it:
                sp.wait_ge(ln, it * (3 * GT) + BASE)
                sp.dma_start(h[:, :, :], rows(fused, it)).then_inc(loaded, 16)
                sp.wait_ge(ln, it * (3 * GT) + (BASE + 3 * GT))
                sp.dma_start(rows(normed, it), xn[:, :, :]).then_inc(kept, 16)
                sp.wait_ge(lg_done, it + (BASE + 1))
                sp.dma_start(rows(logits_dram, it), logits[:, :, :]).then_inc(kept, 16)
            sp.wait_ge(kept, 32 * turns + BASE)
            sp.wait_ge(filled, 16)

        @block.gpsimd
        def _(g):
            nc.gpsimd.memset(half[:, :], -0.5)
            with g.Fori(0, turns) as it:
                g.wait_ge(ln, it * (3 * GT) + (BASE + 2 * GT))
                rsqrt_steps(nc, g, tick, rstd[:, :], mv[:, :, 1], var_eps[:, :], half[:, :], rst, it * 2 + 1)

        @block.tensor
        def _(pe):
            pe.wait_ge(fixed_in, 32)
            with pe.Fori(0, turns) as it:
                pe.wait_ge(ln, it * (3 * GT) + (BASE + 3 * GT))
                pe.wait_ge(xt_done, it + BASE)
                for c in range(2):
                    for i in range(GT):
                        last = nc.tensor.transpose(ps_t[0:KC, c, P * i:P * i + P], xn[:, i, KC * c:KC * c + KC], ident[:, :])
                last.then_inc(mm_t, 1)
                pe.wait_ge(xt_done, it + (BASE + 1))
                pe.wait_ge(lg_done, it + BASE)
                for i in range(GT):
                    for c in range(2):
                        last = nc.tensor.matmul(ps_g[:, EXPERTS * i:EXPERTS * i + EXPERTS], xT[:, c, P * i:P * i + P],
                                                gate_w[:, c, :], start=(c == 0), stop=(c == 1))
                last.then_inc(mm_g, 1)

        @block.scalar
        def _(sc):
            sc.wait_ge(zeroed, 1)
            sc.dma_start(slots_in[:, :].rearrange("(p n) d -> p n d", p=P),
                         zeros[:, :, :].to_broadcast([P, NBLOCKS * BLOCK // P, D])).then_inc(filled, 16)
            with sc.Fori(0, turns) as it:
                sc.wait_ge(mm_t, it + 1)
                nc.scalar.activation(xT[:, :, :], ps_t[0:KC, :, :], ACT.Copy).then_inc(xt_done, 1)

        @block.vector
        def _(v):
            nc.vector.memset(zeros[:, :, :], 0.0).then_inc(zeroed, 1)
            for s in (ln, xt_done, lg_done, kept):
                v.sem_inc(s, BASE)
            with v.Fori(0, turns) as it:
                v.wait_ge(loaded, it * 16 + 16)
                for i in range(GT):
                    nc.vector.bn_stats(stats[:, i, :], h[:, i, :]).then_inc(ln, 1)
                v.wait_ge(ln, it * (3 * GT) + (BASE + GT))
                v.sem_inc(tick, 1)
                for i in range(GT):
                    nc.vector.bn_aggr(mv[:, i, :], stats[:, i, :]).then_inc(ln, 1)
                v.wait_ge(rst, it * 2 + 2)
                v.wait_ge(kept, it * 32 + BASE)
                for i in range(GT):
                    nc.vector.tensor_scalar(xn[:, i, :], h[:, i, :], mv[:, i, 0:1], rstd[:, i:i + 1],
                                            ALU.subtract, ALU.mult).then_inc(ln, 1)
                v.wait_ge(mm_g, it + 1)
                nc.vector.tensor_copy(logits[:, :, :].rearrange("p i e -> p (i e)"), ps_g[:, 0:GT * EXPERTS]).then_inc(lg_done, 1)


def place_phase(nc, dram, logits_dram, normed, slots_in, expert_rows, weight, slot):
    E, T = EXPERTS, T_ALL
    with ExitStack() as ctx:
        sb = lambda n, s, d=F32: ctx.enter_context(nc.sbuf_tensor(n, s, d))
        sem = lambda n: ctx.enter_context(nc.semaphore("p_" + n))
        logits = sb("p_logits", [P, T, E])
        top = sb("p_top", [P, T])
        ex = sb("p_ex", [P, T, E])
        total = sb("p_total", [P, T])
        pr = sb("p_pr", [P, T, E])
        over = sb("p_over", [P, T, E, E])
        rank = sb("p_rank", [P, T, E])
        is_k = [sb(f"p_is{k}", [P, T, E]) for k in range(2)]
        sel = sb("p_sel", [P, T, E])
        valid = sb("p_valid", [P, T])
        before = sb("p_before", [P, P])
        ones = sb("p_ones", [P, P])
        run = [sb(f"p_run{k}", [P, T, E]) for k in range(2)]
        place = sb("p_place", [P, T, E])
        prod = [sb(f"p_prod{k}", [P, T, E]) for k in range(2)]
        slot_f = sb("p_slot_f", [P, 2, T])
        levels = sb("p_levels", [P, MOST])
        numbers = sb("p_numbers", [P, NBLOCKS])
        lane = sb("p_lane", [P, 1])
        upto = sb("p_upto", [P, E, E])
        needs = sb("p_needs", [P, E, MOST])
        nblk = sb("p_nblk", [P, E])
        cum = sb("p_cum", [P, E, E])
        ends = sb("p_ends", [P, E])
        base = sb("p_base", [P, E])
        past = sb("p_past", [P, NBLOCKS, E])
        owner = sb("p_owner", [P, NBLOCKS])
        rows_f = sb("p_rows_f", [P, 3, NBLOCKS])
        rows_i = sb("p_rows_i", [P, NBLOCKS, 3], U32)
        xn = sb("p_xn", [P, T, D])
        ps = [ctx.enter_context(nc.psum_tensor(f"p_ps{k}", [P, 512], F32)) for k in range(2)]
        fixed_in, lg_in, xn_in, done, exp_done, mm, kept, scattered = (
            sem(n) for n in ("fixed_in", "lg_in", "xn_in", "done", "exp", "mm", "kept", "scattered"))
        block = ctx.enter_context(nc.Block())
        progress = {}

        @block.vector
        def _(v):
            at = [0]

            def link(ins, name=None):
                at[0] += 1
                ins.then_inc(done, 1)
                v.wait_ge(done, at[0])
                if name:
                    progress[name] = at[0]

            tt = nc.vector.tensor_tensor
            per_tile = lambda t: t[:, :].rearrange("p (i a) -> p i a", a=1).to_broadcast([P, T, E])
            nc.vector.memset(ones[:, :], 1.0)
            nc.vector.memset(over[:, :, :, :], 0.0)
            v.wait_ge(fixed_in, 96)
            v.wait_ge(lg_in, 16)
            link(nc.vector.tensor_reduce(top[:, :], logits[:, :, :], AX, ALU.max))
            link(tt(logits[:, :, :], logits[:, :, :], per_tile(top), ALU.subtract), "shifted")
            v.wait_ge(exp_done, 1)
            link(nc.vector.tensor_reduce(total[:, :], ex[:, :, :], AX, ALU.add))
            link(nc.vector.reciprocal(total[:, :], total[:, :]))
            link(tt(pr[:, :, :], ex[:, :, :], per_tile(total), ALU.mult))
            for e in range(E):
                mine = lambda n: pr[:, :, e:e + 1].to_broadcast([P, T, n])
                if e:
                    ins = tt(over[:, :, e, 0:e], pr[:, :, 0:e], mine(e), ALU.is_ge)
                if e < E - 1:
                    ins = tt(over[:, :, e, e + 1:E], pr[:, :, e + 1:E], mine(E - 1 - e), ALU.is_gt)
            link(ins)
            link(nc.vector.tensor_reduce(rank[:, :, :], over[:, :, :, :], AX, ALU.add))
            for k in range(2):
                ins = nc.vector.tensor_scalar(is_k[k][:, :, :], rank[:, :, :], float(k), None, ALU.is_equal)
            link(ins)
            for k in range(2):
                ins = tt(is_k[k][:, :, :], is_k[k][:, :, :], per_tile(valid), ALU.mult)
            link(ins)
            link(tt(sel[:, :, :], is_k[0][:, :, :], is_k[1][:, :, :], ALU.add), "selected")
            for k in range(2):
                ins = tt(prod[k][:, :, :], is_k[k][:, :, :], pr[:, :, :], ALU.mult)
            link(ins)
            for k in range(2):
                ins = nc.vector.tensor_reduce(weight[:, k, :], prod[k][:, :, :], AX, ALU.add)
            link(ins)
            v.wait_ge(mm, 1)
            link(nc.vector.tensor_copy(run[0][:, :, :].rearrange("p t e -> p (t e)"), ps[1][:, 0:T * E]))
            a, d = 0, 1
            while d < T:
                nc.vector.tensor_copy(run[1 - a][:, 0:d, :], run[a][:, 0:d, :])
                link(tt(run[1 - a][:, d:T, :], run[a][:, d:T, :], run[a][:, 0:T - d, :], ALU.add))
                a, d = 1 - a, 2 * d
            count = run[a][:, T - 1, :].rearrange("p (e j) -> p e j", j=1).to_broadcast([P, E, MOST])
            link(tt(needs[:, :, :], count, levels[:, :].rearrange("p (e j) -> p e j", e=1).to_broadcast([P, E, MOST]), ALU.is_gt))
            link(nc.vector.tensor_reduce(nblk[:, :], needs[:, :, :], AX, ALU.add))
            link(tt(cum[:, :, :], upto[:, :, :], nblk[:, :].rearrange("p (a e) -> p a e", a=1).to_broadcast([P, E, E]), ALU.mult))
            link(nc.vector.tensor_reduce(ends[:, :], cum[:, :, :], AX, ALU.add))
            link(tt(base[:, :], ends[:, :], nblk[:, :], ALU.subtract))
            link(nc.vector.tensor_scalar(base[:, :], base[:, :], float(BLOCK), None, ALU.mult))
            flat_te = lambda t: t[:, :, :].rearrange("p t e -> p (t e)")
            link(tt(flat_te(place), flat_te(run[a]), ps[1][:, 0:T * E], ALU.subtract))
            link(tt(flat_te(place), flat_te(place), ps[0][:, 0:T * E], ALU.add))
            link(tt(place[:, :, :], place[:, :, :], base[:, :].rearrange("p (a e) -> p a e", a=1).to_broadcast([P, T, E]), ALU.add))
            for k in range(2):
                ins = tt(prod[k][:, :, :], is_k[k][:, :, :], place[:, :, :], ALU.mult)
            link(ins)
            for k in range(2):
                ins = nc.vector.tensor_reduce(slot_f[:, k, :], prod[k][:, :, :], AX, ALU.add)
            link(ins)
            link(nc.vector.tensor_copy(slot[:, :, :], slot_f[:, :, :]), "slots")
            link(tt(past[:, :, :], ends[:, :].rearrange("p (a e) -> p a e", a=1).to_broadcast([P, NBLOCKS, E]),
                    numbers[:, :].rearrange("p (n a) -> p n a", a=1).to_broadcast([P, NBLOCKS, E]), ALU.is_le))
            link(nc.vector.tensor_reduce(owner[:, :], past[:, :, :], AX, ALU.add))
            link(nc.vector.tensor_scalar(rows_f[:, 2, :], owner[:, :], float(E - 1), None, ALU.min))
            for k, per in enumerate((KC, P)):
                ins = nc.vector.tensor_scalar(rows_f[:, k, :], rows_f[:, 2, :], float(per), lane[:, 0:1], ALU.mult, ALU.add)
            link(ins)
            link(nc.vector.tensor_copy(rows_i[:, :, :].rearrange("p n k -> p k n"), rows_f[:, :, :]), "rows")

        @block.sync
        def _(sp):
            sp.dma_start(logits[:, :, :], logits_dram[:, :].rearrange("(t p) e -> p t e", p=P)).then_inc(lg_in, 16)
            for dst, src in ((valid[:, :], dram["valid"]), (before[:, :], dram["before"]), (lane[:, :], dram["lane"]),
                             (levels[:, :], dram["levels"].partition_broadcast(P)),
                             (numbers[:, :], dram["numbers"].partition_broadcast(P)),
                             (upto[:, :, :], dram["upto"].partition_broadcast(P))):
                sp.dma_start(dst, src).then_inc(fixed_in, 16)
            sp.dma_start(xn[:, :, :], normed[:, :].rearrange("(t p) d -> p t d", p=P)).then_inc(xn_in, 16)
            sp.wait_ge(done, progress["rows"])
            sp.dma_start(expert_rows[:, :].rearrange("(n p) k -> p n k", p=P), rows_i[:, :, :]).then_inc(kept, 16)
            sp.wait_ge(kept, 16)

        @block.scalar
        def _(sc):
            sc.wait_ge(done, progress["shifted"])
            nc.scalar.activation(ex[:, :, :], logits[:, :, :], ACT.Exp).then_inc(exp_done, 1)

        @block.tensor
        def _(pe):
            pe.wait_ge(fixed_in, 96)
            pe.wait_ge(done, progress["selected"])
            rhs = sel[:, :, :].rearrange("p t e -> p (t e)")
            nc.tensor.matmul(ps[0][:, 0:T * E], before[:, :], rhs, start=True, stop=True)
            nc.tensor.matmul(ps[1][:, 0:T * E], ones[:, :], rhs, start=True, stop=True).then_inc(mm, 1)

        @block.gpsimd
        def _(g):
            g.wait_ge(xn_in, 16)
            g.wait_ge(done, progress["slots"])
            for i in range(T):
                r = P if i < T - 1 else R_LAST
                for k in range(2):
                    g.indirect_dma_start(slots_in, bass.IndirectOffsetOnAxis(ap=slot[0:r, k, i:i + 1], axis=0),
                                         xn[0:r, i, :], None).then_inc(scattered, 16)
            g.wait_ge(scattered, 32 * T)


def block_steps():
    out = [("t", 0)]
    for b in range(PLACES):
        out += [("up", b, m) for m in range(4)]
        out += [("t", b + 1)] if b + 1 < PLACES else []
        out += [("up", b, 4), ("up", b, 5)]
        out += [("down", b, 0), ("down", b, 1)]
    return out


def blocks_phase(nc, dram, slots_in, slots_out, expert_rows):
    C = Counts(block_steps(), ("t", "up", "down"), ("up",), ("t", "down"))
    C.looped = True
    assert len(C.jobs) % RING == 0 and NBLOCKS % PLACES == 0
    turns = NBLOCKS // PLACES
    with ExitStack() as ctx:
        sb = lambda n, s, d=F32: ctx.enter_context(nc.sbuf_tensor(n, s, d))
        each = lambda n, s, d=F32: [sb(f"m_{n}{b}", s, d) for b in range(PLACES)]
        sem = lambda n: ctx.enter_context(nc.semaphore("m_" + n))
        ident = sb("m_ident", [P, P])
        which = each("which", [P, 3], U32)
        wup = each("wup", [KC, 2, FF])
        wdown = each("wdown", [P, 6, D])
        bup = each("bup", [P, 6])
        bdown = each("bdown", [P, D])
        x = each("x", [P, 2, D])
        xT = each("xT", [KC, 2, BLOCK])
        hid = each("hid", [P, 6, BLOCK])
        y = each("y", [P, 2, D])
        ring = [ctx.enter_context(nc.psum_tensor(f"m_ring{i}", [P, 2, 512], F32)) for i in range(RING)]
        fixed_in, mm, act, dve, tick = (sem(n) for n in ("fixed_in", "mm", "act", "dve", "tick"))
        which_in, gathered, x_in, stored = ([sem(f"{n}{b}") for b in range(PLACES)] for n in ("which_in", "gathered", "x_in", "stored"))
        sems = {"mm": mm, "act": act, "dve": dve}
        block = ctx.enter_context(nc.Block())
        of_block = lambda t, n: t[:, :].rearrange("(n i p) d -> n p i d", p=P, i=2)[n]

        @block.sync
        def _(sp):
            sp.dma_start(ident[:, :], dram["ident"]).then_inc(fixed_in, 16)
            with sp.Fori(0, turns) as it:
                for b in range(PLACES):
                    sp.wait_ge(dve, C.value(it, "dve", ("down", b, 1), turns_back=1))
                    sp.sem_inc(tick, 1)
                    sp.dma_start(which[b][:, :], expert_rows[:, :].rearrange("(n p) k -> n p k", p=P)[it * PLACES + b]).then_inc(which_in[b], 16)
                    sp.dma_start(x[b][:, :, :], of_block(slots_in, it * PLACES + b)).then_inc(x_in[b], 16)

        @block.gpsimd
        def _(g):
            with g.Fori(0, turns) as it:
                for b in range(PLACES):
                    g.wait_ge(which_in[b], it * 16 + 16)
                    g.wait_ge(dve, C.value(it, "dve", ("down", b, 1), turns_back=1))
                    g.sem_inc(tick, 1)
                    for dst, table, k, r in ((wup[b][:, :, :].rearrange("p c f -> p (c f)"), "wup_rows", 0, KC),
                                             (wdown[b][:, :, :].rearrange("p k d -> p (k d)"), "wdown_rows", 1, P),
                                             (bup[b][:, :], "bup_rows", 1, P), (bdown[b][:, :], "bdown", 2, P)):
                        g.indirect_dma_start(dst, None, dram[table],
                                             bass.IndirectOffsetOnAxis(ap=which[b][0:r, k:k + 1], axis=0)).then_inc(gathered[b], 16)

        @block.tensor
        def _(pe):
            pe.wait_ge(fixed_in, 16)
            with pe.Fori(0, turns) as it:
                for step in C.steps:
                    kind, b = step[0], step[1]
                    buf = ring[C.buffer(step)]
                    name, value = C.freed(it, step)
                    pe.wait_ge(sems[name], value)
                    if kind == "t":
                        pe.wait_ge(x_in[b], it * 16 + 16)
                        for c in range(2):
                            for i in range(2):
                                last = nc.tensor.transpose(buf[0:KC, 0, BLOCK * c + P * i:BLOCK * c + P * i + P],
                                                           x[b][:, i, KC * c:KC * c + KC], ident[:, :])
                    elif kind == "up":
                        m = step[2]
                        if m == 0:
                            pe.wait_ge(gathered[b], it * 64 + 64)
                            pe.wait_ge(dve, C.value(it, "dve", ("t", b)))
                        for c in range(2):
                            last = nc.tensor.matmul(buf[:, 0, 0:BLOCK], wup[b][:, c, P * m:P * m + P], xT[b][:, c, :],
                                                    start=(c == 0), stop=(c == 1))
                    else:
                        i = step[2]
                        if i == 0:
                            pe.wait_ge(act, C.value(it, "act", ("up", b, 5)))
                        for k in range(6):
                            last = nc.tensor.matmul(buf[:, 0, 0:D], hid[b][:, k, P * i:P * i + P], wdown[b][:, k, :],
                                                    start=(k == 0), stop=(k == 5))
                    last.then_inc(mm, 1)

        @block.scalar
        def _(sc):
            def store(it, b):
                sc.wait_ge(dve, C.value(it, "dve", ("down", b, 1)))
                sc.sem_inc(tick, 1)
                sc.dma_start(of_block(slots_out, it * PLACES + b), y[b][:, :, :]).then_inc(stored[b], 16)

            sc.sem_inc(act, BASE)
            with sc.Fori(0, turns) as it:
                for step in C.steps:
                    kind, b = step[0], step[1]
                    if kind != "up":
                        continue
                    buf = ring[C.buffer(step)]
                    sc.wait_ge(mm, C.value(it, "mm", step))
                    m = step[2]
                    if m == 0:
                        sc.wait_ge(gathered[b], it * 64 + 64)
                    nc.scalar.activation(hid[b][:, m, :], buf[:, 0, 0:BLOCK], ACT.Gelu, bias=bup[b][:, m:m + 1]).then_inc(act, 1)
                    if m == 5 and b:
                        store(it, b - 1)
                store(it, PLACES - 1)
            for b in range(PLACES):
                sc.wait_ge(stored[b], turns * 16 + BASE)

        @block.vector
        def _(v):
            for s in (mm, dve, *stored):
                v.sem_inc(s, BASE)
            with v.Fori(0, turns) as it:
                for step in C.steps:
                    if step[0] == "up":
                        continue
                    b, buf = step[1], ring[C.buffer(step)]
                    if step[0] == "t":
                        v.wait_ge(mm, C.value(it, "mm", step))
                        nc.vector.tensor_copy(xT[b][:, :, :].rearrange("p c n -> p (c n)"), buf[0:KC, 0, :]).then_inc(dve, 1)
                        continue
                    i = step[2]
                    if i == 0:
                        v.wait_ge(stored[b], it * 16 + BASE)
                        v.wait_ge(gathered[b], it * 64 + 64)
                    v.wait_ge(mm, C.value(it, "mm", step))
                    nc.vector.tensor_tensor(y[b][:, i, :], buf[:, 0, 0:D], bdown[b][:, :], ALU.add).then_inc(dve, 1)


def combine_phase(nc, fused, slots_out, weight, slot, out_dram):
    T, CH = T_ALL, 6
    chunks = T // CH
    with ExitStack() as ctx:
        sb = lambda n, s, d=F32: ctx.enter_context(nc.sbuf_tensor(n, s, d))
        sem = lambda n: ctx.enter_context(nc.semaphore("c_" + n))
        h = sb("c_h", [P, T, D])
        got = [sb(f"c_got{k}", [P, T, D]) for k in range(2)]
        h_in, set_up, done, stored = (sem(n) for n in ("h_in", "set_up", "done", "stored"))
        gathered = [sem(f"gathered{c}") for c in range(chunks)]
        rows = lambda t, c: t[0:P * (T - 1), :].rearrange("(t p) d -> p t d", p=P)[:, CH * c:min(CH * c + CH, T - 1), :]
        block = ctx.enter_context(nc.Block())

        @block.gpsimd
        def _(g):
            g.wait_ge(set_up, 1)
            for i in range(T):
                r = P if i < T - 1 else R_LAST
                for k in range(2):
                    g.indirect_dma_start(got[k][0:r, i, :], None, slots_out,
                                         bass.IndirectOffsetOnAxis(ap=slot[0:r, k, i:i + 1], axis=0)).then_inc(gathered[i // CH], 16)

        @block.vector
        def _(v):
            for k in range(2):
                ins = nc.vector.memset(got[k][:, T - 1, :], 0.0)
            ins.then_inc(set_up, 1)
            v.wait_ge(h_in, 16)
            at = 0
            for c in range(chunks):
                v.wait_ge(gathered[c], 32 * CH)
                t = slice(CH * c, CH * c + CH)
                for k in range(2):
                    w = weight[:, k, t].rearrange("p (i a) -> p i a", a=1).to_broadcast([P, CH, D])
                    ins = nc.vector.tensor_tensor(got[k][:, t, :], got[k][:, t, :], w, ALU.mult)
                ins.then_inc(done, 1)
                for k in range(2):
                    at += 1
                    v.wait_ge(done, at)
                    nc.vector.tensor_tensor(h[:, t, :], h[:, t, :], got[k][:, t, :], ALU.add).then_inc(done, 1)
                at += 1
                v.wait_ge(done, at)

        @block.sync
        def _(sp):
            sp.dma_start(h[:, :, :], fused[:, :].rearrange("(t p) d -> p t d", p=P)).then_inc(h_in, 16)
            for c in range(chunks):
                sp.wait_ge(done, 3 * c + 3)
                last = min(CH * c + CH, T - 1)
                sp.dma_start(rows(out_dram, c), h[:, CH * c:last, :]).then_inc(stored, 16)
            sp.dma_start(out_dram[P * (T - 1):B * N, :], h[0:R_LAST, T - 1, :]).then_inc(stored, 16)
            sp.wait_ge(stored, 16 * (chunks + 1))


def experts_phase(nc, dram, fused, out_dram):
    internal = lambda n, s, d=F32: nc.dram_tensor(n, s, d, kind="Internal").ap()
    normed = internal("normed", [P * T_ALL, D])
    logits = internal("gate_logits", [P * T_ALL, EXPERTS])
    slots_in = internal("slots_in", [NBLOCKS * BLOCK, D])
    slots_out = internal("slots_out", [NBLOCKS * BLOCK, D])
    expert_rows = internal("expert_rows", [NBLOCKS * P, 3], U32)
    with ExitStack() as ctx:
        weight = ctx.enter_context(nc.sbuf_tensor("weight", [P, 2, T_ALL], F32))
        slot = ctx.enter_context(nc.sbuf_tensor("slot", [P, 2, T_ALL], U32))
        route_phase(nc, dram, fused, normed, logits, slots_in)
        place_phase(nc, dram, logits, normed, slots_in, expert_rows, weight, slot)
        blocks_phase(nc, dram, slots_in, slots_out, expert_rows)
        combine_phase(nc, fused, slots_out, weight, slot, out_dram)


def build(nc, dram, out):
    tokens = nc.dram_tensor("tokens", [(B + 1) * N, D], F32, kind="Internal").ap()
    fused = nc.dram_tensor("fused", [P * T_ALL, D], F32, kind="Internal").ap()
    embed_phase(nc, dram, tokens)
    encoder_phase(nc, dram, tokens)
    attention_phase(nc, dram, tokens, fused)
    experts_phase(nc, dram, fused, out.rearrange("b n d -> (b n) d"))


def kernel(**inputs):
    import concourse.bacc as _bacc
    from concourse.bass_utils import run_bass_kernel_spmd as _run

    a = {k: np.asarray(v) for k, v in inputs.items()}
    con = np.ascontiguousarray
    laid = {}
    x = a["x"].reshape(B, 3, 7, 16, 7, 16).transpose(0, 2, 4, 1, 3, 5).reshape(B * IMG, 768)
    laid["patches"] = x.T.reshape(6, P, B * IMG).transpose(1, 0, 2)
    laid["wproj"] = a["L0_tok_W_proj"].T.reshape(6, P, D).transpose(1, 0, 2)
    laid["tok_rows"] = np.stack([a["L0_tok_b_proj"], a["L0_tok_gamma"], a["L0_tok_beta"]])
    laid["ids"] = a["x_txt"].reshape(B * TXT // P, P).T
    laid["emb"] = a["L0_txt_emb"]
    pe = np.zeros((TXT, D), np.float32)
    where = np.arange(TXT, dtype=np.float32)[:, None]
    div = np.exp(np.arange(0, D, 2, dtype=np.float32) * (-np.log(10000.0) / D))
    pe[:, 0::2] = np.sin(where * div)
    pe[:, 1::2] = np.cos(where * div)
    laid["pos"] = pe.reshape(4, P, D).transpose(1, 0, 2)
    laid["ident"] = np.eye(P, dtype=np.float32)
    chunks = lambda w: w.reshape(w.shape[:-2] + (2, KC, w.shape[-1])).swapaxes(-3, -2)
    laid["wqk"] = chunks(np.concatenate([a["L0_txt_Wq"], a["L0_txt_Wk"]], axis=2))
    laid["wv"] = chunks(a["L0_txt_Wv"])
    laid["bqk"] = np.concatenate([a["L0_txt_bq"], a["L0_txt_bk"]], axis=1).reshape(LAYERS, 3, P).swapaxes(1, 2)
    laid["bv2"] = np.concatenate([a["L0_txt_bv"], a["L0_txt_bv"]], axis=1)
    wo = np.zeros((LAYERS, 3, 4, 32, D), np.float32)
    wo[:, :, :, 0:DK, :] = a["L0_txt_Wo"].reshape(LAYERS, 3, 4, DK, D)
    laid["wo"] = wo.reshape(LAYERS, 3, P, D).swapaxes(1, 2)
    laid["w1"] = chunks(a["L0_txt_W1"])
    laid["b1"] = a["L0_txt_bw1"].reshape(LAYERS, 6, P).swapaxes(1, 2)
    laid["w2"] = a["L0_txt_W2"].reshape(LAYERS, 6, P, D).swapaxes(1, 2)
    laid["enc_rows"] = np.stack([a["L0_txt_" + n] for n in ("bo", "g1", "bn1", "bw2", "g2", "bn2")], axis=1)
    w = a["L0_attn_W_qkv"].T
    laid["a_wqk"] = chunks(w[:, 0:2 * H2 * DH])
    laid["a_wv"] = chunks(w[:, 2 * H2 * DH:])
    laid["a_wo"] = a["L0_attn_W_out"].T.reshape(6, P, D).transpose(1, 0, 2)
    laid["a_scale"] = a["L0_attn_scale"]
    laid["a_bout"] = a["L0_attn_b_out"].reshape(1, D)
    laid["gate_w"] = chunks(a["L0_ffn_gate_w"])
    laid["wup_rows"] = chunks(a["L0_ffn_w_up"]).reshape(EXPERTS * KC, 2 * FF)
    laid["bup_rows"] = a["L0_ffn_b_up"].reshape(EXPERTS, 6, P).swapaxes(1, 2).reshape(EXPERTS * P, 6)
    laid["wdown_rows"] = a["L0_ffn_w_down"].reshape(EXPERTS, 6, P, D).swapaxes(1, 2).reshape(EXPERTS * P, 6 * D)
    laid["bdown"] = a["L0_ffn_b_down"]
    number = lambda n: np.arange(n, dtype=np.float32)
    laid["valid"] = (number(T_ALL)[None, :] * P + number(P)[:, None] < B * N).astype(np.float32)
    laid["before"] = np.triu(np.ones((P, P), np.float32), 1)
    laid["lane"] = number(P)[:, None]
    laid["levels"] = number(MOST) * BLOCK
    laid["numbers"] = number(NBLOCKS)
    laid["upto"] = np.tril(np.ones((EXPERTS, EXPERTS), np.float32))
    nc = _bacc.Bacc("TRN2", target_bir_lowering=False, num_devices=1)
    arrays, dram = {}, {}
    for name, value in laid.items():
        arrays[f"in_{name}"] = con(value)
        dram[name] = nc.dram_tensor(f"in_{name}", value.shape, mybir.dt.from_np(value.dtype), kind="ExternalInput").ap()
    out = nc.dram_tensor("out", (B, N, D), F32, kind="ExternalOutput").ap()
    build(nc, dram, out)
    r = _run(nc, [arrays], core_ids=[0])
    return r.results[0]["out"]
```
